# Optimizing a Trainium2 kernel written in Bass

```python
import numpy as np
import jax
import jax.numpy as jnp

def _softmax(x, axis=-1):
    return jax.nn.softmax(x, axis=axis)

def _gelu(x):
    return jax.nn.gelu(x, approximate=True)

def _silu(x):
    return jax.nn.silu(x)

def _sigmoid(x):
    return jax.nn.sigmoid(x)

def _layernorm(x, axis=-1, eps=1e-05):
    m = jnp.mean(x, axis=axis, keepdims=True)
    v = jnp.var(x, axis=axis, keepdims=True)
    return (x - m) / jnp.sqrt(v + eps)

def _scatter_add(tgt, idx, src, axis=0):
    return tgt.at[idx].add(src)

def _segment_sum(src, seg, n):
    return jax.ops.segment_sum(src, seg, n)
kernel_name = 'mk_prb_d1_jaxref_r8_57330d'

def setup_inputs(seed: int=0):
    np.random.seed(seed)
    _w = jnp.asarray

    def _L0_attn_setup():
        import jax, jax.numpy as jnp
        import numpy as np
        LN_EPS = 1e-05
        NEG_INF = -1e+38

        def _layer_norm(x, g, b):
            mu = x.mean(-1, keepdims=True)
            var = ((x - mu) ** 2).mean(-1, keepdims=True)
            return (x - mu) * jax.lax.rsqrt(var + LN_EPS) * g + b

        def _wkv(w, u, k, v):
            B, T, C = k.shape
            kt = jnp.swapaxes(k, 0, 1)
            vt = jnp.swapaxes(v, 0, 1)
            aa0 = jnp.zeros((B, C), k.dtype)
            bb0 = jnp.zeros((B, C), k.dtype)
            pp0 = jnp.full((B, C), NEG_INF, k.dtype)

            def step(carry, inp):
                aa, bb, pp = carry
                kk, vv = inp
                p = jnp.maximum(pp, u + kk)
                e1 = jnp.exp(pp - p)
                e2 = jnp.exp(u + kk - p)
                y = (e1 * aa + e2 * vv) / (e1 + e2)
                p2 = jnp.maximum(pp + w, w + kk)
                e1u = jnp.exp(pp + w - p2)
                e2u = jnp.exp(w + kk - p2)
                aa2 = e1u * aa + e2u * vv
                bb2 = e1u + e2u
                pp2 = p2 + jnp.log(bb2)
                return ((aa2, bb2, pp2), y)
            _, ys = jax.lax.scan(step, (aa0, bb0, pp0), (kt, vt))
            return jnp.swapaxes(ys, 0, 1)

        def _shift(h):
            return jnp.pad(h[:, :-1, :], ((0, 0), (1, 0), (0, 0)))
        key = jax.random.key(seed)
        B, T, C = (8, 256, 128)
        ks = jax.random.split(key, 12)
        s = 0.02
        return {'x': jax.random.normal(ks[0], (B, T, C), jnp.float32), 'time_decay': jax.random.normal(ks[1], (C,), jnp.float32) * 0.01, 'time_first': jax.random.normal(ks[2], (C,), jnp.float32) * 0.01, 'w_tk': jax.random.normal(ks[3], (C, C), jnp.float32) * s, 'w_tv': jax.random.normal(ks[4], (C, C), jnp.float32) * s, 'w_tr': jax.random.normal(ks[5], (C, C), jnp.float32) * s, 'w_ck': jax.random.normal(ks[6], (C, 4 * C), jnp.float32) * s, 'w_cv': jax.random.normal(ks[7], (4 * C, C), jnp.float32) * s, 'w_cr': jax.random.normal(ks[8], (C, C), jnp.float32) * s, 'ln1_g': jnp.ones((C,), jnp.float32), 'ln1_b': jnp.zeros((C,), jnp.float32), 'ln2_g': jnp.ones((C,), jnp.float32), 'ln2_b': jnp.zeros((C,), jnp.float32), 'mix_k': jnp.ones((1, 1, C), jnp.float32), 'mix_v': jnp.ones((1, 1, C), jnp.float32), 'mix_r': jnp.ones((1, 1, C), jnp.float32), 'cmix_k': jnp.ones((1, 1, C), jnp.float32), 'cmix_r': jnp.ones((1, 1, C), jnp.float32)}
    _L0_attn_in = _L0_attn_setup()

    def _L0_ffn_setup():
        import jax, jax.numpy as jnp
        import numpy as np
        E, TOPK, R = (8, 2, 16)
        D, H, GH = (128, 16, 32)
        HD = D // H
        SCALE = HD ** (-0.5)

        def _svd_moe(x, Wm, U, S, V, b, idx, gates):
            main = jnp.einsum('bsd,od->bso', x, Wm)
            Ug, Sg, Vg = (U[idx], S[idx], V[idx])
            xv = jnp.einsum('bsd,bkrd->bksr', x, Vg)
            xvs = xv * Sg[:, :, None, :]
            eo = jnp.einsum('bksr,bkor->bkso', xvs, Ug)
            expert = jnp.einsum('bkso,bk->bso', eo, gates)
            return main + expert + b
        key = jax.random.key(seed)
        ks = jax.random.split(key, 32)
        B, S = (32, 257)
        inp = {'hidden_states': jax.random.normal(ks[0], (B, S, D), jnp.float32)}
        inp['gw1'] = jax.random.normal(ks[1], (GH, D), jnp.float32) * 0.02
        inp['gb1'] = jnp.zeros((GH,), jnp.float32)
        inp['gw2'] = jax.random.normal(ks[2], (E, GH), jnp.float32) * 0.02
        inp['gb2'] = jnp.zeros((E,), jnp.float32)
        i = 3
        for p in ('q', 'k', 'v', 'o'):
            inp[p + 'Wm'] = jax.random.normal(ks[i], (D, D), jnp.float32) * 0.02
            i += 1
            inp[p + 'U'] = jax.random.normal(ks[i], (E, D, R), jnp.float32) * 0.02
            i += 1
            inp[p + 'S'] = jax.random.normal(ks[i], (E, R), jnp.float32) * 0.1
            i += 1
            inp[p + 'V'] = jax.random.normal(ks[i], (E, R, D), jnp.float32) * 0.02
            i += 1
            inp[p + 'b'] = jnp.zeros((D,), jnp.float32)
        return inp
    _L0_ffn_in = _L0_ffn_setup()
    _d = {'L0_attn_x': _L0_attn_in['x'], 'L0_attn_time_decay': _L0_attn_in['time_decay'], 'L0_attn_time_first': _L0_attn_in['time_first'], 'L0_attn_w_tk': _L0_attn_in['w_tk'], 'L0_attn_w_tv': _L0_attn_in['w_tv'], 'L0_attn_w_tr': _L0_attn_in['w_tr'], 'L0_attn_w_ck': _L0_attn_in['w_ck'], 'L0_attn_w_cv': _L0_attn_in['w_cv'], 'L0_attn_w_cr': _L0_attn_in['w_cr'], 'L0_attn_ln1_g': _L0_attn_in['ln1_g'], 'L0_attn_ln1_b': _L0_attn_in['ln1_b'], 'L0_attn_ln2_g': _L0_attn_in['ln2_g'], 'L0_attn_ln2_b': _L0_attn_in['ln2_b'], 'L0_attn_mix_k': _L0_attn_in['mix_k'], 'L0_attn_mix_v': _L0_attn_in['mix_v'], 'L0_attn_mix_r': _L0_attn_in['mix_r'], 'L0_attn_cmix_k': _L0_attn_in['cmix_k'], 'L0_attn_cmix_r': _L0_attn_in['cmix_r'], 'L0_ffn_gw1': _L0_ffn_in['gw1'], 'L0_ffn_gb1': _L0_ffn_in['gb1'], 'L0_ffn_gw2': _L0_ffn_in['gw2'], 'L0_ffn_gb2': _L0_ffn_in['gb2'], 'L0_ffn_qWm': _L0_ffn_in['qWm'], 'L0_ffn_qU': _L0_ffn_in['qU'], 'L0_ffn_qS': _L0_ffn_in['qS'], 'L0_ffn_qV': _L0_ffn_in['qV'], 'L0_ffn_qb': _L0_ffn_in['qb'], 'L0_ffn_kWm': _L0_ffn_in['kWm'], 'L0_ffn_kU': _L0_ffn_in['kU'], 'L0_ffn_kS': _L0_ffn_in['kS'], 'L0_ffn_kV': _L0_ffn_in['kV'], 'L0_ffn_kb': _L0_ffn_in['kb'], 'L0_ffn_vWm': _L0_ffn_in['vWm'], 'L0_ffn_vU': _L0_ffn_in['vU'], 'L0_ffn_vS': _L0_ffn_in['vS'], 'L0_ffn_vV': _L0_ffn_in['vV'], 'L0_ffn_vb': _L0_ffn_in['vb'], 'L0_ffn_oWm': _L0_ffn_in['oWm'], 'L0_ffn_oU': _L0_ffn_in['oU'], 'L0_ffn_oS': _L0_ffn_in['oS'], 'L0_ffn_oV': _L0_ffn_in['oV'], 'L0_ffn_ob': _L0_ffn_in['ob']}
    _x0 = _d['L0_attn_x']
    _d['L0_attn_x'] = jax.random.normal(jax.random.fold_in(jax.random.key(seed), 1), (2, 1024, 128), dtype=_x0.dtype)
    del _x0
    return _d

def reference(L0_attn_x, L0_attn_time_decay, L0_attn_time_first, L0_attn_w_tk, L0_attn_w_tv, L0_attn_w_tr, L0_attn_w_ck, L0_attn_w_cv, L0_attn_w_cr, L0_attn_ln1_g, L0_attn_ln1_b, L0_attn_ln2_g, L0_attn_ln2_b, L0_attn_mix_k, L0_attn_mix_v, L0_attn_mix_r, L0_attn_cmix_k, L0_attn_cmix_r, L0_ffn_gw1, L0_ffn_gb1, L0_ffn_gw2, L0_ffn_gb2, L0_ffn_qWm, L0_ffn_qU, L0_ffn_qS, L0_ffn_qV, L0_ffn_qb, L0_ffn_kWm, L0_ffn_kU, L0_ffn_kS, L0_ffn_kV, L0_ffn_kb, L0_ffn_vWm, L0_ffn_vU, L0_ffn_vS, L0_ffn_vV, L0_ffn_vb, L0_ffn_oWm, L0_ffn_oU, L0_ffn_oS, L0_ffn_oV, L0_ffn_ob):

    def _L0_attn_ref(x, time_decay, time_first, w_tk, w_tv, w_tr, w_ck, w_cv, w_cr, ln1_g, ln1_b, ln2_g, ln2_b, mix_k, mix_v, mix_r, cmix_k, cmix_r):
        import jax, jax.numpy as jnp
        import numpy as np
        LN_EPS = 1e-05
        NEG_INF = -1e+38

        def _layer_norm(x, g, b):
            mu = x.mean(-1, keepdims=True)
            var = ((x - mu) ** 2).mean(-1, keepdims=True)
            return (x - mu) * jax.lax.rsqrt(var + LN_EPS) * g + b

        def _wkv(w, u, k, v):
            B, T, C = k.shape
            kt = jnp.swapaxes(k, 0, 1)
            vt = jnp.swapaxes(v, 0, 1)
            aa0 = jnp.zeros((B, C), k.dtype)
            bb0 = jnp.zeros((B, C), k.dtype)
            pp0 = jnp.full((B, C), NEG_INF, k.dtype)

            def step(carry, inp):
                aa, bb, pp = carry
                kk, vv = inp
                p = jnp.maximum(pp, u + kk)
                e1 = jnp.exp(pp - p)
                e2 = jnp.exp(u + kk - p)
                y = (e1 * aa + e2 * vv) / (e1 + e2)
                p2 = jnp.maximum(pp + w, w + kk)
                e1u = jnp.exp(pp + w - p2)
                e2u = jnp.exp(w + kk - p2)
                aa2 = e1u * aa + e2u * vv
                bb2 = e1u + e2u
                pp2 = p2 + jnp.log(bb2)
                return ((aa2, bb2, pp2), y)
            _, ys = jax.lax.scan(step, (aa0, bb0, pp0), (kt, vt))
            return jnp.swapaxes(ys, 0, 1)

        def _shift(h):
            return jnp.pad(h[:, :-1, :], ((0, 0), (1, 0), (0, 0)))
        h = _layer_norm(x, ln1_g, ln1_b)
        hp = _shift(h)
        xk = h * mix_k + hp * (1.0 - mix_k)
        xv = h * mix_v + hp * (1.0 - mix_v)
        xr = h * mix_r + hp * (1.0 - mix_r)
        k = xk @ w_tk
        v = xv @ w_tv
        r = jax.nn.sigmoid(xr @ w_tr)
        y = _wkv(time_decay, time_first, k, v)
        x = x + r * y
        h2 = _layer_norm(x, ln2_g, ln2_b)
        hp2 = _shift(h2)
        ck = h2 * cmix_k + hp2 * (1.0 - cmix_k)
        cr = h2 * cmix_r + hp2 * (1.0 - cmix_r)
        kk = jnp.square(jax.nn.relu(ck @ w_ck))
        x = x + jax.nn.sigmoid(cr @ w_cr) * (kk @ w_cv)
        return x

    def _L0_ffn_ref(hidden_states, gw1, gb1, gw2, gb2, qWm, qU, qS, qV, qb, kWm, kU, kS, kV, kb, vWm, vU, vS, vV, vb, oWm, oU, oS, oV, ob):
        import jax, jax.numpy as jnp
        import numpy as np
        E, TOPK, R = (8, 2, 16)
        D, H, GH = (128, 16, 32)
        HD = D // H
        SCALE = HD ** (-0.5)

        def _svd_moe(x, Wm, U, S, V, b, idx, gates):
            main = jnp.einsum('bsd,od->bso', x, Wm)
            Ug, Sg, Vg = (U[idx], S[idx], V[idx])
            xv = jnp.einsum('bsd,bkrd->bksr', x, Vg)
            xvs = xv * Sg[:, :, None, :]
            eo = jnp.einsum('bksr,bkor->bkso', xvs, Ug)
            expert = jnp.einsum('bkso,bk->bso', eo, gates)
            return main + expert + b
        B, S, _ = hidden_states.shape
        pooled = hidden_states.mean(axis=1)
        h = jax.nn.relu(pooled @ gw1.T + gb1)
        logits = h @ gw2.T + gb2
        top_vals, top_idx = jax.lax.top_k(logits, TOPK)
        gates = jax.nn.softmax(top_vals, axis=-1)
        q = _svd_moe(hidden_states, qWm, qU, qS, qV, qb, top_idx, gates) * SCALE
        k = _svd_moe(hidden_states, kWm, kU, kS, kV, kb, top_idx, gates)
        v = _svd_moe(hidden_states, vWm, vU, vS, vV, vb, top_idx, gates)

        def shp(t):
            return t.reshape(B, S, H, HD).transpose(0, 2, 1, 3)
        q, k, v = (shp(q), shp(k), shp(v))
        attn = jax.nn.softmax(jnp.einsum('bhsd,bhtd->bhst', q, k), axis=-1)
        ctx = jnp.einsum('bhst,bhtd->bhsd', attn, v)
        ctx = ctx.transpose(0, 2, 1, 3).reshape(B, S, D)
        out = _svd_moe(ctx, oWm, oU, oS, oV, ob, top_idx, gates)
        return out
    x = L0_attn_x
    xn = _layernorm(x, axis=-1)
    x = x + _L0_attn_ref(xn, L0_attn_time_decay, L0_attn_time_first, L0_attn_w_tk, L0_attn_w_tv, L0_attn_w_tr, L0_attn_w_ck, L0_attn_w_cv, L0_attn_w_cr, L0_attn_ln1_g, L0_attn_ln1_b, L0_attn_ln2_g, L0_attn_ln2_b, L0_attn_mix_k, L0_attn_mix_v, L0_attn_mix_r, L0_attn_cmix_k, L0_attn_cmix_r) + _L0_ffn_ref(xn, L0_ffn_gw1, L0_ffn_gb1, L0_ffn_gw2, L0_ffn_gb2, L0_ffn_qWm, L0_ffn_qU, L0_ffn_qS, L0_ffn_qV, L0_ffn_qb, L0_ffn_kWm, L0_ffn_kU, L0_ffn_kS, L0_ffn_kV, L0_ffn_kb, L0_ffn_vWm, L0_ffn_vU, L0_ffn_vS, L0_ffn_vV, L0_ffn_vb, L0_ffn_oWm, L0_ffn_oU, L0_ffn_oS, L0_ffn_oV, L0_ffn_ob)
    return x

_drawn_inputs = setup_inputs


def setup_inputs(seed=0):
    import zlib

    import numpy as np

    out = dict(_drawn_inputs(seed))
    spreads = {'L0_attn_ln1_g': (1.0, 0.6),
     'L0_attn_ln1_b': (0.0, 0.1),
     'L0_attn_ln2_g': (1.0, 0.6),
     'L0_attn_ln2_b': (0.0, 0.8),
     'L0_attn_mix_k': (1.0, 0.6),
     'L0_attn_mix_v': (1.0, 0.6),
     'L0_attn_mix_r': (1.0, 0.6),
     'L0_attn_cmix_k': (1.0, 0.6),
     'L0_attn_cmix_r': (1.0, 0.6),
     'L0_ffn_gb1': (0.0, 2.0),
     'L0_ffn_gb2': (0.0, 0.8),
     'L0_ffn_qb': (0.0, 0.8),
     'L0_ffn_kb': (0.0, 2.0),
     'L0_ffn_vb': (0.0, 0.8),
     'L0_ffn_ob': (0.0, 2.0)}
    factors = {'L0_attn_time_decay': 2.888,
     'L0_attn_time_first': 64.0,
     'L0_attn_w_tr': 4.454,
     'L0_attn_w_ck': 6.721,
     'L0_attn_w_cv': 6.205,
     'L0_attn_w_cr': 8.0,
     'L0_ffn_gw1': 64.0,
     'L0_ffn_gw2': 64.0,
     'L0_ffn_qWm': 8.0,
     'L0_ffn_qU': 8.0,
     'L0_ffn_qS': 8.0,
     'L0_ffn_qV': 8.0,
     'L0_ffn_kWm': 8.0,
     'L0_ffn_kU': 8.0,
     'L0_ffn_kS': 8.0,
     'L0_ffn_kV': 8.0,
     'L0_ffn_vWm': 8.0,
     'L0_ffn_vU': 22.719,
     'L0_ffn_vS': 23.315,
     'L0_ffn_vV': 21.787,
     'L0_ffn_oWm': 5.144,
     'L0_ffn_oU': 8.0,
     'L0_ffn_oS': 8.0,
     'L0_ffn_oV': 8.0}
    for name, (base, spread) in spreads.items():
        noise = np.random.default_rng([zlib.crc32(name.encode()), seed]).standard_normal(out[name].shape)
        drawn = base * np.exp(spread * noise) if base else spread * noise
        out[name] = jnp.asarray(drawn.astype(out[name].dtype))
    for name, factor in factors.items():
        out[name] = (out[name] * factor).astype(out[name].dtype)
    return out
```

```python
import concourse.bass as bass
from concourse import mybir
from contextlib import ExitStack

B, T, C = 2, 1024, 128
P = 128
TILES = B * T // P
CHUNK = 512
CHUNKS = B * T // CHUNK
HEADS, HD = 16, 8
EXPERTS, RANK, GATE_H = 8, 16, 32
PAIRS = B * HEADS // 2
KEY_TILES = T // P
PARTS = 3
ROWS = PARTS * PARTS * HD
MAX_ROW = 96
LEAD = 12
A_PLACES = 33
PV_BANK, A_BANK = 4, 5
WEFF_BANKS = (5, 6, 7, 4)
SETS = 4
QUARTERS, QT = 4, 256
PARTS_OUT = 16 * (PARTS * PARTS + PARTS)
EPS = 1e-5
NEG_INF = -1e38
SCALE = float(HD) ** -0.5

COLS = ["ln1_g", "ln1_b", "ln2_g", "ln2_b", "mix_k", "mix_v", "mix_r", "cmix_k", "cmix_r",
        "decay", "first", "qb", "kb", "qS", "kS", "vS", "oS"]
MATS = ["qW", "kW", "vW", "oW", "qV", "kV", "vV", "oV", "qU", "kU", "vU", "oU",
        "tk", "tv", "tr", "cr", "ck0", "ck1", "ck2", "ck3", "cv0", "cv1", "cv2", "cv3"]
MOE = 12


def build(nc, x, cols, mats, rows, gw1, gb1, gw2, gb2, out):
    F32, BF16 = mybir.dt.float32, mybir.dt.bfloat16
    ALU, ACT, AX = mybir.AluOpType, mybir.ActivationFunctionType, mybir.AxisListType

    ctx = ExitStack()
    with ctx:
        def sb(name, shape, dt=F32):
            return ctx.enter_context(nc.sbuf_tensor(name, shape, dt))

        def sem(name):
            return ctx.enter_context(nc.semaphore(name))

        col_sb = sb("col_sb", [P, len(COLS)])
        mat_sb = sb("mat_sb", [P, len(MATS), P])
        vb_ob = sb("vb_ob", [P, 2, C])
        gw1_sb = sb("gw1_sb", [C, GATE_H])
        gb1_sb = sb("gb1_sb", [GATE_H, 1])
        gw2_sb = sb("gw2_sb", [GATE_H, EXPERTS])
        gb2_sb = sb("gb2_sb", [B, EXPERTS])
        x_sb = sb("x_sb", [P, TILES, C])
        xT = sb("xT", [P, CHUNKS, CHUNK])
        xc = sb("xc", [P, CHUNKS, CHUNK])
        sq = sb("sq", [P, CHUNKS, CHUNK])
        rstd = sb("rstd", [P, CHUNKS, CHUNK])
        xnT = sb("xnT", [P, B, T])
        hT = sb("hT", [P, B, 1 + T])
        RT = sb("RT", [P, B, T])
        ident = sb("ident", [P, P])
        mean_w = sb("mean_w", [P, P])
        eps_c = sb("eps_c", [P, 1])
        zero_c = sb("zero_c", [P, 1])
        neg_first = sb("neg_first", [P, 1])
        qb_s = sb("qb_s", [P, 1])
        pooled = sb("pooled", [C, B])
        gate_h = sb("gate_h", [GATE_H, B])
        logits = sb("logits", [B, EXPERTS])
        gt = sb("gt", [B, EXPERTS, EXPERTS])
        eq = sb("eq", [B, EXPERTS, EXPERTS])
        lower = sb("lower", [B, EXPERTS, EXPERTS])
        rank = sb("rank", [B, EXPERTS])
        chosen = sb("chosen", [B, EXPERTS])
        neg_top = sb("neg_top", [B, 1])
        gexp = sb("gexp", [B, EXPERTS])
        gsum = sb("gsum", [B, 1])
        gates = sb("gates", [B, EXPERTS])
        gates_r = sb("gates_r", [B, EXPERTS, RANK])
        gcol = sb("gcol", [P, B])
        sg = sb("sg", [P, 4, B])
        u_s = sb("u_s", [P, 4, B, P])
        w_eff = sb("w_eff", [P, 4, B, P])
        qk_f = sb("qk_f", [P, 2, CHUNKS, CHUNK])
        parts = sb("parts", [P, 2, PARTS, CHUNKS, CHUNK], BF16)
        V = sb("V", [P, PAIRS, KEY_TILES, 2 * HD])
        q_op = sb("q_op", [P, SETS, 2, T], BF16)
        k_op = sb("k_op", [P, SETS, 2, T], BF16)
        v_op = sb("v_op", [P, 2, KEY_TILES, 2, 32])
        probs = sb("probs", [P, 4, 2, CHUNK])
        res = probs[:, :, :, :].rearrange("p (t n) h c -> p t (n h) c", t=2)
        neg_half = sb("neg_half", [P, 2, KEY_TILES * 2 * 2])
        neg_max = sb("neg_max", [P, 2, KEY_TILES * 2])
        max_rows = sb("max_rows", [2 * KEY_TILES, 2, P])
        max_res = sb("max_res", [2 * KEY_TILES, 2, P])
        zero_rows = sb("zero_rows", [2 * KEY_TILES, P])
        max_parts = sb("max_parts", [2 * KEY_TILES, 2, PARTS, P], BF16)
        ctx_sb = sb("ctx_sb", [P, 2, CHUNK])
        q_dram = nc.dram_tensor("q_dram", [B * HEADS, PARTS, PARTS, HD, T], BF16).ap()
        k_dram = nc.dram_tensor("k_dram", [B * HEADS, PARTS, HD, T], BF16).ap()
        ctx_dram = nc.dram_tensor("ctx_dram", [PAIRS, 4, HD + 1, CHUNK], F32).ap()

        banks = ctx.enter_context(nc.psum_tensor("banks", [P, 8, CHUNK], F32))

        def col(name):
            i = COLS.index(name)
            return col_sb[:, i:i + 1]

        def mat(name):
            return mat_sb[:, MATS.index(name), :]

        max_parts_ready = sem("max_parts_ready")
        ctx_copied = sem("ctx_copied")
        moe_in = sem("moe_in")
        rest_in = sem("rest_in")
        cleared = sem("cleared")
        q_split = sem("q_split")
        k_split = sem("k_split")
        v_ready = sem("v_ready")
        v_set = sem("v_set")
        b_ready = sem("b_ready")
        pv_done = sem("pv_done")
        final_ready = sem("final_ready")
        out_done = sem("out_done")
        consts = sem("consts")
        mean_w_ok = sem("mean_w_ok")
        ident_ok = sem("ident_ok")
        lower_ok = sem("lower_ok")
        zeros_ok = sem("zeros_ok")
        eps_ok = sem("eps_ok")
        run_set = sem("run_set")
        ones_set = sem("ones_set")
        qk_ready = sem("qk_ready")
        k_part = sem("k_part")
        var_copied = sem("var_copied")
        xn_ready = sem("xn_ready")
        rstd_sq = sem("rstd_sq")
        var2_ready = sem("var2_ready")
        rstd2_ready = sem("rstd2_ready")
        h_hat = sem("h_hat")
        cols_in = sem("cols_in")
        h_ready = sem("h_ready")
        rows_in = sem("rows_in")
        x_transposed = sem("x_transposed")
        xob_ready = sem("xob_ready")
        a_read = sem("a_read")
        max_part = sem("max_part")
        shift_diff = sem("shift_diff")
        scaled_diff = sem("scaled_diff")
        mixed = sem("mixed")
        rt_ready = sem("rt_ready")
        carried = sem("carried")
        windows = sem("windows")
        run_max_ready = sem("run_max_ready")
        exponents = sem("exponents")
        log_sum = sem("log_sum")
        pp_less_k = sem("pp_less_k")
        weights_ready = sem("weights_ready")
        ev_ready = sem("ev_ready")
        y_terms = sem("y_terms")
        den_ready = sem("den_ready")
        log_den = sem("log_den")
        log_both = sem("log_both")
        acc_ready = sem("acc_ready")
        num_ready = sem("num_ready")
        rec_ready = sem("rec_ready")
        ry_ready = sem("ry_ready")
        x1_ready = sem("x1_ready")
        centred2 = sem("centred2")
        squared2 = sem("squared2")
        rs2_ready = sem("rs2_ready")
        h2_hat = sem("h2_hat")
        h2_scaled = sem("h2_scaled")
        h2_ready = sem("h2_ready")
        relu_ready = sem("relu_ready")
        kk_ready = sem("kk_ready")
        small_in = sem("small_in")
        xT_ready = sem("xT_ready")
        centred = sem("centred")
        squared = sem("squared")
        var_ready = sem("var_ready")
        log_var = sem("log_var")
        rstd_ready = sem("rstd_ready")
        gate_h_ps = sem("gate_h_ps")
        gate_h_ready = sem("gate_h_ready")
        shifted_ready = sem("shifted_ready")
        gexp_ready = sem("gexp_ready")
        qb_ready = sem("qb_ready")
        proj_ps = sem("proj_ps")
        log_var2 = sem("log_var2")
        kvr_ps = sem("kvr_ps")
        kvr_read = sem("kvr_read")
        log_gate = sem("log_gate")
        decays_ready = sem("decays_ready")
        sum_ready = sem("sum_ready")
        clipped = sem("clipped")
        var2_ps = sem("var2_ps")
        log_var_q = sem("log_var_q")
        ck_ps = sem("ck_ps")
        cr_ps = sem("cr_ps")
        cr_step = sem("cr_step")
        cr_ready = sem("cr_ready")
        b_read = sem("b_read")
        mean_ready = sem("mean_ready")
        pooled_ready = sem("pooled_ready")
        gate_chain = sem("gate_chain")
        logits_ps = sem("logits_ps")
        gates_ready = sem("gates_ready")
        gcol_ps = sem("gcol_ps")
        sg_ready = sem("sg_ready")
        us_ready = sem("us_ready")
        weff_ps = sem("weff_ps")
        weff_ready = sem("weff_ready")
        q_part = sem("q_part")
        v_ps = sem("v_ps")
        mean2_ps = sem("mean2_ps")
        cv_ps = sem("cv_ps")
        gated = sem("gated")
        a_ready = sem("a_ready")
        half_combined = sem("half_combined")
        den_rec = sem("den_rec")
        attn_ready = sem("attn_ready")
        final_ps = sem("final_ps")
        x_in = [sem(f"x_in{n}") for n in range(CHUNKS)]
        parts_out = [sem(f"parts_out{b}") for b in range(B)]
        op_in = [sem(f"op_in{s}") for s in range(SETS)]
        v_in = [sem(f"v_in{s}") for s in range(2)]
        max_in = [sem(f"max_in{s}") for s in range(2)]
        ctx_out = [sem(f"ctx_out{s}") for s in range(2)]
        attn_in = [sem(f"attn_in{b}") for b in range(B)]

        free = [t[:, n, :].rearrange("p (b t) -> p b t", b=B) for t in (xc, sq, rstd, qk_f[:, 0, :, :], qk_f[:, 1, :, :])
                for n in range(CHUNKS)]
        (dh, mix_k, mix_v, mix_r, k_q, v_q, er, d1, d2, d3, w1, w2, ln_s,
         lo_u, hi_u, lo_y, hi_y, ev, num, den) = free
        mix_in = [mix_k, mix_v, mix_r]
        h_in = xT[:, :, :].rearrange("p n t -> p (n t)")[:, 0:B * (QT + 1)].rearrange("p (b t) -> p b t", b=B)
        x_in_q = xT[:, 2, :].rearrange("p (b t) -> p b t", b=B)
        rec = sb("rec", [P, B, QT])
        x1, sq2, xc2, rs2 = w1, d1, d2, d3
        kk = [lo_u, hi_u, lo_y, hi_y]
        ecr, gx = er, rec
        run = sb("run", [P, 4, B, QT + 1])
        run_max, run_sum, run_acc, h2 = (run[:, i, :, :] for i in range(4))

        def var_sb(n):
            return RT[:, n // 2, CHUNK * (n % 2):CHUNK * (n % 2 + 1)]

        def bank(i):
            return banks[:, i, :]

        def bank_q(i):
            return banks[:, i, :].rearrange("p (b t) -> p b t", b=B)

        def flat(t):
            return t[:, :, :].rearrange("p b t -> p (b t)")

        def places(first, last):
            out = []
            for n in range(first, last):
                d, k = divmod(n, A_PLACES)
                out.append((d, k))
            return out

        def a_count(p, d, k):
            if isinstance(p, int) and p + d == 0:
                return k if k < 2 else k - 1
            if isinstance(p, int) and p + d == PAIRS:
                return PAIRS * A_PLACES - 1
            return (p + d) * A_PLACES + k - 1

        def a_slot(p, d, k):
            return A_BANK + (a_count(p, d, k) if isinstance(p, int) else k - 1) % 3

        def exists(p, d, k):
            if not isinstance(p, int):
                return True
            if k == 2:
                return 1 <= p + d <= PAIRS
            return p + d < PAIRS

        def step_places(step):
            lo, hi = A_PLACES * step // KEY_TILES, A_PLACES * (step + 1) // KEY_TILES
            return places(A_PLACES + LEAD + lo, A_PLACES + LEAD + hi)

        def program(eng, head, rest, tail):
            head(0, 0, 0)
            with eng.Fori(0, PAIRS // SETS - 1) as it:
                for j in range(SETS):
                    rest(it * SETS + j, j, it)
                    head(it * SETS + j + 1, j + 1, it)
            for p in range(PAIRS - SETS, PAIRS):
                rest(p, p % SETS, p // SETS)
                if p + 1 < PAIRS:
                    head(p + 1, (p + 1) % SETS, (p + 1) // SETS)
            tail()

        def first(p):
            return isinstance(p, int) and p == 0

        def recurrent(eng, quarter_1, quarter_2):
            with eng.Fori(0, QUARTERS) as q:
                quarter_1(q)
                quarter_2(q)

        block = ctx.enter_context(nc.Block())

        @block.sync
        def _(sp):
            def load_pair(p, s):
                sp.dma_start(q_op[0:ROWS, s, :, :],
                             bass.AP(q_dram.tensor, p * (2 * ROWS * T), [[T, ROWS], [ROWS * T, 2], [1, T]])
                             ).then_inc(op_in[s], 16)
                for e in range(2):
                    sp.dma_start(k_op[0:ROWS, s, e, :],
                                 bass.AP(k_dram.tensor, (p * 2 + e) * (PARTS * HD * T),
                                         [[0, PARTS], [T, PARTS * HD], [1, T]])).then_inc(op_in[s], 16)

            def place_max(p, s):
                sp.wait_ge(max_parts_ready, p + 1)
                for i in range(PARTS):
                    sp.dma_start(q_op[MAX_ROW + i:MAX_ROW + i + 1, s, :, :],
                                 max_parts[:, s % 2, i, :]).then_inc(max_in[s % 2], 16)

            def stage_v(p, s):
                for e in range(2):
                    sp.dma_start(v_op[:, s % 2, :, e, 0:HD],
                                 V[:, bass.ds(p, 1), :, HD * e:HD * e + HD].rearrange("p o k d -> p (o k) d")
                                 ).then_inc(v_in[s % 2], 16)

            def store_ctx(p, s):
                sp.wait_ge(ctx_copied, p + 2)
                for g in range(4):
                    sp.dma_start(bass.AP(ctx_dram.tensor, (p * 4 + g) * ((HD + 1) * CHUNK),
                                         [[CHUNK, HD + 1], [1, CHUNK]]),
                                 ctx_sb[32 * g:32 * g + HD + 1, s % 2, :]).then_inc(ctx_out[s % 2], 16)

            xv = x.rearrange("b (n k p) c -> (b n) p k c", p=P, k=CHUNK // P)
            for n in range(CHUNKS):
                sp.dma_start(x_sb[:, 4 * n:4 * n + 4, :], xv[n]).then_inc(x_in[n], 16)
            sp.dma_start(mat_sb[:, 0:MOE, :], mats[:, 0:MOE, :]).then_inc(moe_in, 16)
            sp.dma_start(mat_sb[:, MOE:, :], mats[:, MOE:, :]).then_inc(rest_in, 16)
            sp.wait_ge(cleared, 2)
            for b in range(B):
                here = slice(b * HEADS, (b + 1) * HEADS)
                for t, split in ((0, q_split), (1, k_split)):
                    sp.wait_ge(split, 2 * (b + 1))
                    for i in range(PARTS):
                        src = parts[:, t, i, 2 * b:2 * b + 2, :].rearrange("p n t -> p (n t)")
                        for dst in ([q_dram[here, i, j, :, :] for j in range(PARTS)] if t == 0
                                    else [k_dram[here, i, :, :]]):
                            sp.dma_start(dst, src).then_inc(parts_out[b], 16)
                if b == 0:
                    sp.wait_ge(parts_out[b], PARTS_OUT)
                    for p in range(3):
                        load_pair(p, p)
            sp.wait_ge(v_ready, CHUNKS)
            sp.wait_ge(v_set, 2)
            stage_v(0, 0)
            place_max(0, 0)
            sp.wait_ge(parts_out[1], PARTS_OUT)

            def head(p, j, it):
                if not first(p):
                    store_ctx(p - 1, (j - 1) % SETS)

            def rest(p, j, it):
                if not isinstance(p, int) or p + 3 < PAIRS:
                    sp.wait_ge(b_ready, p * 16 + 1)
                    load_pair(p + 3, (j + 3) % SETS)
                if not isinstance(p, int) or p + 1 < PAIRS:
                    sp.wait_ge(pv_done, p * 8 + 1)
                    stage_v(p + 1, (j + 1) % SETS)
                    place_max(p + 1, (j + 1) % SETS)

            def tail():
                store_ctx(PAIRS - 1, SETS - 1)
                for s in range(2):
                    sp.wait_ge(ctx_out[s], 16 * 4 * PAIRS // 2 + 1)
                for b in range(B):
                    for hs in range(2):
                        at = (b * (HEADS // 2) * 4 + hs) * (HD + 1) * CHUNK
                        head_step = 2 * (HD + 1) * CHUNK
                        sp.dma_start(xT[:, 2 * b + hs, :], bass.AP(
                            ctx_dram.tensor, at, [[head_step, HEADS], [CHUNK, HD], [1, CHUNK]])
                        ).then_inc(attn_in[b], 16)
                        sp.dma_start(sq[:, 2 * b + hs, :], bass.AP(
                            ctx_dram.tensor, at + HD * CHUNK, [[head_step, HEADS], [0, HD], [1, CHUNK]])
                        ).then_inc(attn_in[b], 16)
                ov = out.rearrange("b (n k p) c -> (b n) p k c", p=P, k=CHUNK // P)
                for n in range(CHUNKS):
                    sp.wait_ge(final_ready, n + 1)
                    sp.dma_start(ov[n], x_sb[:, 4 * n:4 * n + 4, :]).then_inc(out_done, 16)
                sp.wait_ge(out_done, 16 * CHUNKS)

            program(sp, head, rest, tail)

        @block.gpsimd
        def _(pool):
            g = nc.gpsimd
            g.memset(ident[:, :], 0.0).then_inc(consts, 1)
            g.memset(mean_w[:, :], 1.0 / C).then_inc(mean_w_ok, 1)
            pool.wait_ge(consts, 1)
            g.affine_select(out=ident[:, :], in_=ident[:, :], compare_op=ALU.not_equal, fill=1.0, base=0,
                            pattern=[[-1, P]], channel_multiplier=1).then_inc(ident_ok, 1)
            g.memset(lower[:, :, :], 1.0).then_inc(consts, 1)
            pool.wait_ge(consts, 2)
            g.affine_select(out=lower[:, :, :], in_=lower[:, :, :], compare_op=ALU.is_gt, fill=0.0, base=0,
                            pattern=[[1, EXPERTS], [-1, EXPERTS]], channel_multiplier=0).then_inc(lower_ok, 1)
            g.memset(zero_c[:, :], 0.0)
            g.memset(zero_rows[:, :], 0.0).then_inc(zeros_ok, 1)
            g.memset(eps_c[:, :], EPS).then_inc(eps_ok, 1)
            g.memset(hT[:, :, 0:1], 0.0)
            g.memset(run[:, 0, :, QT:QT + 1], NEG_INF)
            g.memset(run[:, 1, :, QT:QT + 1], 1.0)
            g.memset(run[:, 2:4, :, QT:QT + 1], 0.0).then_inc(run_set, 1)
            pool.nop().then_inc(rt_ready, 1)
            for s in range(2):
                g.memset(ctx_sb[:, s, 0:1], 0.0).then_inc(ctx_out[s], 1)
            g.memset(k_op[:, :, :, :], 0.0).then_inc(cleared, 1)
            g.memset(q_op[:, :, :, :], 0.0).then_inc(cleared, 1)
            pool.wait_ge(cleared, 2)
            g.memset(k_op[MAX_ROW:MAX_ROW + PARTS, :, :, :], 1.0).then_inc(ones_set, 1)
            pool.wait_ge(ones_set, 1)
            g.memset(v_op[:, :, :, :, :], 0.0).then_inc(v_set, 1)
            pool.wait_ge(v_set, 1)
            g.memset(v_op[:, :, :, :, HD:HD + 1], 1.0).then_inc(v_set, 1)
            for n in range(CHUNKS):
                pool.wait_ge(qk_ready, CHUNKS + n + 1)
                kf, kr = qk_f[:, 1, n, :], res[:, 1, n, :]
                k0, k1, k2 = (parts[:, 1, i, n, :] for i in range(PARTS))
                g.tensor_copy(k0, kf).then_inc(k_part, 1)
                pool.wait_ge(k_part, 3 * n + 1)
                g.tensor_tensor(kr, kf, k0, ALU.subtract).then_inc(k_part, 1)
                pool.wait_ge(k_part, 3 * n + 2)
                g.tensor_copy(k1, kr).then_inc(k_part, 1)
                pool.wait_ge(k_part, 3 * n + 3)
                g.tensor_tensor(k2, kr, k1, ALU.subtract).then_inc(k_split, 1)
            for n in range(CHUNKS):
                pool.wait_ge(var_copied, n + 1)
                pool.wait_ge(xn_ready, n + 1)
                g.tensor_tensor(xc[:, n, :], rstd[:, n, :], rstd[:, n, :], ALU.mult).then_inc(rstd_sq, 1)
            for n in range(CHUNKS):
                pool.wait_ge(rstd_sq, n + 1)
                g.tensor_tensor(xc[:, n, :], xc[:, n, :], var_sb(n), ALU.mult).then_inc(var2_ready, 1)
            for n in range(CHUNKS):
                here = hT[:, n // 2, 1 + CHUNK * (n % 2):1 + CHUNK * (n % 2 + 1)]
                pool.wait_ge(rstd2_ready, n + 1)
                xn = xnT[:, n // 2, CHUNK * (n % 2):CHUNK * (n % 2 + 1)]
                g.tensor_tensor(here, xn, rstd[:, n, :], ALU.mult).then_inc(h_hat, 1)
                pool.wait_ge(h_hat, n + 1)
                if n == 0:
                    pool.wait_ge(cols_in, 16)
                g.tensor_scalar(here, here, col("ln1_g"), col("ln1_b"), ALU.mult, ALU.add).then_inc(h_ready, 1)
            pool.wait_ge(rows_in, 16)
            pool.wait_ge(x_transposed, CHUNKS)
            for i in range(TILES):
                g.tensor_tensor(x_sb[:, i, :], x_sb[:, i, :], vb_ob[:, 1, :], ALU.add).then_inc(xob_ready, 1)
            pool.wait_ge(h_ready, CHUNKS)
            pool.wait_ge(run_set, 1)

            def split_max(p, s):
                rows_, res_ = max_rows[:, s % 2, :], max_res[:, s % 2, :]
                m0, m1, m2 = (max_parts[:, s % 2, i, :] for i in range(PARTS))
                transposed = a_count(p, 1, 2) + 1
                pool.wait_ge(a_read, transposed)
                if not (isinstance(p, int) and p < 2):
                    pool.wait_ge(b_ready, (p - 1) * 16 + 1)
                g.tensor_tensor(m0, rows_, zero_rows[:, :], ALU.add).then_inc(max_part, 1)
                pool.wait_ge(max_part, p * 3 + 1)
                g.tensor_tensor(res_, rows_, m0, ALU.subtract).then_inc(max_part, 1)
                pool.wait_ge(max_part, p * 3 + 2)
                g.tensor_tensor(m1, res_, zero_rows[:, :], ALU.add).then_inc(max_part, 1)
                pool.wait_ge(max_part, p * 3 + 3)
                g.tensor_tensor(m2, res_, m1, ALU.subtract).then_inc(max_parts_ready, 1)

            def by_channel(name):
                return col(name).to_broadcast([P, B * QT]).rearrange("p (b t) -> p b t", b=B)

            def mix(q, cur, prev, names, n, m):
                g.tensor_tensor(dh[:, :, :], cur, prev, ALU.subtract).then_inc(shift_diff, 1)
                pool.wait_ge(shift_diff, q * 2 + m + 1)
                for i, name in enumerate(names):
                    g.tensor_tensor(mix_in[i][:, :, :], dh[:, :, :], by_channel(name), ALU.mult).then_inc(scaled_diff, 1)
                for i, name in enumerate(names):
                    pool.wait_ge(scaled_diff, q * 5 + n + i + 1)
                    g.tensor_tensor(mix_in[i][:, :, :], mix_in[i][:, :, :], prev, ALU.add).then_inc(mixed, 1)

            def quarter_1(q):
                pool.wait_ge(rt_ready, q + 1)
                ends = run[:, :, :, :].rearrange("p i b t -> p (i b) t")
                g.tensor_tensor(ends[:, :, 0], ends[:, :, QT], zero_c[:, 0:1].to_broadcast([P, 4 * B]),
                                ALU.add).then_inc(carried, 1)
                g.tensor_copy(h_in, hT[:, :, bass.ds(q * QT, QT + 1)]).then_inc(windows, 1)
                g.tensor_copy(x_in_q, xnT[:, :, bass.ds(q * QT, QT)]).then_inc(windows, 1)
                pool.wait_ge(windows, q * 2 + 2)
                mix(q, h_in[:, :, 1:], h_in[:, :, 0:QT], ("mix_k", "mix_v", "mix_r"), 0, 0)
                pool.wait_ge(run_max_ready, q * 2 + 2)
                g.tensor_tensor(d1[:, :, :], run_max[:, :, 0:QT], run_max[:, :, 1:], ALU.subtract).then_inc(exponents, 1)
                g.tensor_tensor(d2[:, :, :], k_q[:, :, :], run_max[:, :, 1:], ALU.subtract).then_inc(exponents, 1)
                g.tensor_tensor(d3[:, :, :], run_max[:, :, 0:QT], k_q[:, :, :], ALU.subtract).then_inc(exponents, 1)
                pool.wait_ge(exponents, q * 3 + 3)
                pool.wait_ge(log_sum, q + 1)
                g.tensor_tensor(d3[:, :, :], d3[:, :, :], ln_s[:, :, :], ALU.add).then_inc(pp_less_k, 1)
                pool.wait_ge(weights_ready, q * 4 + 2)
                g.tensor_tensor(ev[:, :, :], hi_u[:, :, :], v_q[:, :, :], ALU.mult).then_inc(ev_ready, 1)
                pool.wait_ge(weights_ready, q * 4 + 4)
                g.tensor_tensor(num[:, :, :], hi_y[:, :, :], v_q[:, :, :], ALU.mult).then_inc(y_terms, 1)
                g.tensor_tensor(den[:, :, :], lo_y[:, :, :], hi_y[:, :, :], ALU.add).then_inc(den_ready, 1)
                pool.wait_ge(log_den, q + 1)
                g.tensor_tensor(den[:, :, :], den[:, :, :], er[:, :, :], ALU.add).then_inc(log_both, 1)
                pool.wait_ge(acc_ready, q * 2 + 2)
                g.tensor_tensor(ev[:, :, :], lo_y[:, :, :], run_acc[:, :, 0:QT], ALU.mult).then_inc(y_terms, 1)
                pool.wait_ge(y_terms, q * 2 + 2)
                g.tensor_tensor(num[:, :, :], num[:, :, :], ev[:, :, :], ALU.add).then_inc(num_ready, 1)
                pool.wait_ge(num_ready, q + 1)
                pool.wait_ge(rec_ready, q + 1)
                g.tensor_tensor(num[:, :, :], num[:, :, :], rec[:, :, :], ALU.mult).then_inc(ry_ready, 1)
                pool.wait_ge(ry_ready, q + 1)
                g.tensor_tensor(x1[:, :, :], num[:, :, :], x_in_q, ALU.add).then_inc(x1_ready, 1)

            def quarter_2(q):
                pool.wait_ge(centred2, q + 1)
                g.tensor_tensor(sq2[:, :, :], xc2[:, :, :], xc2[:, :, :], ALU.mult).then_inc(squared2, 1)
                pool.wait_ge(rs2_ready, q + 1)
                g.tensor_tensor(h2[:, :, 1:], xc2[:, :, :], rs2[:, :, :], ALU.mult).then_inc(h2_hat, 1)
                pool.wait_ge(h2_hat, q + 1)
                g.tensor_tensor(h2[:, :, 1:], h2[:, :, 1:], by_channel("ln2_g"), ALU.mult).then_inc(h2_scaled, 1)
                pool.wait_ge(h2_scaled, q + 1)
                g.tensor_tensor(h2[:, :, 1:], h2[:, :, 1:], by_channel("ln2_b"), ALU.add).then_inc(h2_ready, 1)
                pool.wait_ge(h2_ready, q + 1)
                pool.wait_ge(carried, q + 1)
                mix(q, h2[:, :, 1:], h2[:, :, 0:QT], ("cmix_k", "cmix_r"), 3, 1)
                for i in range(4):
                    pool.wait_ge(relu_ready, q * 4 + i + 1)
                    g.tensor_tensor(kk[i][:, :, :], kk[i][:, :, :], kk[i][:, :, :], ALU.mult).then_inc(kk_ready, 1)

            pool.wait_ge(zeros_ok, 1)
            recurrent(pool, quarter_1, quarter_2)
            split_max(0, 0)

            def head(p, j, it):
                pass

            def rest(p, j, it):
                if not isinstance(p, int) or p + 1 < PAIRS:
                    split_max(p + 1, (j + 1) % SETS)

            program(pool, head, rest, lambda: None)

        @block.scalar
        def _(act):
            a = nc.scalar
            a.preload_act_table_set("natural_log_exp_and_others")
            act.nop().then_inc(ctx_copied, 1)
            act.dma_start(col_sb[:, :], cols).then_inc(cols_in, 16)
            act.dma_start(vb_ob[:, :, :], rows.rearrange("(o r) c -> o r c", o=1).to_broadcast([P, 2, C])).then_inc(rows_in, 16)
            act.dma_start(gw1_sb[:, :], gw1).then_inc(small_in, 16)
            act.dma_start(gb1_sb[:, :], gb1).then_inc(small_in, 16)
            act.dma_start(gw2_sb[:, :], gw2).then_inc(small_in, 16)
            act.dma_start(gb2_sb[:, :], gb2.to_broadcast([B, EXPERTS])).then_inc(small_in, 16)
            for n in range(CHUNKS):
                act.wait_ge(x_transposed, n + 1)
                a.copy(xT[:, n, :], bank(n)).then_inc(xT_ready, 1)
            for n in range(CHUNKS):
                act.wait_ge(centred, n + 1)
                a.activation(sq[:, n, :], xc[:, n, :], ACT.Square).then_inc(squared, 1)
            act.wait_ge(eps_ok, 1)
            for n in range(CHUNKS):
                act.wait_ge(var_ready, n + 1)
                a.activation(sq[:, n, :], bank(n), ACT.Ln, bias=eps_c[:, 0:1]).then_inc(log_var, 1)
                a.copy(var_sb(n), bank(n)).then_inc(var_copied, 1)
                act.wait_ge(log_var, n + 1)
                a.activation(rstd[:, n, :], sq[:, n, :], ACT.Exp, scale=-0.5).then_inc(rstd_ready, 1)
            act.wait_ge(gate_h_ps, 1)
            act.wait_ge(small_in, 64)
            a.activation(gate_h[:, :], banks[0:GATE_H, 4, 0:B], ACT.Relu, bias=gb1_sb[:, 0:1],
                         scale=1.0 / T).then_inc(gate_h_ready, 1)
            act.wait_ge(shifted_ready, 1)
            a.activation(gexp[:, :], logits[:, :], ACT.Exp, bias=neg_top[:, 0:1]).then_inc(gexp_ready, 1)
            act.wait_ge(cols_in, 16)
            a.activation(qb_s[:, :], col("qb"), ACT.Copy, scale=SCALE).then_inc(qb_ready, 1)
            a.activation(neg_first[:, :], col("first"), ACT.Copy, scale=-1.0).then_inc(qb_ready, 1)
            act.wait_ge(qb_ready, 2)
            for t, (scale, bias) in enumerate(((SCALE, qb_s[:, 0:1]), (1.0, col("kb")))):
                for n in range(CHUNKS):
                    act.wait_ge(proj_ps, CHUNKS * t + n + 1)
                    a.activation(qk_f[:, t, n, :], bank(4 * t + n), ACT.Identity, bias=bias,
                                 scale=scale).then_inc(qk_ready, 1)

            for n in range(CHUNKS):
                act.wait_ge(var2_ready, n + 1)
                a.activation(xc[:, n, :], xc[:, n, :], ACT.Ln, bias=eps_c[:, 0:1]).then_inc(log_var2, 1)
            for n in range(CHUNKS):
                act.wait_ge(log_var2, n + 1)
                a.activation(rstd[:, n, :], xc[:, n, :], ACT.Exp, scale=-0.5).then_inc(rstd2_ready, 1)

            def quarter_1(q):
                act.wait_ge(kvr_ps, q * 3 + 1)
                a.copy(flat(k_q), bank(0)).then_inc(kvr_read, 1)
                act.wait_ge(kvr_ps, q * 3 + 2)
                a.copy(flat(v_q), bank(1)).then_inc(kvr_read, 1)
                act.wait_ge(kvr_ps, q * 3 + 3)
                a.activation(flat(er), bank(2), ACT.Exp, scale=-1.0).then_inc(kvr_read, 1)
                act.wait_ge(kvr_read, q * 3 + 3)
                a.activation(er[:, :, :], er[:, :, :], ACT.Ln, bias=1.0).then_inc(log_gate, 1)
                for i, (d, w) in enumerate(((d1, w1), (d2, w2))):
                    act.wait_ge(exponents, q * 3 + i + 1)
                    a.activation(w[:, :, :], d[:, :, :], ACT.Exp, bias=col("decay")).then_inc(decays_ready, 1)
                act.wait_ge(sum_ready, q * 2 + 2)
                a.activation(ln_s[:, :, :], run_sum[:, :, 0:QT], ACT.Ln).then_inc(log_sum, 1)
                act.wait_ge(pp_less_k, q + 1)
                weights = ((lo_u, -1.0, 0.0), (hi_u, 1.0, 0.0), (lo_y, -1.0, col("first")), (hi_y, 1.0, neg_first[:, :]))
                for t, sign, bias in weights:
                    a.activation(t[:, :, :], d3[:, :, :], ACT.Relu, scale=sign, bias=bias).then_inc(clipped, 1)
                for i, (t, _, _) in enumerate(weights):
                    act.wait_ge(clipped, q * 4 + i + 1)
                    a.activation(t[:, :, :], t[:, :, :], ACT.Exp, scale=-1.0).then_inc(weights_ready, 1)
                act.wait_ge(den_ready, q + 1)
                a.activation(den[:, :, :], den[:, :, :], ACT.Ln).then_inc(log_den, 1)
                act.wait_ge(log_both, q + 1)
                a.activation(rec[:, :, :], den[:, :, :], ACT.Exp, scale=-1.0).then_inc(rec_ready, 1)

            def quarter_2(q):
                act.wait_ge(var2_ps, q + 1)
                a.activation(flat(rs2), bank(4), ACT.Ln, bias=eps_c[:, 0:1]).then_inc(log_var_q, 1)
                act.wait_ge(log_var_q, q + 1)
                a.activation(rs2[:, :, :], rs2[:, :, :], ACT.Exp, scale=-0.5).then_inc(rs2_ready, 1)
                for i in range(4):
                    act.wait_ge(ck_ps, q * 4 + i + 1)
                    a.activation(flat(kk[i]), bank((5 + i) % 8), ACT.Relu).then_inc(relu_ready, 1)
                act.wait_ge(cr_ps, q + 1)
                a.activation(flat(ecr), bank(1), ACT.Exp, scale=-1.0).then_inc(cr_step, 1)
                act.wait_ge(cr_step, q * 2 + 1)
                a.activation(ecr[:, :, :], ecr[:, :, :], ACT.Ln, bias=1.0).then_inc(cr_step, 1)
                act.wait_ge(cr_step, q * 2 + 2)
                a.activation(ecr[:, :, :], ecr[:, :, :], ACT.Exp, scale=-1.0).then_inc(cr_ready, 1)

            recurrent(act, quarter_1, quarter_2)

            def exps(p, step):
                for e in range(2):
                    act.wait_ge(b_ready, p * 16 + 2 * step + e + 1)
                    a.activation(probs[:, (2 * step + e) % 4, :, :], banks[:, 2 * e:2 * e + 2, :],
                                 ACT.Exp).then_inc(b_read, 1)

            def copy_ctx(p, s, before):
                act.wait_ge(pv_done, (p + 1) * 8)
                act.wait_ge(ctx_out[s % 2], before * 64 + 1)
                a.copy(ctx_sb[:, s % 2, :], bank(PV_BANK)).then_inc(ctx_copied, 1)

            def head(p, j, it):
                exps(p, 0)
                if not first(p):
                    copy_ctx(p - 1, (j - 1) % SETS, it * 2 + (j - 1) // 2)

            def rest(p, j, it):
                for step in range(1, KEY_TILES):
                    exps(p, step)

            program(act, head, rest, lambda: copy_ctx(PAIRS - 1, SETS - 1, (PAIRS - 1) // 2))

        @block.vector
        def _(dve):
            v = nc.vector
            for n in range(CHUNKS):
                dve.wait_ge(mean_ready, n + 1)
                v.tensor_tensor(xc[:, n, :], xT[:, n, :], bank(4 + n), ALU.subtract).then_inc(centred, 1)
            for n in range(CHUNKS):
                dve.wait_ge(rstd_ready, n + 1)
                v.tensor_tensor(xnT[:, n // 2, CHUNK * (n % 2):CHUNK * (n % 2 + 1)], xc[:, n, :], rstd[:, n, :],
                                ALU.mult).then_inc(xn_ready, 1)
            dve.wait_ge(xn_ready, CHUNKS)
            v.reduce_sum(pooled[:, :], xnT[:, :, :], axis=AX.X).then_inc(pooled_ready, 1)

            chain = [0]

            def link(ins):
                ins.then_inc(gate_chain, 1)
                chain[0] += 1
                dve.wait_ge(gate_chain, chain[0])

            dve.wait_ge(logits_ps, 1)
            dve.wait_ge(small_in, 64)
            link(v.tensor_tensor(logits[:, :], banks[0:B, 4, 8:8 + EXPERTS], gb2_sb[:, :], ALU.add))
            v.tensor_reduce(neg_top[:, :], logits[:, :], axis=AX.X, op=ALU.max, negate=True).then_inc(shifted_ready, 1)
            sh = [B, EXPERTS, EXPERTS]
            of_j = logits[:, :].rearrange("b (o j) -> b o j", o=1).to_broadcast(sh)
            of_e = logits[:, :].rearrange("b (e o) -> b e o", o=1).to_broadcast(sh)
            link(v.tensor_tensor(gt[:, :, :], of_j, of_e, ALU.is_gt))
            link(v.tensor_tensor(eq[:, :, :], of_j, of_e, ALU.is_equal))
            dve.wait_ge(lower_ok, 1)
            link(v.tensor_tensor(eq[:, :, :], eq[:, :, :], lower[:, :, :], ALU.mult))
            link(v.tensor_tensor(gt[:, :, :], gt[:, :, :], eq[:, :, :], ALU.add))
            link(v.reduce_sum(rank[:, :], gt[:, :, :], axis=AX.X))
            link(v.tensor_scalar(chosen[:, :], rank[:, :], 2.0, None, ALU.is_lt))
            dve.wait_ge(gexp_ready, 1)
            link(v.tensor_tensor(gexp[:, :], gexp[:, :], chosen[:, :], ALU.mult))
            link(v.reduce_sum(gsum[:, :], gexp[:, :], axis=AX.X))
            link(v.reciprocal(gsum[:, :], gsum[:, :]))
            link(v.tensor_scalar(gates[:, :], gexp[:, :], gsum[:, 0:1], None, ALU.mult))
            v.tensor_copy(gates_r[:, :, :], gates[:, :].rearrange("b (e o) -> b e o", o=1).to_broadcast(
                [B, EXPERTS, RANK])).then_inc(gates_ready, 1)
            dve.wait_ge(gcol_ps, 1)
            link(v.tensor_copy(gcol[:, :], banks[:, 4, 16:16 + B]))
            dve.wait_ge(cols_in, 16)
            for i, name in enumerate(("qS", "kS", "vS", "oS")):
                v.tensor_scalar(sg[:, i, :], gcol[:, :], col(name), None, ALU.mult).then_inc(sg_ready, 1)
            dve.wait_ge(sg_ready, 4)
            dve.wait_ge(moe_in, 16)
            for i, name in enumerate(("qU", "kU", "vU", "oU")):
                for b in range(B):
                    v.tensor_scalar(u_s[:, i, b, :], mat(name), sg[:, i, b:b + 1], None, ALU.mult).then_inc(us_ready, 1)
            for i, name in enumerate(("qW", "kW", "vW", "oW")):
                dve.wait_ge(weff_ps, i + 1)
                v.tensor_tensor(w_eff[:, i, :, :], bank(WEFF_BANKS[i])[:, 0:B * P].rearrange(
                    "p (b o) -> p b o", b=B), mat(name).rearrange("p (u o) -> p u o", u=1).to_broadcast([P, B, P]),
                    ALU.add).then_inc(weff_ready, 1)
            for n in range(CHUNKS):
                dve.wait_ge(qk_ready, n + 1)
                qf, qr = qk_f[:, 0, n, :], res[:, 0, n, :]
                q0, q1, q2 = (parts[:, 0, i, n, :] for i in range(PARTS))
                v.tensor_copy(q0, qf).then_inc(q_part, 1)
                dve.wait_ge(q_part, 3 * n + 1)
                v.tensor_tensor(qr, qf, q0, ALU.subtract).then_inc(q_part, 1)
                dve.wait_ge(q_part, 3 * n + 2)
                v.tensor_copy(q1, qr).then_inc(q_part, 1)
                dve.wait_ge(q_part, 3 * n + 3)
                v.tensor_tensor(q2, qr, q1, ALU.subtract).then_inc(q_split, 1)
            dve.wait_ge(rows_in, 16)
            vb = vb_ob[:, 0:1, :].rearrange("p u (r w) -> p u r w", w=2 * HD).to_broadcast([P, 4, 8, 2 * HD])
            for n in range(CHUNKS):
                dve.wait_ge(v_ps, n + 1)
                for k in range(4):
                    tc = 4 * (n % 2) + k
                    ins = v.tensor_tensor(V[:, 8 * (n // 2):8 * (n // 2) + 8, tc, :],
                                          bank(n)[:, P * k:P * k + P].rearrange("p (r w) -> p r w", w=2 * HD),
                                          vb[:, 0, :, :], ALU.add)
                ins.then_inc(v_ready, 1)

            def scan(q, out_, c0, c1, op0, op1, done):
                for b in range(B):
                    data1 = c1.to_broadcast([P, QT]) if c1 is not None and len(c1.shape) == 2 else c1[:, b, :]
                    v.tensor_tensor_scan(out_[:, b, 1:], c0[:, b, :], data1, out_[:, b, 0:1], op0, op1).then_inc(done, 1)

            def quarter_1(q):
                dve.wait_ge(carried, q + 1)
                dve.wait_ge(kvr_read, q * 3 + 1)
                scan(q, run_max, k_q, col("decay"), ALU.max, ALU.add, run_max_ready)
                dve.wait_ge(decays_ready, q * 2 + 2)
                scan(q, run_sum, w1, w2, ALU.mult, ALU.add, sum_ready)
                dve.wait_ge(ev_ready, q + 1)
                scan(q, run_acc, lo_u, ev, ALU.mult, ALU.add, acc_ready)

            def quarter_2(q):
                dve.wait_ge(mean2_ps, q + 1)
                v.tensor_tensor(flat(xc2), flat(x1), bank(3), ALU.subtract).then_inc(centred2, 1)
                dve.wait_ge(cr_ready, q + 1)
                dve.wait_ge(cv_ps, q + 1)
                v.tensor_tensor(flat(gx), bank(2), flat(ecr), ALU.mult).then_inc(gated, 1)
                dve.wait_ge(gated, q + 1)
                v.tensor_tensor(RT[:, :, bass.ds(q * QT, QT)], x1[:, :, :], gx[:, :, :], ALU.add).then_inc(rt_ready, 1)

            recurrent(dve, quarter_1, quarter_2)

            def read_place(p, j, d, k):
                zero = isinstance(p, int) and p + d == 0
                if not exists(p, d, k) or (zero and k == 2):
                    return
                src = bank(a_slot(p, d, k))
                n = a_count(p, d, k)
                ps = (j + d) % 2
                if k == 2:
                    prev = p + d - 1
                    if not isinstance(prev, int) or prev >= 1:
                        dve.wait_ge(max_parts_ready, prev)
                    dve.wait_ge(a_ready, n + 1)
                    v.tensor_copy(max_rows[:, (ps + 1) % 2, :], src[0:2 * KEY_TILES, 0:P]).then_inc(a_read, 1)
                    return
                u = k if k < 2 else k - 1
                dve.wait_ge(a_ready, n + 1)
                v.tensor_reduce(neg_half[:, ps, u:u + 1], src, axis=AX.X, op=ALU.max, negate=True).then_inc(a_read, 1)
                if u == 31:
                    dve.wait_ge(a_read, n + 1)
                    v.tensor_reduce(neg_max[:, ps, :], neg_half[:, ps, :].rearrange("p (c h) -> p c h", h=2),
                                    axis=AX.X, op=ALU.min).then_inc(half_combined, 1)

            for d, k in places(0, A_PLACES + LEAD):
                read_place(0, 0, d, k)

            def head(p, j, it):
                for d, k in step_places(0):
                    read_place(p, j, d, k)

            def rest(p, j, it):
                for step in range(1, KEY_TILES):
                    for d, k in step_places(step):
                        read_place(p, j, d, k)

            def tail():
                for b in range(B):
                    dve.wait_ge(attn_in[b], 64)
                    c2, n2 = xT[:, 2 * b:2 * b + 2, :], sq[:, 2 * b:2 * b + 2, :]
                    v.reciprocal(n2, n2).then_inc(den_rec, 1)
                    dve.wait_ge(den_rec, b + 1)
                    v.tensor_tensor(c2, c2, n2, ALU.mult).then_inc(attn_ready, 1)
                dve.wait_ge(xob_ready, TILES)
                for n in range(CHUNKS):
                    dve.wait_ge(final_ps, n + 1)
                    here = x_sb[:, 4 * n:4 * n + 4, :].rearrange("p k c -> p (k c)")
                    v.tensor_tensor(here, here, bank(n), ALU.add).then_inc(final_ready, 1)

            program(dve, head, rest, tail)

        @block.tensor
        def _(pe):
            mm = nc.tensor.matmul
            pe.wait_ge(ident_ok, 1)
            for n in range(CHUNKS):
                pe.wait_ge(x_in[n], 16)
                for k in range(4):
                    last = nc.tensor.transpose(bank(n)[:, P * k:P * k + P], x_sb[:, 4 * n + k, :], ident[:, :])
                last.then_inc(x_transposed, 1)
            pe.wait_ge(mean_w_ok, 1)
            for n in range(CHUNKS):
                pe.wait_ge(xT_ready, n + 1)
                mm(bank(4 + n), mean_w[:, :], xT[:, n, :], start=True, stop=True).then_inc(mean_ready, 1)
            for n in range(CHUNKS):
                pe.wait_ge(squared, n + 1)
                mm(bank(n), mean_w[:, :], sq[:, n, :], start=True, stop=True).then_inc(var_ready, 1)
            pe.wait_ge(pooled_ready, 1)
            pe.wait_ge(small_in, 64)
            mm(banks[0:GATE_H, 4, 0:B], gw1_sb[:, :], pooled[:, :], start=True, stop=True).then_inc(gate_h_ps, 1)
            pe.wait_ge(gate_h_ready, 1)
            mm(banks[0:B, 4, 8:8 + EXPERTS], gate_h[:, :], gw2_sb[:, :], start=True, stop=True).then_inc(logits_ps, 1)
            pe.wait_ge(gates_ready, 1)
            mm(banks[:, 4, 16:16 + B], gates_r[:, :, :].rearrange("b e r -> b (e r)"), ident[0:B, 0:B],
               start=True, stop=True).then_inc(gcol_ps, 1)
            pe.wait_ge(moe_in, 16)
            for i, name in enumerate(("qV", "kV", "vV", "oV")):
                pe.wait_ge(us_ready, 2 * i + 2)
                mm(bank(WEFF_BANKS[i])[:, 0:B * P], mat(name),
                   u_s[:, i, :, :].rearrange("p b o -> p (b o)"), start=True, stop=True).then_inc(weff_ps, 1)
            for t in range(2):
                pe.wait_ge(weff_ready, 4 if t else 1)
                for n in range(CHUNKS):
                    if t == 0:
                        pe.wait_ge(var_copied, n + 1)
                    mm(bank(4 * t + n), w_eff[:, t, n // 2, :], xnT[:, n // 2, CHUNK * (n % 2):CHUNK * (n % 2 + 1)],
                       start=True, stop=True).then_inc(proj_ps, 1)
            for n in range(CHUNKS):
                pe.wait_ge(qk_ready, n + 1)
                for k in range(4):
                    at = CHUNK * (n % 2) + P * k
                    last = mm(bank(n)[:, P * k:P * k + P], xnT[:, n // 2, at:at + P], w_eff[:, 2, n // 2, :],
                              start=True, stop=True)
                last.then_inc(v_ps, 1)
            pe.wait_ge(v_ready, CHUNKS)
            pe.wait_ge(qk_ready, 2 * CHUNKS)
            pe.wait_ge(rest_in, 16)

            def quarter_1(q):
                for i, name in enumerate(("tk", "tv", "tr")):
                    pe.wait_ge(mixed, q * 5 + i + 1)
                    mm(bank(i), mat(name), flat(mix_in[i]), start=True, stop=True).then_inc(kvr_ps, 1)

            def quarter_2(q):
                pe.wait_ge(x1_ready, q + 1)
                mm(bank(3), mean_w[:, :], flat(x1), start=True, stop=True).then_inc(mean2_ps, 1)
                pe.wait_ge(squared2, q + 1)
                mm(bank(4), mean_w[:, :], flat(sq2), start=True, stop=True).then_inc(var2_ps, 1)
                pe.wait_ge(mixed, q * 5 + 4)
                for i in range(4):
                    mm(bank((5 + i) % 8), mat(f"ck{i}"), flat(mix_in[0]), start=True, stop=True).then_inc(ck_ps, 1)
                pe.wait_ge(mixed, q * 5 + 5)
                mm(bank(1), mat("cr"), flat(mix_in[1]), start=True, stop=True).then_inc(cr_ps, 1)
                for i in range(4):
                    pe.wait_ge(kk_ready, q * 4 + i + 1)
                    last = mm(bank(2), mat(f"cv{i}"), flat(kk[i]), start=(i == 0), stop=(i == 3))
                last.then_inc(cv_ps, 1)

            recurrent(pe, quarter_1, quarter_2)
            pe.wait_ge(rt_ready, QUARTERS + 1)
            pe.wait_ge(ones_set, 1)

            def fill_place(p, j, it, d, k):
                zero = isinstance(p, int) and p + d == 0
                if not exists(p, d, k) or (zero and k == 2):
                    return
                dst = bank(a_slot(p, d, k))
                n = a_count(p, d, k)
                if not isinstance(n, int) or n >= 3:
                    pe.wait_ge(a_read, n - 2)
                ps, s = (j + d) % 2, (j + d) % SETS
                if k == 2:
                    pe.wait_ge(half_combined, p + d)
                    nc.tensor.transpose(dst[0:2 * KEY_TILES, 0:P], neg_max[:, (ps + 1) % 2, :],
                                        ident[:, :]).then_inc(a_ready, 1)
                    return
                u = k if k < 2 else k - 1
                if u == 0:
                    pe.wait_ge(op_in[s], (it + (j + d) // SETS + 1) * 48)
                e, c, h = u // 16, u // 2 % 8, u % 2
                mm(dst, q_op[0:MAX_ROW, s, e, P * c:P * c + P],
                   k_op[0:MAX_ROW, s, e, CHUNK * h:CHUNK * h + CHUNK],
                   start=True, stop=True).then_inc(a_ready, 1)

            for d, k in places(0, A_PLACES + LEAD):
                fill_place(0, 0, 0, d, k)

            def scores(p, s, step, e):
                if not (first(p) and step == 0):
                    pe.wait_ge(b_read, p * 16 + 2 * step + e - 1)
                for h in range(2):
                    last = mm(bank(2 * e + h), k_op[0:MAX_ROW + PARTS, s, e, P * step:P * step + P],
                              q_op[0:MAX_ROW + PARTS, s, e, CHUNK * h:CHUNK * h + CHUNK], start=True, stop=True)
                last.then_inc(b_ready, 1)

            def values(p, s, step):
                pe.wait_ge(b_read, p * 16 + 2 * step + 2)
                for e in range(2):
                    for h in range(2):
                        g = 32 * (2 * e + h)
                        last = mm(banks[g:g + 32, PV_BANK, :], v_op[:, s % 2, step, e, :],
                                  probs[:, (2 * step + e) % 4, h, :], start=(step == 0), stop=(step == KEY_TILES - 1))
                last.then_inc(pv_done, 1)

            def one_step(p, j, it, step):
                todo = step_places(step)
                scores(p, j % SETS, step, 0)
                for d, k in todo[:2]:
                    fill_place(p, j, it, d, k)
                scores(p, j % SETS, step, 1)
                for d, k in todo[2:]:
                    fill_place(p, j, it, d, k)

            def head(p, j, it):
                pe.wait_ge(max_in[j % 2], (it * 2 + j // 2 + 1) * 16 * PARTS)
                one_step(p, j, it, 0)
                if not first(p):
                    values(p - 1, (j - 1) % SETS, KEY_TILES - 1)

            def rest(p, j, it):
                for step in range(1, KEY_TILES):
                    one_step(p, j, it, step)
                    if step == 1:
                        pe.wait_ge(v_in[j % 2], (it * 2 + j // 2 + 1) * 32)
                        pe.wait_ge(ctx_copied, p + 1)
                    values(p, j % SETS, step - 1)

            def tail():
                values(PAIRS - 1, SETS - 1, KEY_TILES - 1)
                for n in range(CHUNKS):
                    pe.wait_ge(attn_ready, n // 2 + 1)
                    for k in range(4):
                        at, dst = CHUNK * (n % 2) + P * k, bank(n)[:, P * k:P * k + P]
                        mm(dst, xT[:, n, P * k:P * k + P], w_eff[:, 3, n // 2, :], start=True, stop=False)
                        last = mm(dst, RT[:, n // 2, at:at + P], ident[:, :], start=False, stop=True)
                    last.then_inc(final_ps, 1)

            program(pe, head, rest, tail)


def kernel(**inputs):
    import numpy as np
    import concourse.bacc as bacc
    from concourse.bass_utils import run_bass_kernel_spmd

    def arr(name):
        return np.asarray(inputs[name])

    a, f = "L0_attn_", "L0_ffn_"
    col_of = {n: arr(a + n).reshape(C) for n in COLS[:9]}
    col_of.update(decay=arr(a + "time_decay"), first=arr(a + "time_first"), qb=arr(f + "qb"), kb=arr(f + "kb"))
    for p in "qkvo":
        col_of[p + "S"] = arr(f + p + "S").reshape(EXPERTS * RANK)
    mat_of = {n: arr(a + "w_" + n) for n in ("tk", "tv", "tr", "cr")}
    for i in range(4):
        mat_of[f"ck{i}"] = arr(a + "w_ck")[:, P * i:P * (i + 1)]
        mat_of[f"cv{i}"] = arr(a + "w_cv")[P * i:P * (i + 1), :]
    for p in "qkvo":
        mat_of[p + "W"] = arr(f + p + "Wm").T
        mat_of[p + "V"] = arr(f + p + "V").reshape(EXPERTS * RANK, C)
        mat_of[p + "U"] = arr(f + p + "U").transpose(0, 2, 1).reshape(EXPERTS * RANK, C)
    arrays = {
        "x": arr(a + "x"),
        "cols": np.stack([col_of[n] for n in COLS], axis=1),
        "mats": np.stack([mat_of[n] for n in MATS], axis=1),
        "rows": np.stack([arr(f + "vb"), arr(f + "ob")]),
        "gw1": arr(f + "gw1").T,
        "gb1": arr(f + "gb1").reshape(GATE_H, 1),
        "gw2": arr(f + "gw2").T,
        "gb2": arr(f + "gb2").reshape(1, EXPERTS),
    }
    arrays = {f"in_{n}_dram": np.ascontiguousarray(v) for n, v in arrays.items()}
    nc = bacc.Bacc("TRN2", target_bir_lowering=False, num_devices=1)
    args = [nc.dram_tensor(n, v.shape, mybir.dt.from_np(v.dtype), kind="ExternalInput").ap()
            for n, v in arrays.items()]
    out = nc.dram_tensor("out_0_dram", (B, T, C), mybir.dt.float32, kind="ExternalOutput").ap()
    build(nc, *args, out)
    r = run_bass_kernel_spmd(nc, [arrays], core_ids=[0])
    return r.results[0]["out_0_dram"]
```

```python
import concourse.bass as bass
from concourse import mybir
from contextlib import ExitStack

B, T, C = 2, 1024, 128
P = 128
TILES = B * T // P
CHUNK = 512
CHUNKS = B * T // CHUNK
HEADS, HD = 16, 8
EXPERTS, RANK, GATE_H = 8, 16, 32
PAIRS = B * HEADS // 2
KEY_TILES = T // P
PARTS = 3
ROWS = PARTS * PARTS * HD
MAX_ROW = 96
SPLIT_STEP = 5
LEAD = 12
A_PLACES = 33
PV_BANK, A_BANK = 4, 5
WEFF_BANKS = (5, 6, 7, 4)
SETS = 4
QUARTERS, QT = 4, 256
PRODUCT_STEP = {"k": 3, "v": 4, "r": 5, "mean": 15, "var": 16, "ck0": 20, "ck1": 21, "ck2": 22, "ck3": 23,
                "cr": 24, "cv": 26}
PARTS_OUT = 16 * (PARTS * PARTS + PARTS)
EPS = 1e-5
NEG_INF = -1e38
SCALE = float(HD) ** -0.5

COLS = ["ln1_g", "ln1_b", "ln2_g", "ln2_b", "mix_k", "mix_v", "mix_r", "cmix_k", "cmix_r",
        "decay", "first", "qb", "kb", "qS", "kS", "vS", "oS"]
MATS = ["qW", "kW", "vW", "oW", "qV", "kV", "vV", "oV", "qU", "kU", "vU", "oU",
        "tk", "tv", "tr", "cr", "ck0", "ck1", "ck2", "ck3", "cv0", "cv1", "cv2", "cv3"]
MOE = 12


def build(nc, x, cols, mats, rows, gw1, gb1, gw2, gb2, out):
    F32, BF16 = mybir.dt.float32, mybir.dt.bfloat16
    ALU, ACT, AX = mybir.AluOpType, mybir.ActivationFunctionType, mybir.AxisListType

    ctx = ExitStack()
    with ctx:
        def sb(name, shape, dt=F32):
            return ctx.enter_context(nc.sbuf_tensor(name, shape, dt))

        def sem(name):
            return ctx.enter_context(nc.semaphore(name))

        col_sb = sb("col_sb", [P, len(COLS)])
        mat_sb = sb("mat_sb", [P, len(MATS), P])
        vb_ob = sb("vb_ob", [P, 2, C])
        gw1_sb = sb("gw1_sb", [C, GATE_H])
        gb1_sb = sb("gb1_sb", [GATE_H, 1])
        gw2_sb = sb("gw2_sb", [GATE_H, EXPERTS])
        gb2_sb = sb("gb2_sb", [B, EXPERTS])
        x_sb = sb("x_sb", [P, TILES, C])
        xT = sb("xT", [P, CHUNKS, CHUNK])
        xc = sb("xc", [P, CHUNKS, CHUNK])
        sq = sb("sq", [P, CHUNKS, CHUNK])
        rstd = sb("rstd", [P, CHUNKS, CHUNK])
        xnT = sb("xnT", [P, B, T])
        hT = sb("hT", [P, B, 1 + T])
        RT = sb("RT", [P, B, T])
        ident = sb("ident", [P, P])
        mean_w = sb("mean_w", [P, P])
        eps_c = sb("eps_c", [P, 1])
        zero_c = sb("zero_c", [P, 1])
        neg_first = sb("neg_first", [P, 1])
        qb_s = sb("qb_s", [P, 1])
        pooled = sb("pooled", [C, B])
        gate_h = sb("gate_h", [GATE_H, B])
        logits = sb("logits", [B, EXPERTS])
        gt = sb("gt", [B, EXPERTS, EXPERTS])
        eq = sb("eq", [B, EXPERTS, EXPERTS])
        lower = sb("lower", [B, EXPERTS, EXPERTS])
        rank = sb("rank", [B, EXPERTS])
        chosen = sb("chosen", [B, EXPERTS])
        neg_top = sb("neg_top", [B, 1])
        gexp = sb("gexp", [B, EXPERTS])
        gsum = sb("gsum", [B, 1])
        gates = sb("gates", [B, EXPERTS])
        gates_r = sb("gates_r", [B, EXPERTS, RANK])
        gcol = sb("gcol", [P, B])
        sg = sb("sg", [P, 4, B])
        u_s = sb("u_s", [P, 4, B, P])
        w_eff = sb("w_eff", [P, 4, B, P])
        qk_f = sb("qk_f", [P, 2, CHUNKS, CHUNK])
        parts = sb("parts", [P, 2, PARTS, CHUNKS, CHUNK], BF16)
        ctx_T, den_T = (parts[:, t, 0:2, :, :].rearrange("p i n t -> p (i n t)").bitcast(F32).rearrange(
            "p (n t) -> p n t", t=CHUNK) for t in range(2))
        V = sb("V", [P, PAIRS, KEY_TILES, 2 * HD])
        q_op = sb("q_op", [P, SETS, 2, T], BF16)
        k_op = sb("k_op", [P, SETS, 2, T], BF16)
        v_op = sb("v_op", [P, 2, KEY_TILES, 2, 32])
        probs = sb("probs", [P, 4, 2, CHUNK])
        res = probs[:, :, :, :].rearrange("p (t n) h c -> p t (n h) c", t=2)
        neg_half = sb("neg_half", [P, 2, KEY_TILES * 2 * 2])
        neg_max = sb("neg_max", [P, 2, KEY_TILES * 2])
        max_rows = sb("max_rows", [2 * KEY_TILES, 2, P])
        max_res = sb("max_res", [2 * KEY_TILES, 2, P])
        zero_rows = sb("zero_rows", [2 * KEY_TILES, P])
        max_parts = sb("max_parts", [2 * KEY_TILES, 2, PARTS, P], BF16)
        ctx_sb = sb("ctx_sb", [P, 2, CHUNK])
        q_dram = nc.dram_tensor("q_dram", [B * HEADS, PARTS, PARTS, HD, T], BF16).ap()
        k_dram = nc.dram_tensor("k_dram", [B * HEADS, PARTS, HD, T], BF16).ap()
        ctx_dram = nc.dram_tensor("ctx_dram", [PAIRS, 4, HD + 1, CHUNK], F32).ap()

        banks = ctx.enter_context(nc.psum_tensor("banks", [P, 8, CHUNK], F32))

        def col(name):
            i = COLS.index(name)
            return col_sb[:, i:i + 1]

        def mat(name):
            return mat_sb[:, MATS.index(name), :]

        kvr_read = sem("kvr_read")
        centred2 = sem("centred2")
        log_var_q = sem("log_var_q")
        cr_step = sem("cr_step")
        gated = sem("gated")
        relu_ready = sem("relu_ready")
        a_read = sem("a_read")
        max_parts_ready = sem("max_parts_ready")
        ctx_copied = sem("ctx_copied")
        moe_in = sem("moe_in")
        rest_in = sem("rest_in")
        cleared = sem("cleared")
        q_split = sem("q_split")
        k0_split = sem("k0_split")
        k1_split = sem("k1_split")
        v_ready = sem("v_ready")
        v_set = sem("v_set")
        b_ready = sem("b_ready")
        pv_done = sem("pv_done")
        final_ready = sem("final_ready")
        out_done = sem("out_done")
        consts = sem("consts")
        mean_w_ok = sem("mean_w_ok")
        ident_ok = sem("ident_ok")
        lower_ok = sem("lower_ok")
        zeros_ok = sem("zeros_ok")
        eps_ok = sem("eps_ok")
        run_set = sem("run_set")
        rt_ready = sem("rt_ready")
        ones_set = sem("ones_set")
        rows_in = sem("rows_in")
        x_transposed = sem("x_transposed")
        xob_ready = sem("xob_ready")
        qk_ready = sem("qk_ready")
        k_part = sem("k_part")
        rstd_sq = sem("rstd_sq")
        var_copied = sem("var_copied")
        var2_ready = sem("var2_ready")
        rstd2_ready = sem("rstd2_ready")
        xn_ready = sem("xn_ready")
        h_hat = sem("h_hat")
        max_part = sem("max_part")
        shift_diff = sem("shift_diff")
        scaled_diff = sem("scaled_diff")
        mixed = sem("mixed")
        carried = sem("carried")
        windows = sem("windows")
        run_max_ready = sem("run_max_ready")
        exponents = sem("exponents")
        log_sum = sem("log_sum")
        pp_less_k = sem("pp_less_k")
        weights_ready = sem("weights_ready")
        ev_ready = sem("ev_ready")
        den_ready = sem("den_ready")
        y_terms = sem("y_terms")
        log_den = sem("log_den")
        log_both = sem("log_both")
        acc_ready = sem("acc_ready")
        num_ready = sem("num_ready")
        rec_ready = sem("rec_ready")
        ry_ready = sem("ry_ready")
        x1_ready = sem("x1_ready")
        squared2 = sem("squared2")
        rs2_ready = sem("rs2_ready")
        h2_hat = sem("h2_hat")
        h2_ready = sem("h2_ready")
        kk_ready = sem("kk_ready")
        h_ready = sem("h_ready")
        cols_in = sem("cols_in")
        small_in = sem("small_in")
        xT_ready = sem("xT_ready")
        centred = sem("centred")
        squared = sem("squared")
        var_ready = sem("var_ready")
        log_var = sem("log_var")
        rstd_ready = sem("rstd_ready")
        gate_h_ps = sem("gate_h_ps")
        gate_h_ready = sem("gate_h_ready")
        shifted_ready = sem("shifted_ready")
        gexp_ready = sem("gexp_ready")
        qb_ready = sem("qb_ready")
        proj_ps = sem("proj_ps")
        log_var2 = sem("log_var2")
        clipped = sem("clipped")
        kvr_ps = sem("kvr_ps")
        log_gate = sem("log_gate")
        decays_ready = sem("decays_ready")
        sum_ready = sem("sum_ready")
        var2_ps = sem("var2_ps")
        ck_ps = sem("ck_ps")
        cr_ps = sem("cr_ps")
        cr_ready = sem("cr_ready")
        b_read = sem("b_read")
        den_step = sem("den_step")
        mean_ready = sem("mean_ready")
        pooled_ready = sem("pooled_ready")
        gate_chain = sem("gate_chain")
        logits_ps = sem("logits_ps")
        gates_ready = sem("gates_ready")
        gcol_ps = sem("gcol_ps")
        sg_ready = sem("sg_ready")
        us_ready = sem("us_ready")
        weff_ps = sem("weff_ps")
        weff_ready = sem("weff_ready")
        q_part = sem("q_part")
        k0_part = sem("k0_part")
        v_ps = sem("v_ps")
        mean2_ps = sem("mean2_ps")
        cv_ps = sem("cv_ps")
        a_ready = sem("a_ready")
        half_combined = sem("half_combined")
        attn_ready = sem("attn_ready")
        final_ps = sem("final_ps")
        x_in = [sem(f"x_in{n}") for n in range(CHUNKS)]
        parts_out = [sem(f"parts_out{b}") for b in range(B)]
        op_in = [sem(f"op_in{s}") for s in range(SETS)]
        v_in = [sem(f"v_in{s}") for s in range(2)]
        max_in = [sem(f"max_in{s}") for s in range(2)]
        ctx_out = [sem(f"ctx_out{s}") for s in range(2)]
        attn_in = [sem(f"attn_in{b}") for b in range(B)]

        free = [t[:, n, :].rearrange("p (b t) -> p b t", b=B) for t in (xc, sq, rstd, qk_f[:, 0, :, :], qk_f[:, 1, :, :])
                for n in range(CHUNKS)]
        (dh, mix_k, mix_v, mix_r, k_q, v_q, er, d1, d2, d3, w1, w2, ln_s,
         lo_u, hi_u, lo_y, hi_y, ev, num, den) = free
        mix_in = [mix_k, mix_v, mix_r]
        h_in = xT[:, :, :].rearrange("p n t -> p (n t)")[:, 0:B * (QT + 1)].rearrange("p (b t) -> p b t", b=B)
        x_in_q = xT[:, 2, :].rearrange("p (b t) -> p b t", b=B)
        rec = sb("rec", [P, B, QT])
        x1, sq2, xc2, rs2 = w1, d1, d2, d3
        kk = [lo_u, hi_u, lo_y, hi_y]
        ecr, gx = er, rec
        run = sb("run", [P, 4, B, QT + 1])
        run_max, run_sum, run_acc, h2 = (run[:, i, :, :] for i in range(4))

        def var_sb(n):
            return RT[:, n // 2, CHUNK * (n % 2):CHUNK * (n % 2 + 1)]

        def bank(i):
            return banks[:, i, :]

        def flat(t):
            return t[:, :, :].rearrange("p b t -> p (b t)")

        def places(first, last):
            return [divmod(n, A_PLACES) for n in range(first, last)]

        def exists(it, pair, k):
            n = it * SETS + pair
            if not isinstance(n, int):
                return True
            return 1 <= n <= PAIRS if k == 2 else n < PAIRS

        def a_count(it, pair, k):
            n = it * SETS + pair
            if isinstance(n, int) and n == 0:
                return k if k < 2 else k - 1
            if isinstance(n, int) and n == PAIRS:
                return PAIRS * A_PLACES - 1
            return n * A_PLACES + k - 1

        turns, place_turns = [], []
        for t in range(SETS * KEY_TILES):
            at = A_PLACES + LEAD
            here = places(at + A_PLACES * t // KEY_TILES, at + A_PLACES * (t + 1) // KEY_TILES)
            place_turns.append(range(len(turns), len(turns) + len(here)))
            turns += here
            turns += [name for name, step in PRODUCT_STEP.items() if step == t]
        assert (len(turns) + 1) % 3 == 0

        def turn_bank(turn):
            return bank(A_BANK + (turn + A_PLACES + LEAD - 1) % 3)

        taken_by = {"k": (kvr_read, 3, 1), "v": (kvr_read, 3, 2), "r": (kvr_read, 3, 3),
                    "mean": (centred2, 1, 1), "var": (log_var_q, 1, 1), "cr": (cr_step, 2, 1),
                    "cv": (gated, 1, 1)}
        for i in range(4):
            taken_by[f"ck{i}"] = (relu_ready, 4, i + 1)

        def wait_for_bank(pe, it, turn):
            if turn < 3:
                pe.wait_ge(a_read, a_count(it, *turns[turn]) - 1)
                return
            turn -= 3
            while isinstance(turns[turn], tuple) and not exists(it, *turns[turn]):
                turn -= 3
            if isinstance(turns[turn], tuple):
                pe.wait_ge(a_read, a_count(it, *turns[turn]) + 1)
            else:
                taken, of, n = taken_by[turns[turn]]
                pe.wait_ge(taken, it * of + n)

        def program(eng, head, rest, tail):
            head(0, 0, 0)
            with eng.Fori(0, PAIRS // SETS - 1) as it:
                for j in range(SETS):
                    rest(it * SETS + j, j, it)
                    head(it * SETS + j + 1, (j + 1) % SETS, it + (j + 1) // SETS)
            for p in range(PAIRS - SETS, PAIRS):
                rest(p, p % SETS, p // SETS)
                if p + 1 < PAIRS:
                    head(p + 1, (p + 1) % SETS, (p + 1) // SETS)
            tail()

        def first(p):
            return isinstance(p, int) and p == 0

        block = ctx.enter_context(nc.Block())

        @block.sync
        def _(sp):
            def load_pair(p, s):
                sp.dma_start(q_op[0:ROWS, s, :, :],
                             bass.AP(q_dram.tensor, p * (2 * ROWS * T), [[T, ROWS], [ROWS * T, 2], [1, T]])
                             ).then_inc(op_in[s], 16)
                for e in range(2):
                    sp.dma_start(k_op[0:ROWS, s, e, :],
                                 bass.AP(k_dram.tensor, (p * 2 + e) * (PARTS * HD * T),
                                         [[0, PARTS], [T, PARTS * HD], [1, T]])).then_inc(op_in[s], 16)

            def place_max(p, s):
                sp.wait_ge(max_parts_ready, p + 1)
                for i in range(PARTS):
                    sp.dma_start(q_op[MAX_ROW + i:MAX_ROW + i + 1, s, :, :],
                                 max_parts[:, s % 2, i, :]).then_inc(max_in[s % 2], 16)

            def stage_v(p, s):
                for e in range(2):
                    sp.dma_start(v_op[:, s % 2, :, e, 0:HD],
                                 V[:, bass.ds(p, 1), :, HD * e:HD * e + HD].rearrange("p o k d -> p (o k) d")
                                 ).then_inc(v_in[s % 2], 16)

            def store_ctx(p, s):
                sp.wait_ge(ctx_copied, p + 2)
                for g in range(4):
                    sp.dma_start(bass.AP(ctx_dram.tensor, (p * 4 + g) * ((HD + 1) * CHUNK),
                                         [[CHUNK, HD + 1], [1, CHUNK]]),
                                 ctx_sb[32 * g:32 * g + HD + 1, s % 2, :]).then_inc(ctx_out[s % 2], 16)

            xv = x.rearrange("b (n k p) c -> (b n) p k c", p=P, k=CHUNK // P)
            for n in range(CHUNKS):
                sp.dma_start(x_sb[:, 4 * n:4 * n + 4, :], xv[n]).then_inc(x_in[n], 16)
            sp.dma_start(mat_sb[:, 0:MOE, :], mats[:, 0:MOE, :]).then_inc(moe_in, 16)
            sp.dma_start(mat_sb[:, MOE:, :], mats[:, MOE:, :]).then_inc(rest_in, 16)
            sp.wait_ge(cleared, 2)
            def store_parts(b, t, split, count):
                sp.wait_ge(split, count)
                here = slice(b * HEADS, (b + 1) * HEADS)
                for i in range(PARTS):
                    src = parts[:, t, i, 2 * b:2 * b + 2, :].rearrange("p n t -> p (n t)")
                    for dst in ([q_dram[here, i, j, :, :] for j in range(PARTS)] if t == 0
                                else [k_dram[here, i, :, :]]):
                        sp.dma_start(dst, src).then_inc(parts_out[b], 16)

            store_parts(0, 0, q_split, 2)
            store_parts(0, 1, k0_split, 2)
            sp.wait_ge(parts_out[0], PARTS_OUT)
            for p in range(3):
                load_pair(p, p)
            store_parts(1, 0, q_split, 4)
            store_parts(1, 1, k1_split, 2)
            sp.wait_ge(v_ready, CHUNKS)
            sp.wait_ge(v_set, 2)
            stage_v(0, 0)
            place_max(0, 0)
            sp.wait_ge(parts_out[1], PARTS_OUT)

            def head(p, j, it):
                if not first(p):
                    store_ctx(p - 1, (j - 1) % SETS)

            def rest(p, j, it):
                if not isinstance(p, int) or p + 3 < PAIRS:
                    sp.wait_ge(b_ready, p * 16 + 1)
                    load_pair(p + 3, (j + 3) % SETS)
                if not isinstance(p, int) or p + 1 < PAIRS:
                    sp.wait_ge(pv_done, p * 8 + 1)
                    stage_v(p + 1, (j + 1) % SETS)
                    place_max(p + 1, (j + 1) % SETS)

            def load_contexts(b):
                for s in range(2):
                    sp.wait_ge(ctx_out[s], 64 * (PAIRS // 4) * (b + 1) + 1)
                for hs in range(2):
                    at = (b * (HEADS // 2) * 4 + hs) * (HD + 1) * CHUNK
                    head_step = 2 * (HD + 1) * CHUNK
                    sp.dma_start(den_T[:, 2 * b + hs, :], bass.AP(
                        ctx_dram.tensor, at + HD * CHUNK, [[head_step, HEADS], [0, HD], [1, CHUNK]])
                    ).then_inc(attn_in[b], 16)
                    sp.dma_start(ctx_T[:, 2 * b + hs, :], bass.AP(
                        ctx_dram.tensor, at, [[head_step, HEADS], [CHUNK, HD], [1, CHUNK]])
                    ).then_inc(attn_in[b], 16)

            def tail():
                store_ctx(PAIRS - 1, SETS - 1)
                load_contexts(0)
                load_contexts(1)
                ov = out.rearrange("b (n k p) c -> (b n) p k c", p=P, k=CHUNK // P)
                for n in range(CHUNKS):
                    sp.wait_ge(final_ready, n + 1)
                    sp.dma_start(ov[n], x_sb[:, 4 * n:4 * n + 4, :]).then_inc(out_done, 16)
                sp.wait_ge(out_done, 16 * CHUNKS)

            program(sp, head, rest, tail)

        @block.gpsimd
        def _(pool):
            g = nc.gpsimd
            g.memset(ident[:, :], 0.0).then_inc(consts, 1)
            g.memset(mean_w[:, :], 1.0 / C).then_inc(mean_w_ok, 1)
            pool.wait_ge(consts, 1)
            g.affine_select(out=ident[:, :], in_=ident[:, :], compare_op=ALU.not_equal, fill=1.0, base=0,
                            pattern=[[-1, P]], channel_multiplier=1).then_inc(ident_ok, 1)
            g.memset(lower[:, :, :], 1.0).then_inc(consts, 1)
            pool.wait_ge(consts, 2)
            g.affine_select(out=lower[:, :, :], in_=lower[:, :, :], compare_op=ALU.is_gt, fill=0.0, base=0,
                            pattern=[[1, EXPERTS], [-1, EXPERTS]], channel_multiplier=0).then_inc(lower_ok, 1)
            g.memset(zero_c[:, :], 0.0)
            g.memset(zero_rows[:, :], 0.0).then_inc(zeros_ok, 1)
            g.memset(eps_c[:, :], EPS).then_inc(eps_ok, 1)
            g.memset(hT[:, :, 0:1], 0.0)
            g.memset(run[:, 0, :, QT:QT + 1], NEG_INF)
            g.memset(run[:, 1, :, QT:QT + 1], 1.0)
            g.memset(run[:, 2:4, :, QT:QT + 1], 0.0).then_inc(run_set, 1)
            pool.nop().then_inc(rt_ready, 1)
            for s in range(2):
                g.memset(ctx_sb[:, s, 0:1], 0.0).then_inc(ctx_out[s], 1)
            g.memset(k_op[:, :, :, :], 0.0).then_inc(cleared, 1)
            g.memset(q_op[:, :, :, :], 0.0).then_inc(cleared, 1)
            pool.wait_ge(cleared, 2)
            g.memset(k_op[MAX_ROW:MAX_ROW + PARTS, :, :, :], 1.0).then_inc(ones_set, 1)
            pool.wait_ge(ones_set, 1)
            g.memset(v_op[:, :, :, :, :], 0.0).then_inc(v_set, 1)
            pool.wait_ge(v_set, 1)
            g.memset(v_op[:, :, :, :, HD:HD + 1], 1.0).then_inc(v_set, 1)
            pool.wait_ge(rows_in, 16)
            pool.wait_ge(x_transposed, CHUNKS)
            for n in range(CHUNKS):
                here = x_sb[:, 4 * n:4 * n + 4, :]
                g.tensor_tensor(here, here, vb_ob[:, 1:2, :].to_broadcast([P, 4, C]), ALU.add).then_inc(xob_ready, 1)
            pool.wait_ge(zeros_ok, 1)
            zeros = zero_c[:, 0:1].to_broadcast([P, CHUNK])
            for n in range(2, CHUNKS):
                pool.wait_ge(qk_ready, CHUNKS + n + 1)
                kf, kr = qk_f[:, 1, n, :], res[:, 1, n, :]
                k0, k1, k2 = (parts[:, 1, i, n, :] for i in range(PARTS))
                g.tensor_tensor(k0, kf, zeros, ALU.add).then_inc(k_part, 1)
                pool.wait_ge(k_part, 3 * n - 5)
                g.tensor_tensor(kr, kf, k0, ALU.subtract).then_inc(k_part, 1)
                pool.wait_ge(k_part, 3 * n - 4)
                g.tensor_tensor(k1, kr, zeros, ALU.add).then_inc(k_part, 1)
                pool.wait_ge(k_part, 3 * n - 3)
                g.tensor_tensor(k2, kr, k1, ALU.subtract).then_inc(k1_split, 1)
            for n in range(CHUNKS):
                pool.wait_ge(rstd_sq, n + 1)
                pool.wait_ge(var_copied, n + 1)
                g.tensor_tensor(xc[:, n, :], xc[:, n, :], var_sb(n), ALU.mult).then_inc(var2_ready, 1)
            for n in range(CHUNKS):
                here = hT[:, n // 2, 1 + CHUNK * (n % 2):1 + CHUNK * (n % 2 + 1)]
                pool.wait_ge(rstd2_ready, n + 1)
                pool.wait_ge(xn_ready, n + 1)
                xn = xnT[:, n // 2, CHUNK * (n % 2):CHUNK * (n % 2 + 1)]
                g.tensor_tensor(here, xn, rstd[:, n, :], ALU.mult).then_inc(h_hat, 1)
            pool.wait_ge(run_set, 1)

            def split_max(p, s, it=0, pair=0):
                rows_, res_ = max_rows[:, s % 2, :], max_res[:, s % 2, :]
                m0, m1, m2 = (max_parts[:, s % 2, i, :] for i in range(PARTS))
                transposed = a_count(it, pair + 1, 2) + 1
                pool.wait_ge(a_read, transposed)
                if not (isinstance(p, int) and p < 2):
                    pool.wait_ge(b_ready, (p - 1) * 16 + 1)
                g.tensor_tensor(m0, rows_, zero_rows[:, :], ALU.add).then_inc(max_part, 1)
                pool.wait_ge(max_part, p * 3 + 1)
                g.tensor_tensor(res_, rows_, m0, ALU.subtract).then_inc(max_part, 1)
                pool.wait_ge(max_part, p * 3 + 2)
                g.tensor_tensor(m1, res_, zero_rows[:, :], ALU.add).then_inc(max_part, 1)
                pool.wait_ge(max_part, p * 3 + 3)
                g.tensor_tensor(m2, res_, m1, ALU.subtract).then_inc(max_parts_ready, 1)

            def less_previous(cur, prev):
                g.tensor_tensor(dh[:, :, :], cur, prev, ALU.subtract).then_inc(shift_diff, 1)

            def mix(q, i, prev, n):
                pool.wait_ge(scaled_diff, q * 5 + n + 1)
                g.tensor_tensor(mix_in[i][:, :, :], mix_in[i][:, :, :], prev, ALU.add).then_inc(mixed, 1)

            def branch(t, q):
                if t == 1:
                    pool.wait_ge(rt_ready, q + 1)
                    ends = run[:, :, :, :].rearrange("p i b t -> p (i b) t")
                    g.tensor_tensor(ends[:, :, 0], ends[:, :, QT], zero_c[:, 0:1].to_broadcast([P, 4 * B]),
                                    ALU.add).then_inc(carried, 1)
                    g.tensor_copy(h_in, hT[:, :, bass.ds(q * QT, QT + 1)]).then_inc(windows, 1)
                    pool.wait_ge(windows, q * 2 + 1)
                    less_previous(h_in[:, :, 1:], h_in[:, :, 0:QT])
                if t == 3:
                    for i in range(3):
                        mix(q, i, h_in[:, :, 0:QT], i)
                    g.tensor_copy(x_in_q, xnT[:, :, bass.ds(q * QT, QT)]).then_inc(windows, 1)
                if t == 5:
                    pool.wait_ge(run_max_ready, q * 2 + 2)
                    for d, above, below in ((d1, run_max[:, :, 0:QT], run_max[:, :, 1:]), (d2, k_q[:, :, :], run_max[:, :, 1:]),
                                            (d3, run_max[:, :, 0:QT], k_q[:, :, :])):
                        g.tensor_tensor(d[:, :, :], above, below, ALU.subtract).then_inc(exponents, 1)
                if t == 9:
                    pool.wait_ge(exponents, q * 3 + 3)
                    pool.wait_ge(log_sum, q + 1)
                    g.tensor_tensor(d3[:, :, :], d3[:, :, :], ln_s[:, :, :], ALU.add).then_inc(pp_less_k, 1)
                if t == 10:
                    pool.wait_ge(weights_ready, q * 4 + 2)
                    g.tensor_tensor(ev[:, :, :], hi_u[:, :, :], v_q[:, :, :], ALU.mult).then_inc(ev_ready, 1)
                if t == 11:
                    pool.wait_ge(weights_ready, q * 4 + 4)
                    g.tensor_tensor(den[:, :, :], lo_y[:, :, :], hi_y[:, :, :], ALU.add).then_inc(den_ready, 1)
                    g.tensor_tensor(num[:, :, :], hi_y[:, :, :], v_q[:, :, :], ALU.mult).then_inc(y_terms, 1)
                if t == 12:
                    pool.wait_ge(log_den, q + 1)
                    g.tensor_tensor(den[:, :, :], den[:, :, :], er[:, :, :], ALU.add).then_inc(log_both, 1)
                    pool.wait_ge(acc_ready, q * 2 + 2)
                    g.tensor_tensor(ev[:, :, :], lo_y[:, :, :], run_acc[:, :, 0:QT], ALU.mult).then_inc(y_terms, 1)
                    pool.wait_ge(y_terms, q * 2 + 2)
                    g.tensor_tensor(num[:, :, :], num[:, :, :], ev[:, :, :], ALU.add).then_inc(num_ready, 1)
                if t == 14:
                    pool.wait_ge(num_ready, q + 1)
                    pool.wait_ge(rec_ready, q + 1)
                    g.tensor_tensor(num[:, :, :], num[:, :, :], rec[:, :, :], ALU.mult).then_inc(ry_ready, 1)
                    pool.wait_ge(ry_ready, q + 1)
                    g.tensor_tensor(x1[:, :, :], num[:, :, :], x_in_q, ALU.add).then_inc(x1_ready, 1)
                if t == 15:
                    pool.wait_ge(centred2, q + 1)
                    g.tensor_tensor(sq2[:, :, :], xc2[:, :, :], xc2[:, :, :], ALU.mult).then_inc(squared2, 1)
                if t == 16:
                    pool.wait_ge(rs2_ready, q + 1)
                    g.tensor_tensor(h2[:, :, 1:], xc2[:, :, :], rs2[:, :, :], ALU.mult).then_inc(h2_hat, 1)
                if t == 17:
                    pool.wait_ge(h2_ready, q + 1)
                    pool.wait_ge(carried, q + 1)
                    less_previous(h2[:, :, 1:], h2[:, :, 0:QT])
                if t == 19:
                    for i in range(2):
                        mix(q, i, h2[:, :, 0:QT], 3 + i)
                if 20 <= t < 24:
                    i = t - 20
                    pool.wait_ge(relu_ready, q * 4 + i + 1)
                    g.tensor_tensor(kk[i][:, :, :], kk[i][:, :, :], kk[i][:, :, :], ALU.mult).then_inc(kk_ready, 1)

            split_max(0, 0)
            pool.wait_ge(h_ready, CHUNKS)

            def head(p, j, it):
                branch(j * KEY_TILES, it)

            def rest(p, j, it):
                for step in range(1, KEY_TILES):
                    branch(j * KEY_TILES + step, it)
                    if step == SPLIT_STEP and (not isinstance(p, int) or p + 1 < PAIRS):
                        split_max(p + 1, (j + 1) % SETS, it, j + 1)

            program(pool, head, rest, lambda: None)

        @block.scalar
        def _(act):
            a = nc.scalar
            a.preload_act_table_set("natural_log_exp_and_others")
            act.nop().then_inc(ctx_copied, 1)
            act.dma_start(col_sb[:, :], cols).then_inc(cols_in, 16)
            act.dma_start(vb_ob[:, :, :], rows.rearrange("(o r) c -> o r c", o=1).to_broadcast([P, 2, C])).then_inc(rows_in, 16)
            act.dma_start(gw1_sb[:, :], gw1).then_inc(small_in, 16)
            act.dma_start(gb1_sb[:, :], gb1).then_inc(small_in, 16)
            act.dma_start(gw2_sb[:, :], gw2).then_inc(small_in, 16)
            act.dma_start(gb2_sb[:, :], gb2.to_broadcast([B, EXPERTS])).then_inc(small_in, 16)
            for n in range(CHUNKS):
                act.wait_ge(x_transposed, n + 1)
                a.copy(xT[:, n, :], bank(n)).then_inc(xT_ready, 1)
            for n in range(CHUNKS):
                act.wait_ge(centred, n + 1)
                a.activation(sq[:, n, :], xc[:, n, :], ACT.Square).then_inc(squared, 1)
            act.wait_ge(eps_ok, 1)
            for n in range(CHUNKS):
                act.wait_ge(var_ready, n + 1)
                a.activation(sq[:, n, :], bank(n), ACT.Ln, bias=eps_c[:, 0:1]).then_inc(log_var, 1)
                a.copy(var_sb(n), bank(n)).then_inc(var_copied, 1)
                act.wait_ge(log_var, n + 1)
                a.activation(rstd[:, n, :], sq[:, n, :], ACT.Exp, scale=-0.5).then_inc(rstd_ready, 1)
            act.wait_ge(gate_h_ps, 1)
            act.wait_ge(small_in, 64)
            a.activation(gate_h[:, :], banks[0:GATE_H, 4, 0:B], ACT.Relu, bias=gb1_sb[:, 0:1],
                         scale=1.0 / T).then_inc(gate_h_ready, 1)
            act.wait_ge(shifted_ready, 1)
            a.activation(gexp[:, :], logits[:, :], ACT.Exp, bias=neg_top[:, 0:1]).then_inc(gexp_ready, 1)
            act.wait_ge(cols_in, 16)
            a.activation(qb_s[:, :], col("qb"), ACT.Copy, scale=SCALE).then_inc(qb_ready, 1)
            a.activation(neg_first[:, :], col("first"), ACT.Copy, scale=-1.0).then_inc(qb_ready, 1)
            act.wait_ge(qb_ready, 2)
            for t, (scale, bias) in enumerate(((SCALE, qb_s[:, 0:1]), (1.0, col("kb")))):
                for n in range(CHUNKS):
                    act.wait_ge(proj_ps, CHUNKS * t + n + 1)
                    a.activation(qk_f[:, t, n, :], bank(4 * t + n), ACT.Identity, bias=bias,
                                 scale=scale).then_inc(qk_ready, 1)

            for n in range(CHUNKS):
                act.wait_ge(xn_ready, n + 1)
                a.activation(xc[:, n, :], rstd[:, n, :], ACT.Square).then_inc(rstd_sq, 1)
            for n in range(CHUNKS):
                act.wait_ge(var2_ready, n + 1)
                a.activation(xc[:, n, :], xc[:, n, :], ACT.Ln, bias=eps_c[:, 0:1]).then_inc(log_var2, 1)
            for n in range(CHUNKS):
                act.wait_ge(log_var2, n + 1)
                a.activation(rstd[:, n, :], xc[:, n, :], ACT.Exp, scale=-0.5).then_inc(rstd2_ready, 1)
            for n in range(CHUNKS):
                here = hT[:, n // 2, 1 + CHUNK * (n % 2):1 + CHUNK * (n % 2 + 1)]
                act.wait_ge(h_hat, n + 1)
                a.activation(here, here, ACT.Identity, bias=col("ln1_b"), scale=col("ln1_g")).then_inc(h_ready, 1)

            def scale_diff(q, names, m):
                act.wait_ge(shift_diff, q * 2 + m + 1)
                for i, name in enumerate(names):
                    a.activation(mix_in[i][:, :, :], dh[:, :, :], ACT.Copy, scale=col(name)).then_inc(scaled_diff, 1)

            weights = ((lo_u, -1.0, 0.0), (hi_u, 1.0, 0.0), (lo_y, -1.0, col("first")), (hi_y, 1.0, neg_first[:, :]))

            def weigh(q, two):
                act.wait_ge(pp_less_k, q + 1)
                for i in two:
                    t, sign, bias = weights[i]
                    a.activation(t[:, :, :], d3[:, :, :], ACT.Relu, scale=sign, bias=bias).then_inc(clipped, 1)
                for i in two:
                    act.wait_ge(clipped, q * 4 + i + 1)
                    a.activation(weights[i][0][:, :, :], weights[i][0][:, :, :], ACT.Exp,
                                 scale=-1.0).then_inc(weights_ready, 1)

            def branch(t, q):
                if t == 2:
                    scale_diff(q, ("mix_k", "mix_v", "mix_r"), 0)
                for i, (out_, func, scale) in enumerate(((k_q, ACT.Copy, 1.0), (v_q, ACT.Copy, 1.0), (er, ACT.Exp, -1.0))):
                    if t == PRODUCT_STEP["kvr"[i]]:
                        act.wait_ge(kvr_ps, q * 3 + i + 1)
                        a.activation(flat(out_), turn_bank(turns.index("kvr"[i])), func, scale=scale).then_inc(kvr_read, 1)
                if t == 6:
                    act.wait_ge(kvr_read, q * 3 + 3)
                    a.activation(er[:, :, :], er[:, :, :], ACT.Ln, bias=1.0).then_inc(log_gate, 1)
                    for i, (d, w) in enumerate(((d1, w1), (d2, w2))):
                        act.wait_ge(exponents, q * 3 + i + 1)
                        a.activation(w[:, :, :], d[:, :, :], ACT.Exp, bias=col("decay")).then_inc(decays_ready, 1)
                if t == 8:
                    act.wait_ge(sum_ready, q * 2 + 2)
                    a.activation(ln_s[:, :, :], run_sum[:, :, 0:QT], ACT.Ln).then_inc(log_sum, 1)
                if t == 9:
                    weigh(q, (0, 1))
                if t == 10:
                    weigh(q, (2, 3))
                if t == 12:
                    act.wait_ge(den_ready, q + 1)
                    a.activation(den[:, :, :], den[:, :, :], ACT.Ln).then_inc(log_den, 1)
                if t == 13:
                    act.wait_ge(log_both, q + 1)
                    a.activation(rec[:, :, :], den[:, :, :], ACT.Exp, scale=-1.0).then_inc(rec_ready, 1)
                if t == PRODUCT_STEP["var"]:
                    act.wait_ge(var2_ps, q + 1)
                    a.activation(flat(rs2), turn_bank(turns.index("var")), ACT.Ln, bias=eps_c[:, 0:1]).then_inc(log_var_q, 1)
                    act.wait_ge(log_var_q, q + 1)
                    a.activation(rs2[:, :, :], rs2[:, :, :], ACT.Exp, scale=-0.5).then_inc(rs2_ready, 1)
                if t == 17:
                    act.wait_ge(h2_hat, q + 1)
                    a.activation(h2[:, :, 1:], h2[:, :, 1:], ACT.Identity, bias=col("ln2_b"), scale=col("ln2_g")).then_inc(h2_ready, 1)
                if t == 18:
                    scale_diff(q, ("cmix_k", "cmix_r"), 1)
                for i in range(4):
                    if t == PRODUCT_STEP[f"ck{i}"]:
                        act.wait_ge(ck_ps, q * 4 + i + 1)
                        a.activation(flat(kk[i]), turn_bank(turns.index(f"ck{i}")), ACT.Relu).then_inc(relu_ready, 1)
                if t == PRODUCT_STEP["cr"]:
                    act.wait_ge(cr_ps, q + 1)
                    a.activation(flat(ecr), turn_bank(turns.index("cr")), ACT.Exp, scale=-1.0).then_inc(cr_step, 1)
                    act.wait_ge(cr_step, q * 2 + 1)
                    a.activation(ecr[:, :, :], ecr[:, :, :], ACT.Ln, bias=1.0).then_inc(cr_step, 1)
                    act.wait_ge(cr_step, q * 2 + 2)
                    a.activation(ecr[:, :, :], ecr[:, :, :], ACT.Exp, scale=-1.0).then_inc(cr_ready, 1)

            def exps(p, step):
                for e in range(2):
                    act.wait_ge(b_ready, p * 16 + 2 * step + e + 1)
                    a.activation(probs[:, (2 * step + e) % 4, :, :], banks[:, 2 * e:2 * e + 2, :],
                                 ACT.Exp).then_inc(b_read, 1)

            def copy_ctx(p, s, before):
                act.wait_ge(pv_done, (p + 1) * 8)
                act.wait_ge(ctx_out[s % 2], before * 64 + 1)
                a.copy(ctx_sb[:, s % 2, :], bank(PV_BANK)).then_inc(ctx_copied, 1)

            def head(p, j, it):
                exps(p, 0)
                branch(j * KEY_TILES, it)
                if not first(p):
                    copy_ctx(p - 1, (j - 1) % SETS, it * 2 + (j - 1) // 2)

            def rest(p, j, it):
                for step in range(1, KEY_TILES):
                    exps(p, step)
                    branch(j * KEY_TILES + step, it)

            def tail():
                copy_ctx(PAIRS - 1, SETS - 1, (PAIRS - 1) // 2)
                for b in range(B):
                    n2 = den_T[:, 2 * b:2 * b + 2, :]
                    act.wait_ge(attn_in[b], 64)
                    a.activation(n2, n2, ACT.Ln).then_inc(den_step, 1)
                    act.wait_ge(den_step, 2 * b + 1)
                    a.activation(n2, n2, ACT.Exp, scale=-1.0).then_inc(den_step, 1)

            program(act, head, rest, tail)

        @block.vector
        def _(dve):
            v = nc.vector
            for n in range(CHUNKS):
                dve.wait_ge(mean_ready, n + 1)
                v.tensor_tensor(xc[:, n, :], xT[:, n, :], bank(4 + n), ALU.subtract).then_inc(centred, 1)
            for n in range(CHUNKS):
                dve.wait_ge(rstd_ready, n + 1)
                v.tensor_tensor(xnT[:, n // 2, CHUNK * (n % 2):CHUNK * (n % 2 + 1)], xc[:, n, :], rstd[:, n, :],
                                ALU.mult).then_inc(xn_ready, 1)
            dve.wait_ge(xn_ready, CHUNKS)
            v.reduce_sum(pooled[:, :], xnT[:, :, :], axis=AX.X).then_inc(pooled_ready, 1)

            chain = [0]

            def link(ins):
                ins.then_inc(gate_chain, 1)
                chain[0] += 1
                dve.wait_ge(gate_chain, chain[0])

            dve.wait_ge(logits_ps, 1)
            dve.wait_ge(small_in, 64)
            link(v.tensor_tensor(logits[:, :], banks[0:B, 4, 8:8 + EXPERTS], gb2_sb[:, :], ALU.add))
            v.tensor_reduce(neg_top[:, :], logits[:, :], axis=AX.X, op=ALU.max, negate=True).then_inc(shifted_ready, 1)
            sh = [B, EXPERTS, EXPERTS]
            of_j = logits[:, :].rearrange("b (o j) -> b o j", o=1).to_broadcast(sh)
            of_e = logits[:, :].rearrange("b (e o) -> b e o", o=1).to_broadcast(sh)
            link(v.tensor_tensor(gt[:, :, :], of_j, of_e, ALU.is_gt))
            link(v.tensor_tensor(eq[:, :, :], of_j, of_e, ALU.is_equal))
            dve.wait_ge(lower_ok, 1)
            link(v.tensor_tensor(eq[:, :, :], eq[:, :, :], lower[:, :, :], ALU.mult))
            link(v.tensor_tensor(gt[:, :, :], gt[:, :, :], eq[:, :, :], ALU.add))
            link(v.reduce_sum(rank[:, :], gt[:, :, :], axis=AX.X))
            link(v.tensor_scalar(chosen[:, :], rank[:, :], 2.0, None, ALU.is_lt))
            dve.wait_ge(gexp_ready, 1)
            link(v.tensor_tensor(gexp[:, :], gexp[:, :], chosen[:, :], ALU.mult))
            link(v.reduce_sum(gsum[:, :], gexp[:, :], axis=AX.X))
            link(v.reciprocal(gsum[:, :], gsum[:, :]))
            link(v.tensor_scalar(gates[:, :], gexp[:, :], gsum[:, 0:1], None, ALU.mult))
            v.tensor_copy(gates_r[:, :, :], gates[:, :].rearrange("b (e o) -> b e o", o=1).to_broadcast(
                [B, EXPERTS, RANK])).then_inc(gates_ready, 1)
            dve.wait_ge(gcol_ps, 1)
            link(v.tensor_copy(gcol[:, :], banks[:, 4, 16:16 + B]))
            dve.wait_ge(cols_in, 16)
            for i, name in enumerate(("qS", "kS", "vS", "oS")):
                v.tensor_scalar(sg[:, i, :], gcol[:, :], col(name), None, ALU.mult).then_inc(sg_ready, 1)
            dve.wait_ge(sg_ready, 4)
            dve.wait_ge(moe_in, 16)
            for i, name in enumerate(("qU", "kU", "vU", "oU")):
                for b in range(B):
                    v.tensor_scalar(u_s[:, i, b, :], mat(name), sg[:, i, b:b + 1], None, ALU.mult).then_inc(us_ready, 1)
            for i, name in enumerate(("qW", "kW", "vW", "oW")):
                dve.wait_ge(weff_ps, i + 1)
                v.tensor_tensor(w_eff[:, i, :, :], bank(WEFF_BANKS[i])[:, 0:B * P].rearrange(
                    "p (b o) -> p b o", b=B), mat(name).rearrange("p (u o) -> p u o", u=1).to_broadcast([P, B, P]),
                    ALU.add).then_inc(weff_ready, 1)
            def split_q(n):
                dve.wait_ge(qk_ready, n + 1)
                qf, qr = qk_f[:, 0, n, :], res[:, 0, n, :]
                q0, q1, q2 = (parts[:, 0, i, n, :] for i in range(PARTS))
                v.tensor_copy(q0, qf).then_inc(q_part, 1)
                dve.wait_ge(q_part, 3 * n + 1)
                v.tensor_tensor(qr, qf, q0, ALU.subtract).then_inc(q_part, 1)
                dve.wait_ge(q_part, 3 * n + 2)
                v.tensor_copy(q1, qr).then_inc(q_part, 1)
                dve.wait_ge(q_part, 3 * n + 3)
                v.tensor_tensor(q2, qr, q1, ALU.subtract).then_inc(q_split, 1)

            def split_k(n):
                dve.wait_ge(qk_ready, CHUNKS + n + 1)
                kf, kr = qk_f[:, 1, n, :], res[:, 1, n, :]
                k0, k1, k2 = (parts[:, 1, i, n, :] for i in range(PARTS))
                v.tensor_copy(k0, kf).then_inc(k0_part, 1)
                dve.wait_ge(k0_part, 3 * n + 1)
                v.tensor_tensor(kr, kf, k0, ALU.subtract).then_inc(k0_part, 1)
                dve.wait_ge(k0_part, 3 * n + 2)
                v.tensor_copy(k1, kr).then_inc(k0_part, 1)
                dve.wait_ge(k0_part, 3 * n + 3)
                v.tensor_tensor(k2, kr, k1, ALU.subtract).then_inc(k0_split, 1)

            for n in (0, 1):
                split_q(n)
            for n in (0, 1):
                split_k(n)
            for n in (2, 3):
                split_q(n)
            dve.wait_ge(rows_in, 16)
            vb = vb_ob[:, 0:1, :].rearrange("p u (r w) -> p u r w", w=2 * HD).to_broadcast([P, 4, 8, 2 * HD])
            for n in range(CHUNKS):
                dve.wait_ge(v_ps, n + 1)
                for k in range(4):
                    tc = 4 * (n % 2) + k
                    ins = v.tensor_tensor(V[:, 8 * (n // 2):8 * (n // 2) + 8, tc, :],
                                          bank(n)[:, P * k:P * k + P].rearrange("p (r w) -> p r w", w=2 * HD),
                                          vb[:, 0, :, :], ALU.add)
                ins.then_inc(v_ready, 1)

            def scan(q, out_, c0, c1, op0, op1, done):
                for b in range(B):
                    data1 = c1.to_broadcast([P, QT]) if c1 is not None and len(c1.shape) == 2 else c1[:, b, :]
                    v.tensor_tensor_scan(out_[:, b, 1:], c0[:, b, :], data1, out_[:, b, 0:1], op0, op1).then_inc(done, 1)

            def branch(t, q):
                if t == 4:
                    dve.wait_ge(carried, q + 1)
                    dve.wait_ge(kvr_read, q * 3 + 1)
                    scan(q, run_max, k_q, col("decay"), ALU.max, ALU.add, run_max_ready)
                if t == 7:
                    dve.wait_ge(decays_ready, q * 2 + 2)
                    scan(q, run_sum, w1, w2, ALU.mult, ALU.add, sum_ready)
                if t == 11:
                    dve.wait_ge(ev_ready, q + 1)
                    scan(q, run_acc, lo_u, ev, ALU.mult, ALU.add, acc_ready)
                if t == PRODUCT_STEP["mean"]:
                    dve.wait_ge(mean2_ps, q + 1)
                    v.tensor_tensor(flat(xc2), flat(x1), turn_bank(turns.index("mean")), ALU.subtract).then_inc(centred2, 1)
                if t == PRODUCT_STEP["cv"]:
                    dve.wait_ge(cr_ready, q + 1)
                    dve.wait_ge(cv_ps, q + 1)
                    v.tensor_tensor(flat(gx), turn_bank(turns.index("cv")), flat(ecr), ALU.mult).then_inc(gated, 1)
                    dve.wait_ge(gated, q + 1)
                    v.tensor_tensor(RT[:, :, bass.ds(q * QT, QT)], x1[:, :, :], gx[:, :, :], ALU.add).then_inc(rt_ready, 1)

            def read_place(it, pair, k, src):
                if not exists(it, pair, k):
                    return
                n, s, pair_n = a_count(it, pair, k), pair % 2, it * SETS + pair
                if k == 2:
                    if not isinstance(pair_n, int) or pair_n >= 2:
                        dve.wait_ge(max_parts_ready, pair_n - 1)
                    dve.wait_ge(a_ready, n + 1)
                    v.tensor_copy(max_rows[:, (s + 1) % 2, :], src[0:2 * KEY_TILES, 0:P]).then_inc(a_read, 1)
                    return
                u = k if k < 2 else k - 1
                dve.wait_ge(a_ready, n + 1)
                v.tensor_reduce(neg_half[:, s, u:u + 1], src, axis=AX.X, op=ALU.max, negate=True).then_inc(a_read, 1)
                if u == 31:
                    dve.wait_ge(a_read, n + 1)
                    v.tensor_reduce(neg_max[:, s, :], neg_half[:, s, :].rearrange("p (c h) -> p c h", h=2),
                                    axis=AX.X, op=ALU.min).then_inc(half_combined, 1)

            for pair, k in places(0, A_PLACES + LEAD):
                read_place(0, pair, k, bank(A_BANK + a_count(0, pair, k) % 3))

            def one_step(t, it):
                for turn in place_turns[t]:
                    read_place(it, *turns[turn], turn_bank(turn))
                branch(t, it)

            def head(p, j, it):
                one_step(j * KEY_TILES, it)

            def rest(p, j, it):
                for step in range(1, KEY_TILES):
                    one_step(j * KEY_TILES + step, it)

            def tail():
                dve.wait_ge(xob_ready, CHUNKS)
                for b in range(B):
                    c2 = ctx_T[:, 2 * b:2 * b + 2, :]
                    dve.wait_ge(attn_in[b], 64)
                    dve.wait_ge(den_step, 2 * b + 2)
                    v.tensor_tensor(c2, c2, den_T[:, 2 * b:2 * b + 2, :], ALU.mult).then_inc(attn_ready, 1)
                    for n in (2 * b, 2 * b + 1):
                        dve.wait_ge(final_ps, n + 1)
                        here = x_sb[:, 4 * n:4 * n + 4, :].rearrange("p k c -> p (k c)")
                        v.tensor_tensor(here, here, bank(n), ALU.add).then_inc(final_ready, 1)

            program(dve, head, rest, tail)

        @block.tensor
        def _(pe):
            mm = nc.tensor.matmul
            pe.wait_ge(ident_ok, 1)
            for n in range(CHUNKS):
                pe.wait_ge(x_in[n], 16)
                for k in range(4):
                    last = nc.tensor.transpose(bank(n)[:, P * k:P * k + P], x_sb[:, 4 * n + k, :], ident[:, :])
                last.then_inc(x_transposed, 1)
            pe.wait_ge(mean_w_ok, 1)
            for n in range(CHUNKS):
                pe.wait_ge(xT_ready, n + 1)
                mm(bank(4 + n), mean_w[:, :], xT[:, n, :], start=True, stop=True).then_inc(mean_ready, 1)
            for n in range(CHUNKS):
                pe.wait_ge(squared, n + 1)
                mm(bank(n), mean_w[:, :], sq[:, n, :], start=True, stop=True).then_inc(var_ready, 1)
            pe.wait_ge(pooled_ready, 1)
            pe.wait_ge(small_in, 64)
            mm(banks[0:GATE_H, 4, 0:B], gw1_sb[:, :], pooled[:, :], start=True, stop=True).then_inc(gate_h_ps, 1)
            pe.wait_ge(gate_h_ready, 1)
            mm(banks[0:B, 4, 8:8 + EXPERTS], gate_h[:, :], gw2_sb[:, :], start=True, stop=True).then_inc(logits_ps, 1)
            pe.wait_ge(gates_ready, 1)
            mm(banks[:, 4, 16:16 + B], gates_r[:, :, :].rearrange("b e r -> b (e r)"), ident[0:B, 0:B],
               start=True, stop=True).then_inc(gcol_ps, 1)
            pe.wait_ge(moe_in, 16)
            for i, name in enumerate(("qV", "kV", "vV", "oV")):
                pe.wait_ge(us_ready, 2 * i + 2)
                mm(bank(WEFF_BANKS[i])[:, 0:B * P], mat(name),
                   u_s[:, i, :, :].rearrange("p b o -> p (b o)"), start=True, stop=True).then_inc(weff_ps, 1)
            for t in range(2):
                pe.wait_ge(weff_ready, 4 if t else 1)
                for n in range(CHUNKS):
                    if t == 0:
                        pe.wait_ge(var_copied, n + 1)
                    mm(bank(4 * t + n), w_eff[:, t, n // 2, :], xnT[:, n // 2, CHUNK * (n % 2):CHUNK * (n % 2 + 1)],
                       start=True, stop=True).then_inc(proj_ps, 1)
            for n in range(CHUNKS):
                pe.wait_ge(qk_ready, n + 1)
                for k in range(4):
                    at = CHUNK * (n % 2) + P * k
                    last = mm(bank(n)[:, P * k:P * k + P], xnT[:, n // 2, at:at + P], w_eff[:, 2, n // 2, :],
                              start=True, stop=True)
                last.then_inc(v_ps, 1)
            pe.wait_ge(v_ready, CHUNKS)
            pe.wait_ge(qk_ready, 2 * CHUNKS)
            pe.wait_ge(rest_in, 16)

            pe.wait_ge(ones_set, 1)

            def fill_place(it, pair, k, dst):
                s = pair % SETS
                if k == 2:
                    pe.wait_ge(half_combined, it * SETS + pair)
                    nc.tensor.transpose(dst[0:2 * KEY_TILES, 0:P], neg_max[:, (pair + 1) % 2, :],
                                        ident[:, :]).then_inc(a_ready, 1)
                    return
                u = k if k < 2 else k - 1
                if u == 0:
                    pe.wait_ge(op_in[s], (it + pair // SETS + 1) * 48)
                e, c, h = u // 16, u // 2 % 8, u % 2
                mm(dst, q_op[0:MAX_ROW, s, e, P * c:P * c + P],
                   k_op[0:MAX_ROW, s, e, CHUNK * h:CHUNK * h + CHUNK],
                   start=True, stop=True).then_inc(a_ready, 1)

            for pair, k in places(0, A_PLACES + LEAD):
                if exists(0, pair, k):
                    n = a_count(0, pair, k)
                    if n >= 3:
                        pe.wait_ge(a_read, n - 2)
                    fill_place(0, pair, k, bank(A_BANK + n % 3))

            def fill_turn(it, turn):
                if exists(it, *turns[turn]):
                    wait_for_bank(pe, it, turn)
                    fill_place(it, *turns[turn], turn_bank(turn))

            def product(q, name):
                turn = turns.index(name)
                dst = turn_bank(turn)
                wait_for_bank(pe, q, turn)
                if name in "kvr":
                    i = "kvr".index(name)
                    pe.wait_ge(mixed, q * 5 + i + 1)
                    mm(dst, mat("t" + name), flat(mix_in[i]), start=True, stop=True).then_inc(kvr_ps, 1)
                elif name == "mean":
                    pe.wait_ge(x1_ready, q + 1)
                    mm(dst, mean_w[:, :], flat(x1), start=True, stop=True).then_inc(mean2_ps, 1)
                elif name == "var":
                    pe.wait_ge(squared2, q + 1)
                    mm(dst, mean_w[:, :], flat(sq2), start=True, stop=True).then_inc(var2_ps, 1)
                elif name == "cr":
                    pe.wait_ge(mixed, q * 5 + 5)
                    mm(dst, mat("cr"), flat(mix_in[1]), start=True, stop=True).then_inc(cr_ps, 1)
                elif name == "cv":
                    for i in range(4):
                        pe.wait_ge(kk_ready, q * 4 + i + 1)
                        last = mm(dst, mat(f"cv{i}"), flat(kk[i]), start=(i == 0), stop=(i == 3))
                    last.then_inc(cv_ps, 1)
                else:
                    pe.wait_ge(mixed, q * 5 + 4)
                    mm(dst, mat(name), flat(mix_in[0]), start=True, stop=True).then_inc(ck_ps, 1)

            def scores(p, s, step, e):
                if not (first(p) and step == 0):
                    pe.wait_ge(b_read, p * 16 + 2 * step + e - 1)
                for h in range(2):
                    last = mm(bank(2 * e + h), k_op[0:MAX_ROW + PARTS, s, e, P * step:P * step + P],
                              q_op[0:MAX_ROW + PARTS, s, e, CHUNK * h:CHUNK * h + CHUNK], start=True, stop=True)
                last.then_inc(b_ready, 1)

            def values(p, s, step):
                pe.wait_ge(b_read, p * 16 + 2 * step + 2)
                for e in range(2):
                    for h in range(2):
                        g = 32 * (2 * e + h)
                        last = mm(banks[g:g + 32, PV_BANK, :], v_op[:, s % 2, step, e, :],
                                  probs[:, (2 * step + e) % 4, h, :], start=(step == 0), stop=(step == KEY_TILES - 1))
                last.then_inc(pv_done, 1)

            def one_step(p, j, it, step):
                t = j * KEY_TILES + step
                todo = place_turns[t]
                scores(p, j, step, 0)
                for turn in todo[:2]:
                    fill_turn(it, turn)
                scores(p, j, step, 1)
                for turn in todo[2:]:
                    fill_turn(it, turn)
                for name, at in PRODUCT_STEP.items():
                    if at == t:
                        product(it, name)

            def head(p, j, it):
                pe.wait_ge(max_in[j % 2], (it * 2 + j // 2 + 1) * 16 * PARTS)
                one_step(p, j, it, 0)
                if not first(p):
                    values(p - 1, (j - 1) % SETS, KEY_TILES - 1)

            def rest(p, j, it):
                for step in range(1, KEY_TILES):
                    one_step(p, j, it, step)
                    if step == 1:
                        pe.wait_ge(v_in[j % 2], (it * 2 + j // 2 + 1) * 32)
                        pe.wait_ge(ctx_copied, p + 1)
                    values(p, j % SETS, step - 1)

            def tail():
                values(PAIRS - 1, SETS - 1, KEY_TILES - 1)
                pe.wait_ge(b_read, PAIRS * 2 * KEY_TILES)
                pe.wait_ge(rt_ready, QUARTERS + 1)
                for n in range(CHUNKS):
                    for k in range(4):
                        at, dst = CHUNK * (n % 2) + P * k, bank(n)[:, P * k:P * k + P]
                        mm(dst, RT[:, n // 2, at:at + P], ident[:, :], start=(k == 0), stop=False)
                for n in range(CHUNKS):
                    pe.wait_ge(attn_ready, n // 2 + 1)
                    for k in range(4):
                        last = mm(bank(n)[:, P * k:P * k + P], ctx_T[:, n, P * k:P * k + P],
                                  w_eff[:, 3, n // 2, :], start=False, stop=(k == 3))
                    last.then_inc(final_ps, 1)

            program(pe, head, rest, tail)


def kernel(**inputs):
    import numpy as np
    import concourse.bacc as bacc
    from concourse.bass_utils import run_bass_kernel_spmd

    def arr(name):
        return np.asarray(inputs[name])

    a, f = "L0_attn_", "L0_ffn_"
    col_of = {n: arr(a + n).reshape(C) for n in COLS[:9]}
    col_of.update(decay=arr(a + "time_decay"), first=arr(a + "time_first"), qb=arr(f + "qb"), kb=arr(f + "kb"))
    for p in "qkvo":
        col_of[p + "S"] = arr(f + p + "S").reshape(EXPERTS * RANK)
    mat_of = {n: arr(a + "w_" + n) for n in ("tk", "tv", "tr", "cr")}
    for i in range(4):
        mat_of[f"ck{i}"] = arr(a + "w_ck")[:, P * i:P * (i + 1)]
        mat_of[f"cv{i}"] = arr(a + "w_cv")[P * i:P * (i + 1), :]
    for p in "qkvo":
        mat_of[p + "W"] = arr(f + p + "Wm").T
        mat_of[p + "V"] = arr(f + p + "V").reshape(EXPERTS * RANK, C)
        mat_of[p + "U"] = arr(f + p + "U").transpose(0, 2, 1).reshape(EXPERTS * RANK, C)
    arrays = {
        "x": arr(a + "x"),
        "cols": np.stack([col_of[n] for n in COLS], axis=1),
        "mats": np.stack([mat_of[n] for n in MATS], axis=1),
        "rows": np.stack([arr(f + "vb"), arr(f + "ob")]),
        "gw1": arr(f + "gw1").T,
        "gb1": arr(f + "gb1").reshape(GATE_H, 1),
        "gw2": arr(f + "gw2").T,
        "gb2": arr(f + "gb2").reshape(1, EXPERTS),
    }
    arrays = {f"in_{n}_dram": np.ascontiguousarray(v) for n, v in arrays.items()}
    nc = bacc.Bacc("TRN2", target_bir_lowering=False, num_devices=1)
    args = [nc.dram_tensor(n, v.shape, mybir.dt.from_np(v.dtype), kind="ExternalInput").ap()
            for n, v in arrays.items()]
    out = nc.dram_tensor("out_0_dram", (B, T, C), mybir.dt.float32, kind="ExternalOutput").ap()
    build(nc, *args, out)
    r = run_bass_kernel_spmd(nc, [arrays], core_ids=[0])
    return r.results[0]["out_0_dram"]
```

```python
import concourse.bass as bass
from concourse import mybir
from contextlib import ExitStack

B, T, C = 2, 1024, 128
P = 128
TILES = B * T // P
CHUNK = 512
CHUNKS = B * T // CHUNK
HEADS, HD = 16, 8
EXPERTS, RANK, GATE_H = 8, 16, 32
PAIRS = B * HEADS // 2
KEY_TILES = T // P
PARTS = 3
ROWS = PARTS * PARTS * HD
MAX_ROW = 96
PROJECT_EARLY, PROJECT_FROM, PROJECT_GAP = 4, 2, 5
LEAD = 12
SPLIT_STEP = 5
A_PLACES = 33
PV_BANK, A_BANK = 4, 5
WEFF_BANKS = (6, 7, 2, 3)
QK_ORDER = [(0, 0), (0, 1), (1, 0), (1, 1), (0, 2), (0, 3), (1, 2), (1, 3)]
SETS = 4
QUARTERS, QT = 4, 256
PRODUCT_STEP = {"mean": 17, "var": 18, "cr": 22, "ck0": 23, "ck1": 25, "ck2": 26, "ck3": 27, "cv": 29}
SLOTS = 2 * PARTS - 1
PARTS_OUT = 16 * (PARTS + SLOTS)
EPS = 1e-5
NEG_INF = -1e38
SCALE = float(HD) ** -0.5

COLS = ["ln1_g", "ln1_b", "ln2_g", "ln2_b", "mix_k", "mix_v", "mix_r", "cmix_k", "cmix_r",
        "decay", "first", "qb", "kb", "qS", "kS", "vS", "oS"]
MATS = ["qW", "kW", "vW", "oW", "qV", "kV", "vV", "oV", "qU", "kU", "vU", "oU",
        "tk", "tv", "tr", "cr", "ck0", "ck1", "ck2", "ck3", "cv0", "cv1", "cv2", "cv3"]
MOE = 12


def build(nc, x, cols, mats, rows, gw1, gb1, gw2, gb2, out):
    F32, BF16 = mybir.dt.float32, mybir.dt.bfloat16
    ALU, ACT, AX = mybir.AluOpType, mybir.ActivationFunctionType, mybir.AxisListType

    ctx = ExitStack()
    with ctx:
        def sb(name, shape, dt=F32):
            return ctx.enter_context(nc.sbuf_tensor(name, shape, dt))

        def sem(name):
            return ctx.enter_context(nc.semaphore(name))

        col_sb = sb("col_sb", [P, len(COLS)])
        mat_sb = sb("mat_sb", [P, len(MATS), P])
        vb_ob = sb("vb_ob", [P, 2, C])
        gw1_sb = sb("gw1_sb", [C, GATE_H])
        gb1_sb = sb("gb1_sb", [GATE_H, 1])
        gw2_sb = sb("gw2_sb", [GATE_H, EXPERTS])
        gb2_sb = sb("gb2_sb", [B, EXPERTS])
        x_sb = sb("x_sb", [P, TILES, C])
        xT = sb("xT", [P, CHUNKS, CHUNK])
        xc = sb("xc", [P, CHUNKS, CHUNK])
        sq = sb("sq", [P, CHUNKS, CHUNK])
        rstd = sb("rstd", [P, CHUNKS, CHUNK])
        xnT = sb("xnT", [P, B, T])
        hT = sb("hT", [P, B, 1 + T])
        RT = sb("RT", [P, B, T])
        ident = sb("ident", [P, P])
        mean_w = sb("mean_w", [P, P])
        eps_c = sb("eps_c", [P, 1])
        zero_c = sb("zero_c", [P, 1])
        neg_first = sb("neg_first", [P, 1])
        qb_s = sb("qb_s", [P, 1])
        pool_sums = sb("pool_sums", [C, CHUNKS])
        pooled = sb("pooled", [C, B])
        gate_h = sb("gate_h", [GATE_H, B])
        logits = sb("logits", [B, EXPERTS])
        gt = sb("gt", [B, EXPERTS, EXPERTS])
        eq = sb("eq", [B, EXPERTS, EXPERTS])
        lower = sb("lower", [B, EXPERTS, EXPERTS])
        rank = sb("rank", [B, EXPERTS])
        chosen = sb("chosen", [B, EXPERTS])
        neg_top = sb("neg_top", [B, 1])
        gexp = sb("gexp", [B, EXPERTS])
        gsum = sb("gsum", [B, 1])
        gates = sb("gates", [B, EXPERTS])
        gates_r = sb("gates_r", [B, EXPERTS, RANK])
        gcol = sb("gcol", [P, B])
        sg = sb("sg", [P, 4, B])
        u_s = sb("u_s", [P, 4, B, P])
        w_eff = sb("w_eff", [P, 4, B, P])
        qk_f = sb("qk_f", [P, 2, CHUNKS, CHUNK])
        parts = sb("parts", [P, 2, PARTS, CHUNKS, CHUNK], BF16)
        ctx_T, den_T = (parts[:, t, 0:2, :, :].rearrange("p i n t -> p (i n t)").bitcast(F32).rearrange(
            "p (n t) -> p n t", t=CHUNK) for t in range(2))
        V = sb("V", [P, PAIRS, KEY_TILES, 2 * HD])
        q_op = sb("q_op", [P, SETS, 2, T], BF16)
        k_op = sb("k_op", [P, SETS, 2, T], BF16)
        v_op = sb("v_op", [P, 2, KEY_TILES, 2, 32])
        probs = sb("probs", [P, 4, 2, CHUNK])
        res = probs[:, :, :, :].rearrange("p (t n) h c -> p t (n h) c", t=2)
        neg_half = sb("neg_half", [P, 2, KEY_TILES * 2 * 2])
        neg_max = sb("neg_max", [P, 2, KEY_TILES * 2])
        max_rows = sb("max_rows", [2 * KEY_TILES, 2, P])
        max_res = sb("max_res", [2 * KEY_TILES, 2, P])
        zero_rows = sb("zero_rows", [2 * KEY_TILES, P])
        max_parts = sb("max_parts", [2 * KEY_TILES, 2, PARTS, P], BF16)
        ctx_sb = sb("ctx_sb", [P, 2, CHUNK])
        q_dram = nc.dram_tensor("q_dram", [B * HEADS, PARTS, HD, T], BF16).ap()
        k_dram = nc.dram_tensor("k_dram", [B * HEADS, SLOTS, HD, T], BF16).ap()
        ctx_dram = nc.dram_tensor("ctx_dram", [PAIRS, 4, HD + 1, CHUNK], F32).ap()

        banks = ctx.enter_context(nc.psum_tensor("banks", [P, 8, CHUNK], F32))

        def col(name):
            i = COLS.index(name)
            return col_sb[:, i:i + 1]

        def mat(name):
            return mat_sb[:, MATS.index(name), :]

        centred2 = sem("centred2")
        log_var_q = sem("log_var_q")
        cr_step = sem("cr_step")
        gated = sem("gated")
        relu_ready = sem("relu_ready")
        a_read = sem("a_read")
        max_parts_ready = sem("max_parts_ready")
        ctx_copied = sem("ctx_copied")
        moe_in = sem("moe_in")
        rest_in = sem("rest_in")
        cleared = sem("cleared")
        ones_set = sem("ones_set")
        q_split = sem("q_split")
        k_split = sem("k_split")
        k1_split = sem("k1_split")
        v_ready = sem("v_ready")
        v_set = sem("v_set")
        b_ready = sem("b_ready")
        pv_done = sem("pv_done")
        final_ready = sem("final_ready")
        out_done = sem("out_done")
        consts = sem("consts")
        mean_w_ok = sem("mean_w_ok")
        ident_ok = sem("ident_ok")
        lower_ok = sem("lower_ok")
        zeros_ok = sem("zeros_ok")
        eps_ok = sem("eps_ok")
        run_set = sem("run_set")
        rt_ready = sem("rt_ready")
        keys_cleared = sem("keys_cleared")
        rstd_sq = sem("rstd_sq")
        var_copied = sem("var_copied")
        var2_ready = sem("var2_ready")
        rstd2_ready = sem("rstd2_ready")
        xn_ready = sem("xn_ready")
        h_hat = sem("h_hat")
        qk_ready = sem("qk_ready")
        k_part = sem("k_part")
        rows_in = sem("rows_in")
        x_transposed = sem("x_transposed")
        xob_ready = sem("xob_ready")
        max_part = sem("max_part")
        shift_diff = sem("shift_diff")
        scaled_diff = sem("scaled_diff")
        mixed = sem("mixed")
        carried = sem("carried")
        windows = sem("windows")
        run_max_ready = sem("run_max_ready")
        exponents = sem("exponents")
        log_sum = sem("log_sum")
        pp_less_k = sem("pp_less_k")
        weights_ready = sem("weights_ready")
        ev_ready = sem("ev_ready")
        den_ready = sem("den_ready")
        y_terms = sem("y_terms")
        log_den = sem("log_den")
        log_both = sem("log_both")
        acc_ready = sem("acc_ready")
        num_ready = sem("num_ready")
        rec_ready = sem("rec_ready")
        ry_ready = sem("ry_ready")
        x1_ready = sem("x1_ready")
        squared2 = sem("squared2")
        rs2_ready = sem("rs2_ready")
        h2_hat = sem("h2_hat")
        h2_ready = sem("h2_ready")
        kk_ready = sem("kk_ready")
        kvr_read = sem("kvr_read")
        gate_ready = sem("gate_ready")
        cols_in = sem("cols_in")
        small_in = sem("small_in")
        xT_ready = sem("xT_ready")
        centred = sem("centred")
        squared = sem("squared")
        var_ready = sem("var_ready")
        log_var = sem("log_var")
        rstd_ready = sem("rstd_ready")
        gate_h_ps = sem("gate_h_ps")
        gate_h_ready = sem("gate_h_ready")
        shifted_ready = sem("shifted_ready")
        gexp_ready = sem("gexp_ready")
        log_var2 = sem("log_var2")
        h_ready = sem("h_ready")
        qb_ready = sem("qb_ready")
        proj_ps = sem("proj_ps")
        less_ready = sem("less_ready")
        weff_ps = sem("weff_ps")
        w_mix_ready = sem("w_mix_ready")
        kvr_ps = sem("kvr_ps")
        decays_ready = sem("decays_ready")
        sum_ready = sem("sum_ready")
        clipped = sem("clipped")
        var2_ps = sem("var2_ps")
        ck_ps = sem("ck_ps")
        cr_ps = sem("cr_ps")
        cr_ready = sem("cr_ready")
        b_read = sem("b_read")
        den_step = sem("den_step")
        mean_ready = sem("mean_ready")
        summed = sem("summed")
        pooled_ready = sem("pooled_ready")
        gate_chain = sem("gate_chain")
        logits_ps = sem("logits_ps")
        gates_ready = sem("gates_ready")
        gcol_ps = sem("gcol_ps")
        sg_ready = sem("sg_ready")
        us_ready = sem("us_ready")
        weff_ready = sem("weff_ready")
        q_part = sem("q_part")
        v_ps = sem("v_ps")
        mean2_ps = sem("mean2_ps")
        cv_ps = sem("cv_ps")
        a_ready = sem("a_ready")
        half_combined = sem("half_combined")
        attn_ready = sem("attn_ready")
        final_ps = sem("final_ps")
        x_in = [sem(f"x_in{n}") for n in range(CHUNKS)]
        parts_out = [sem(f"parts_out{b}") for b in range(B)]
        op_in = [[sem(f"op_in{s}{e}") for e in range(2)] for s in range(SETS)]
        v_in = [sem(f"v_in{s}") for s in range(2)]
        max_in = [sem(f"max_in{s}") for s in range(2)]
        ctx_out = [sem(f"ctx_out{s}") for s in range(2)]
        attn_in = [sem(f"attn_in{n}") for n in range(CHUNKS)]

        w_mix = u_s[:, 0:3, :, :]
        less_mix = sb("less_mix", [P, 3])
        k_all, v_all, gate_all = ([t[:, n, :] for n in range(CHUNKS)] for t in (xT, sq, rstd))
        k_of, v_of, gate_of = (t[:, :, :].rearrange("p (b h) t -> p b (h t)", b=B) for t in (xT, sq, rstd))
        spare = [t[:, n, :] for t in (xc, qk_f[:, 0, :, :], qk_f[:, 1, :, :]) for n in range(CHUNKS)]
        spare += [hT[:, :, :].rearrange("p b t -> p (b t)")[:, CHUNK * n:CHUNK * (n + 1)] for n in range(CHUNKS)]
        spare += [parts[:, t, 2, 2 * n:2 * n + 2, :].rearrange("p n t -> p (n t)").bitcast(F32)
                  for t in range(2) for n in range(2)]
        (dh, mix_r, mix_k, d1, d2, d3, w1, w2, ln_s, lo_u, hi_u, lo_y, hi_y, ev, num, den,
         k_q, v_q, gate_q, x_q) = (t.rearrange("p (b t) -> p b t", b=B) for t in spare)
        mix_in = [mix_r, mix_k]
        rec = sb("rec", [P, B, QT])
        x1, sq2, xc2, rs2 = w1, d1, d2, d3
        kk = [lo_u, hi_u, lo_y, hi_y]
        ecr, gx = gate_q, rec
        run = sb("run", [P, 4, B, QT + 1])
        run_max, run_sum, run_acc, h2 = (run[:, i, :, :] for i in range(4))

        def var_sb(n):
            return RT[:, n // 2, CHUNK * (n % 2):CHUNK * (n % 2 + 1)]

        def bank(i):
            return banks[:, i, :]

        def project_bank(m):
            return bank(4 + m if m < 4 else m % 4)

        def flat(t):
            return t[:, :, :].rearrange("p b t -> p (b t)")

        def places(first, last):
            return [divmod(n, A_PLACES) for n in range(first, last)]

        def exists(it, pair, k):
            n = it * SETS + pair
            if not isinstance(n, int):
                return True
            return 1 <= n <= PAIRS if k == 2 else n < PAIRS

        def a_count(it, pair, k):
            n = it * SETS + pair
            if isinstance(n, int) and n == 0:
                return k if k < 2 else k - 1
            if isinstance(n, int) and n == PAIRS:
                return PAIRS * A_PLACES - 1
            return n * A_PLACES + k - 1

        turns, place_turns = [], []
        for t in range(SETS * KEY_TILES):
            at = A_PLACES + LEAD
            here = places(at + A_PLACES * t // KEY_TILES, at + A_PLACES * (t + 1) // KEY_TILES)
            place_turns.append(range(len(turns), len(turns) + len(here)))
            turns += here
            turns += [name for name, step in PRODUCT_STEP.items() if step == t]
        assert (len(turns) + 1) % 3 == 0

        def product_bank(name):
            return turn_bank(turns.index(name))

        def turn_bank(turn):
            return bank(A_BANK + (turn + A_PLACES + LEAD - 1) % 3)

        taken_by = {"mean": (centred2, 1, 1), "var": (log_var_q, 1, 1), "cr": (cr_step, 2, 1),
                    "cv": (gated, 1, 1)}
        for i in range(4):
            taken_by[f"ck{i}"] = (relu_ready, 4, i + 1)

        def wait_for_bank(pe, it, turn):
            if turn < 3:
                pe.wait_ge(a_read, a_count(it, *turns[turn]) - 1)
                return
            turn -= 3
            while isinstance(turns[turn], tuple) and not exists(it, *turns[turn]):
                turn -= 3
            if isinstance(turns[turn], tuple):
                pe.wait_ge(a_read, a_count(it, *turns[turn]) + 1)
            else:
                taken, of, n = taken_by[turns[turn]]
                pe.wait_ge(taken, it * of + n)

        def program(eng, head, rest, tail):
            head(0, 0, 0)
            with eng.Fori(0, PAIRS // SETS - 1) as it:
                for j in range(SETS):
                    rest(it * SETS + j, j, it)
                    head(it * SETS + j + 1, (j + 1) % SETS, it + (j + 1) // SETS)
            for p in range(PAIRS - SETS, PAIRS):
                rest(p, p % SETS, p // SETS)
                if p + 1 < PAIRS:
                    head(p + 1, (p + 1) % SETS, (p + 1) // SETS)
            tail()

        def first(p):
            return isinstance(p, int) and p == 0

        block = ctx.enter_context(nc.Block())

        @block.sync
        def _(sp):
            def load_pair(p, s):
                for e in range(2):
                    sp.dma_start(q_op[0:ROWS, s, e, :],
                                 bass.AP(q_dram.tensor, (p * 2 + e) * (PARTS * HD * T),
                                         [[0, PARTS], [T, PARTS * HD], [1, T]])).then_inc(op_in[s][e], 16)
                    sp.dma_start(k_op[0:ROWS, s, e, :],
                                 bass.AP(k_dram.tensor, (p * 2 + e) * (SLOTS * HD * T),
                                         [[HD * T, PARTS], [T, PARTS * HD], [1, T]])).then_inc(op_in[s][e], 16)

            def place_max(p, s):
                sp.wait_ge(max_parts_ready, p + 1)
                for i in range(PARTS):
                    sp.dma_start(q_op[MAX_ROW + i:MAX_ROW + i + 1, s, :, :],
                                 max_parts[:, s % 2, i, :]).then_inc(max_in[s % 2], 16)

            def stage_v(p, s):
                for e in range(2):
                    sp.dma_start(v_op[:, s % 2, :, e, 0:HD],
                                 V[:, bass.ds(p, 1), :, HD * e:HD * e + HD].rearrange("p o k d -> p (o k) d")
                                 ).then_inc(v_in[s % 2], 16)

            def store_ctx(p, s):
                sp.wait_ge(ctx_copied, p + 2)
                for g in range(4):
                    sp.dma_start(bass.AP(ctx_dram.tensor, (p * 4 + g) * ((HD + 1) * CHUNK),
                                         [[CHUNK, HD + 1], [1, CHUNK]]),
                                 ctx_sb[32 * g:32 * g + HD + 1, s % 2, :]).then_inc(ctx_out[s % 2], 16)

            xv = x.rearrange("b (n k p) c -> (b n) p k c", p=P, k=CHUNK // P)
            for n in range(CHUNKS):
                sp.dma_start(x_sb[:, 4 * n:4 * n + 4, :], xv[n]).then_inc(x_in[n], 16)
            sp.dma_start(mat_sb[:, 0:MOE, :], mats[:, 0:MOE, :]).then_inc(moe_in, 16)
            sp.dma_start(mat_sb[:, MOE:, :], mats[:, MOE:, :]).then_inc(rest_in, 16)
            sp.wait_ge(cleared, 1)
            sp.wait_ge(ones_set, 1)
            def store_parts(b, t):
                for slot in range(SLOTS if t else PARTS):
                    sp.dma_start((k_dram if t else q_dram)[b * HEADS:(b + 1) * HEADS, slot, :, :],
                                 parts[:, t, slot % PARTS, 2 * b:2 * b + 2, :].rearrange("p n t -> p (n t)")
                                 ).then_inc(parts_out[b], 16)

            sp.wait_ge(q_split, 2)
            store_parts(0, 0)
            sp.wait_ge(k_split, 1)
            sp.wait_ge(k1_split, 1)
            store_parts(0, 1)
            sp.wait_ge(parts_out[0], PARTS_OUT)
            for p in range(3):
                load_pair(p, p)
            sp.wait_ge(q_split, 4)
            store_parts(1, 0)
            sp.wait_ge(k_split, 3)
            store_parts(1, 1)
            sp.wait_ge(v_ready, CHUNKS)
            sp.wait_ge(v_set, 2)
            stage_v(0, 0)
            place_max(0, 0)
            sp.wait_ge(parts_out[1], PARTS_OUT)

            def head(p, j, it):
                if not first(p):
                    store_ctx(p - 1, (j - 1) % SETS)

            def rest(p, j, it):
                if not isinstance(p, int) or p + 3 < PAIRS:
                    sp.wait_ge(b_ready, p * 16 + 1)
                    load_pair(p + 3, (j + 3) % SETS)
                if not isinstance(p, int) or p + 1 < PAIRS:
                    sp.wait_ge(pv_done, p * 8 + 1)
                    stage_v(p + 1, (j + 1) % SETS)
                    place_max(p + 1, (j + 1) % SETS)

            def load_contexts(b):
                for s in range(2):
                    sp.wait_ge(ctx_out[s], 64 * (PAIRS // 4) * (b + 1) + 1)
                for hs in range(2):
                    at = (b * (HEADS // 2) * 4 + hs) * (HD + 1) * CHUNK
                    head_step = 2 * (HD + 1) * CHUNK
                    sp.dma_start(den_T[:, 2 * b + hs, :], bass.AP(
                        ctx_dram.tensor, at + HD * CHUNK, [[head_step, HEADS], [0, HD], [1, CHUNK]])
                    ).then_inc(attn_in[2 * b + hs], 16)
                    sp.dma_start(ctx_T[:, 2 * b + hs, :], bass.AP(
                        ctx_dram.tensor, at, [[head_step, HEADS], [CHUNK, HD], [1, CHUNK]])
                    ).then_inc(attn_in[2 * b + hs], 16)

            def tail():
                load_contexts(0)
                store_ctx(PAIRS - 1, SETS - 1)
                load_contexts(1)
                ov = out.rearrange("b (n k p) c -> (b n) p k c", p=P, k=CHUNK // P)
                for n in range(CHUNKS):
                    sp.wait_ge(final_ready, n + 1)
                    sp.dma_start(ov[n], x_sb[:, 4 * n:4 * n + 4, :]).then_inc(out_done, 16)
                sp.wait_ge(out_done, 16 * CHUNKS)

            program(sp, head, rest, tail)

        @block.gpsimd
        def _(pool):
            g = nc.gpsimd
            g.memset(ident[:, :], 0.0).then_inc(consts, 1)
            g.memset(mean_w[:, :], 1.0 / C).then_inc(mean_w_ok, 1)
            pool.wait_ge(consts, 1)
            g.affine_select(out=ident[:, :], in_=ident[:, :], compare_op=ALU.not_equal, fill=1.0, base=0,
                            pattern=[[-1, P]], channel_multiplier=1).then_inc(ident_ok, 1)
            g.memset(lower[:, :, :], 1.0).then_inc(consts, 1)
            pool.wait_ge(consts, 2)
            g.affine_select(out=lower[:, :, :], in_=lower[:, :, :], compare_op=ALU.is_gt, fill=0.0, base=0,
                            pattern=[[1, EXPERTS], [-1, EXPERTS]], channel_multiplier=0).then_inc(lower_ok, 1)
            g.memset(zero_c[:, :], 0.0)
            g.memset(zero_rows[:, :], 0.0).then_inc(zeros_ok, 1)
            g.memset(eps_c[:, :], EPS).then_inc(eps_ok, 1)
            g.memset(hT[:, :, 0:1], 0.0)
            g.memset(run[:, 0, :, QT:QT + 1], NEG_INF)
            g.memset(run[:, 1, :, QT:QT + 1], 1.0)
            g.memset(run[:, 2:4, :, QT:QT + 1], 0.0).then_inc(run_set, 1)
            pool.nop().then_inc(rt_ready, 1)
            for s in range(2):
                g.memset(ctx_sb[:, s, 0:1], 0.0).then_inc(ctx_out[s], 1)
            g.memset(q_op[:, :, :, :], 0.0).then_inc(cleared, 1)
            pool.wait_ge(cleared, 1)
            pool.wait_ge(keys_cleared, 1)
            g.memset(k_op[MAX_ROW:MAX_ROW + PARTS, :, :, :], 1.0).then_inc(ones_set, 1)
            pool.wait_ge(ones_set, 1)
            g.memset(v_op[:, :, :, :, :], 0.0).then_inc(v_set, 1)
            pool.wait_ge(v_set, 1)
            g.memset(v_op[:, :, :, :, HD:HD + 1], 1.0).then_inc(v_set, 1)
            for n in range(CHUNKS):
                pool.wait_ge(rstd_sq, n + 1)
                pool.wait_ge(var_copied, n + 1)
                g.tensor_tensor(xc[:, n, :], xc[:, n, :], var_sb(n), ALU.mult).then_inc(var2_ready, 1)
            for n in range(CHUNKS):
                here = hT[:, n // 2, 1 + CHUNK * (n % 2):1 + CHUNK * (n % 2 + 1)]
                pool.wait_ge(rstd2_ready, n + 1)
                pool.wait_ge(xn_ready, n + 1)
                xn = xnT[:, n // 2, CHUNK * (n % 2):CHUNK * (n % 2 + 1)]
                g.tensor_tensor(here, xn, rstd[:, n, :], ALU.mult).then_inc(h_hat, 1)
            pool.wait_ge(zeros_ok, 1)
            zeros = zero_c[:, 0:1].to_broadcast([P, CHUNK])
            def split_k(m, n):
                pool.wait_ge(qk_ready, QK_ORDER.index((1, n)) + 1)
                kf, kr = qk_f[:, 1, n, :], res[:, 1, n, :]
                k0, k1, k2 = (parts[:, 1, i, n, :] for i in range(PARTS))
                g.tensor_tensor(k0, kf, zeros, ALU.add).then_inc(k_part, 1)
                pool.wait_ge(k_part, 3 * m + 1)
                g.tensor_tensor(kr, kf, k0, ALU.subtract).then_inc(k_part, 1)
                pool.wait_ge(k_part, 3 * m + 2)
                g.tensor_tensor(k1, kr, zeros, ALU.add).then_inc(k_part, 1)
                pool.wait_ge(k_part, 3 * m + 3)
                g.tensor_tensor(k2, kr, k1, ALU.subtract).then_inc(k_split, 1)
            split_k(0, 0)
            split_k(1, 2)
            split_k(2, 3)
            pool.wait_ge(rows_in, 16)
            pool.wait_ge(x_transposed, CHUNKS)
            for n in range(CHUNKS):
                here = x_sb[:, 4 * n:4 * n + 4, :]
                g.tensor_tensor(here, here, vb_ob[:, 1:2, :].to_broadcast([P, 4, C]), ALU.add
                ).then_inc(xob_ready, 1)
            pool.wait_ge(run_set, 1)

            def split_max(p, s, it=0, pair=0):
                rows_, res_ = max_rows[:, s % 2, :], max_res[:, s % 2, :]
                m0, m1, m2 = (max_parts[:, s % 2, i, :] for i in range(PARTS))
                transposed = a_count(it, pair + 1, 2) + 1
                pool.wait_ge(a_read, transposed)
                if not (isinstance(p, int) and p < 2):
                    pool.wait_ge(b_ready, (p - 1) * 16 + 1)
                g.tensor_tensor(m0, rows_, zero_rows[:, :], ALU.add).then_inc(max_part, 1)
                pool.wait_ge(max_part, p * 3 + 1)
                g.tensor_tensor(res_, rows_, m0, ALU.subtract).then_inc(max_part, 1)
                pool.wait_ge(max_part, p * 3 + 2)
                g.tensor_tensor(m1, res_, zero_rows[:, :], ALU.add).then_inc(max_part, 1)
                pool.wait_ge(max_part, p * 3 + 3)
                g.tensor_tensor(m2, res_, m1, ALU.subtract).then_inc(max_parts_ready, 1)

            def less_previous(cur, prev):
                g.tensor_tensor(dh[:, :, :], cur, prev, ALU.subtract).then_inc(shift_diff, 1)

            def mix(q, i, prev):
                pool.wait_ge(scaled_diff, q * 2 + i + 1)
                g.tensor_tensor(mix_in[i][:, :, :], mix_in[i][:, :, :], prev, ALU.add).then_inc(mixed, 1)

            def branch(t, q):
                if t == 1:
                    pool.wait_ge(rt_ready, q + 1)
                    ends = run[:, :, :, :].rearrange("p i b t -> p (i b) t")
                    g.tensor_tensor(ends[:, :, 0], ends[:, :, QT], zero_c[:, 0:1].to_broadcast([P, 4 * B]),
                                    ALU.add).then_inc(carried, 1)
                    for window, whole in ((k_q, k_of), (gate_q, gate_of), (v_q, v_of), (x_q, xnT[:, :, :])):
                        g.tensor_copy(window[:, :, :], whole[:, :, bass.ds(q * QT, QT)]).then_inc(windows, 1)
                if t == 3:
                    pool.wait_ge(run_max_ready, q * 2 + 2)
                    before, after = run_max[:, :, 0:QT], run_max[:, :, 1:]
                    for d, above, below in ((d1, before, after), (d2, k_q[:, :, :], after),
                                            (d3, before, k_q[:, :, :])):
                        g.tensor_tensor(d[:, :, :], above, below, ALU.subtract).then_inc(exponents, 1)
                if t == 9:
                    pool.wait_ge(exponents, q * 3 + 3)
                    pool.wait_ge(log_sum, q + 1)
                    g.tensor_tensor(d3[:, :, :], d3[:, :, :], ln_s[:, :, :], ALU.add).then_inc(pp_less_k, 1)
                if t == 11:
                    pool.wait_ge(weights_ready, q * 4 + 2)
                    pool.wait_ge(windows, q * 4 + 4)
                    g.tensor_tensor(ev[:, :, :], hi_u[:, :, :], v_q[:, :, :], ALU.mult).then_inc(ev_ready, 1)
                if t == 13:
                    pool.wait_ge(weights_ready, q * 4 + 4)
                    g.tensor_tensor(den[:, :, :], lo_y[:, :, :], hi_y[:, :, :], ALU.add).then_inc(den_ready, 1)
                    g.tensor_tensor(num[:, :, :], hi_y[:, :, :], v_q[:, :, :], ALU.mult).then_inc(y_terms, 1)
                if t == 14:
                    pool.wait_ge(log_den, q + 1)
                    g.tensor_tensor(den[:, :, :], den[:, :, :], gate_q[:, :, :], ALU.add).then_inc(log_both, 1)
                    pool.wait_ge(acc_ready, q * 2 + 2)
                    g.tensor_tensor(ev[:, :, :], lo_y[:, :, :], run_acc[:, :, 0:QT], ALU.mult).then_inc(y_terms, 1)
                    pool.wait_ge(y_terms, q * 2 + 2)
                    g.tensor_tensor(num[:, :, :], num[:, :, :], ev[:, :, :], ALU.add).then_inc(num_ready, 1)
                if t == 16:
                    pool.wait_ge(num_ready, q + 1)
                    pool.wait_ge(rec_ready, q + 1)
                    g.tensor_tensor(num[:, :, :], num[:, :, :], rec[:, :, :], ALU.mult).then_inc(ry_ready, 1)
                    pool.wait_ge(ry_ready, q + 1)
                    g.tensor_tensor(x1[:, :, :], num[:, :, :], x_q[:, :, :], ALU.add).then_inc(x1_ready, 1)
                if t == 17:
                    pool.wait_ge(centred2, q + 1)
                    g.tensor_tensor(sq2[:, :, :], xc2[:, :, :], xc2[:, :, :], ALU.mult).then_inc(squared2, 1)
                if t == 18:
                    pool.wait_ge(rs2_ready, q + 1)
                    g.tensor_tensor(h2[:, :, 1:], xc2[:, :, :], rs2[:, :, :], ALU.mult).then_inc(h2_hat, 1)
                if t == 19:
                    pool.wait_ge(h2_ready, q + 1)
                    pool.wait_ge(carried, q + 1)
                    less_previous(h2[:, :, 1:], h2[:, :, 0:QT])
                if t == 21:
                    for i in range(2):
                        mix(q, i, h2[:, :, 0:QT])
                for i in range(4):
                    if t != PRODUCT_STEP[f"ck{i}"]:
                        continue
                    pool.wait_ge(relu_ready, q * 4 + i + 1)
                    g.tensor_tensor(kk[i][:, :, :], kk[i][:, :, :], kk[i][:, :, :], ALU.mult).then_inc(kk_ready, 1)

            split_max(0, 0)
            pool.wait_ge(kvr_read, 3 * CHUNKS)
            pool.wait_ge(gate_ready, CHUNKS)
            pool.wait_ge(parts_out[1], PARTS_OUT)

            def head(p, j, it):
                branch(j * KEY_TILES, it)

            def rest(p, j, it):
                for step in range(1, KEY_TILES):
                    branch(j * KEY_TILES + step, it)
                    if step == SPLIT_STEP and (not isinstance(p, int) or p + 1 < PAIRS):
                        split_max(p + 1, (j + 1) % SETS, it, j + 1)

            program(pool, head, rest, lambda: None)

        @block.scalar
        def _(act):
            a = nc.scalar
            a.preload_act_table_set("natural_log_exp_and_others")
            act.nop().then_inc(ctx_copied, 1)
            act.dma_start(col_sb[:, :], cols).then_inc(cols_in, 16)
            act.dma_start(vb_ob[:, :, :], rows.rearrange("(o r) c -> o r c", o=1).to_broadcast([P, 2, C])
            ).then_inc(rows_in, 16)
            act.dma_start(gw1_sb[:, :], gw1).then_inc(small_in, 16)
            act.dma_start(gb1_sb[:, :], gb1).then_inc(small_in, 16)
            act.dma_start(gw2_sb[:, :], gw2).then_inc(small_in, 16)
            act.dma_start(gb2_sb[:, :], gb2.to_broadcast([B, EXPERTS])).then_inc(small_in, 16)
            for n in range(CHUNKS):
                act.wait_ge(x_transposed, n + 1)
                a.copy(xT[:, n, :], bank(n)).then_inc(xT_ready, 1)
            for n in range(CHUNKS):
                act.wait_ge(centred, n + 1)
                a.activation(sq[:, n, :], xc[:, n, :], ACT.Square).then_inc(squared, 1)
            act.wait_ge(eps_ok, 1)
            for n in range(CHUNKS):
                act.wait_ge(var_ready, n + 1)
                a.activation(sq[:, n, :], bank(n), ACT.Ln, bias=eps_c[:, 0:1]).then_inc(log_var, 1)
            for n in range(CHUNKS):
                act.wait_ge(log_var, n + 1)
                a.activation(rstd[:, n, :], sq[:, n, :], ACT.Exp, scale=-0.5).then_inc(rstd_ready, 1)
            for n in range(CHUNKS):
                a.copy(var_sb(n), bank(n)).then_inc(var_copied, 1)
            for n in range(CHUNKS):
                act.wait_ge(xn_ready, n + 1)
                a.activation(xc[:, n, :], rstd[:, n, :], ACT.Square).then_inc(rstd_sq, 1)
            act.wait_ge(gate_h_ps, 1)
            act.wait_ge(small_in, 64)
            a.activation(gate_h[:, :], banks[0:GATE_H, 4, 0:B], ACT.Relu, bias=gb1_sb[:, 0:1],
                         scale=1.0 / T).then_inc(gate_h_ready, 1)
            act.wait_ge(shifted_ready, 1)
            a.activation(gexp[:, :], logits[:, :], ACT.Exp, bias=neg_top[:, 0:1]).then_inc(gexp_ready, 1)
            for n in range(CHUNKS):
                act.wait_ge(var2_ready, n + 1)
                a.activation(xc[:, n, :], xc[:, n, :], ACT.Ln, bias=eps_c[:, 0:1]).then_inc(log_var2, 1)
                act.wait_ge(log_var2, n + 1)
                a.activation(rstd[:, n, :], xc[:, n, :], ACT.Exp, scale=-0.5).then_inc(rstd2_ready, 1)
            for n in range(CHUNKS):
                here = hT[:, n // 2, 1 + CHUNK * (n % 2):1 + CHUNK * (n % 2 + 1)]
                act.wait_ge(h_hat, n + 1)
                a.activation(here, here, ACT.Identity, bias=col("ln1_b"), scale=col("ln1_g")).then_inc(h_ready, 1)

            act.wait_ge(cols_in, 16)
            a.activation(qb_s[:, :], col("qb"), ACT.Copy, scale=SCALE).then_inc(qb_ready, 1)
            a.activation(neg_first[:, :], col("first"), ACT.Copy, scale=-1.0).then_inc(qb_ready, 1)
            act.wait_ge(qb_ready, 2)
            for m, (t, n) in enumerate(QK_ORDER):
                act.wait_ge(proj_ps, m + 1)
                a.activation(qk_f[:, t, n, :], bank(4 * t + n), ACT.Identity, bias=col("kb") if t else qb_s[:, 0:1],
                             scale=1.0 if t else SCALE).then_inc(qk_ready, 1)

            first_mix = COLS.index("mix_k")
            a.activation(less_mix[:, :], col_sb[:, first_mix:first_mix + 3], ACT.Identity, bias=1.0,
                         scale=-1.0).then_inc(less_ready, 1)
            act.wait_ge(rest_in, 16)
            act.wait_ge(weff_ps, 4)
            for i, name in enumerate("kvr"):
                a.activation(w_mix[:, i, 0, :], mat("t" + name), ACT.Copy, scale=col("mix_" + name)
                ).then_inc(w_mix_ready, 1)
            act.wait_ge(less_ready, 1)
            for i, name in enumerate("kvr"):
                a.activation(w_mix[:, i, 1, :], mat("t" + name), ACT.Copy, scale=less_mix[:, i:i + 1]
                ).then_inc(w_mix_ready, 1)
            for n in range(CHUNKS):
                kept = ((k_all, ACT.Copy, 1.0), (v_all, ACT.Copy, 1.0), (gate_all, ACT.Exp, -1.0))
                for i, (there, func, scale) in enumerate(kept):
                    act.wait_ge(kvr_ps, 3 * n + i + 1)
                    a.activation(there[n], project_bank(3 * n + i), func, scale=scale).then_inc(kvr_read, 1)
                act.wait_ge(kvr_read, 3 * n + 3)
                a.activation(gate_all[n], gate_all[n], ACT.Ln, bias=1.0).then_inc(gate_ready, 1)

            weights = ((lo_u, -1.0, 0.0), (hi_u, 1.0, 0.0), (lo_y, -1.0, col("first")), (hi_y, 1.0, neg_first[:, :]))

            def branch(t, q):
                if t == 5:
                    for i, (d, w) in enumerate(((d1, w1), (d2, w2))):
                        act.wait_ge(exponents, q * 3 + i + 1)
                        a.activation(w[:, :, :], d[:, :, :], ACT.Exp, bias=col("decay")).then_inc(decays_ready, 1)
                if t == 8:
                    act.wait_ge(sum_ready, q * 2 + 2)
                    a.activation(ln_s[:, :, :], run_sum[:, :, 0:QT], ACT.Ln).then_inc(log_sum, 1)
                if 9 <= t < 13:
                    weight, sign, bias = weights[t - 9]
                    act.wait_ge(pp_less_k, q + 1)
                    a.activation(weight[:, :, :], d3[:, :, :], ACT.Relu, scale=sign, bias=bias).then_inc(clipped, 1)
                    act.wait_ge(clipped, q * 4 + t - 8)
                    a.activation(weight[:, :, :], weight[:, :, :], ACT.Exp, scale=-1.0).then_inc(weights_ready, 1)
                if t == 14:
                    act.wait_ge(den_ready, q + 1)
                    a.activation(den[:, :, :], den[:, :, :], ACT.Ln).then_inc(log_den, 1)
                if t == 15:
                    act.wait_ge(log_both, q + 1)
                    a.activation(rec[:, :, :], den[:, :, :], ACT.Exp, scale=-1.0).then_inc(rec_ready, 1)
                if t == PRODUCT_STEP["var"]:
                    act.wait_ge(var2_ps, q + 1)
                    a.activation(flat(rs2), product_bank("var"), ACT.Ln, bias=eps_c[:, 0:1]).then_inc(log_var_q, 1)
                    act.wait_ge(log_var_q, q + 1)
                    a.activation(rs2[:, :, :], rs2[:, :, :], ACT.Exp, scale=-0.5).then_inc(rs2_ready, 1)
                if t == 19:
                    act.wait_ge(h2_hat, q + 1)
                    a.activation(h2[:, :, 1:], h2[:, :, 1:], ACT.Identity, bias=col("ln2_b"), scale=col("ln2_g")
                    ).then_inc(h2_ready, 1)
                if t == 20:
                    act.wait_ge(shift_diff, q + 1)
                    for i, name in enumerate(("cmix_r", "cmix_k")):
                        a.activation(mix_in[i][:, :, :], dh[:, :, :], ACT.Copy, scale=col(name)
                        ).then_inc(scaled_diff, 1)
                for i in range(4):
                    if t == PRODUCT_STEP[f"ck{i}"]:
                        act.wait_ge(ck_ps, q * 4 + i + 1)
                        a.activation(flat(kk[i]), product_bank(f"ck{i}"), ACT.Relu).then_inc(relu_ready, 1)
                if t == PRODUCT_STEP["cr"]:
                    act.wait_ge(cr_ps, q + 1)
                    a.activation(flat(ecr), product_bank("cr"), ACT.Exp, scale=-1.0).then_inc(cr_step, 1)
                if t == 24:
                    act.wait_ge(cr_step, q * 2 + 1)
                    a.activation(ecr[:, :, :], ecr[:, :, :], ACT.Ln, bias=1.0).then_inc(cr_step, 1)
                if t == 28:
                    act.wait_ge(cr_step, q * 2 + 2)
                    a.activation(ecr[:, :, :], ecr[:, :, :], ACT.Exp, scale=-1.0).then_inc(cr_ready, 1)

            def exps(p, step):
                for e in range(2):
                    act.wait_ge(b_ready, p * 16 + 2 * step + e + 1)
                    a.activation(probs[:, (2 * step + e) % 4, :, :], banks[:, 2 * e:2 * e + 2, :],
                                 ACT.Exp).then_inc(b_read, 1)

            def copy_ctx(p, s, before):
                act.wait_ge(pv_done, (p + 1) * 8)
                act.wait_ge(ctx_out[s % 2], before * 64 + 1)
                a.copy(ctx_sb[:, s % 2, :], bank(PV_BANK)).then_inc(ctx_copied, 1)

            def head(p, j, it):
                exps(p, 0)
                if not first(p):
                    copy_ctx(p - 1, (j - 1) % SETS, it * 2 + (j - 1) // 2)
                branch(j * KEY_TILES, it)

            def rest(p, j, it):
                for step in range(1, KEY_TILES):
                    exps(p, step)
                    branch(j * KEY_TILES + step, it)

            def tail():
                copy_ctx(PAIRS - 1, SETS - 1, (PAIRS - 1) // 2)
                for n in range(CHUNKS):
                    act.wait_ge(attn_in[n], 32)
                    a.activation(den_T[:, n, :], den_T[:, n, :], ACT.Ln).then_inc(den_step, 1)
                    act.wait_ge(den_step, 2 * n + 1)
                    a.activation(den_T[:, n, :], den_T[:, n, :], ACT.Exp, scale=-1.0).then_inc(den_step, 1)

            program(act, head, rest, tail)

        @block.vector
        def _(dve):
            v = nc.vector
            v.memset(k_op[:, :, :, :], 0.0).then_inc(keys_cleared, 1)
            for n in range(CHUNKS):
                dve.wait_ge(mean_ready, n + 1)
                v.tensor_tensor(xc[:, n, :], xT[:, n, :], bank(4 + n), ALU.subtract).then_inc(centred, 1)
            for n in range(CHUNKS):
                dve.wait_ge(rstd_ready, n + 1)
                v.tensor_tensor(xnT[:, n // 2, CHUNK * (n % 2):CHUNK * (n % 2 + 1)], xc[:, n, :], rstd[:, n, :],
                                ALU.mult).then_inc(xn_ready, 1)
                dve.wait_ge(xn_ready, n + 1)
                v.reduce_sum(pool_sums[:, n:n + 1], xnT[:, n // 2, CHUNK * (n % 2):CHUNK * (n % 2 + 1)],
                             axis=AX.X).then_inc(summed, 1)
            dve.wait_ge(summed, CHUNKS)
            v.tensor_tensor(pooled[:, :], pool_sums[:, 0:CHUNKS:2], pool_sums[:, 1:CHUNKS:2], ALU.add
            ).then_inc(pooled_ready, 1)

            chain = [0]

            def link(ins):
                ins.then_inc(gate_chain, 1)
                chain[0] += 1
                dve.wait_ge(gate_chain, chain[0])

            dve.wait_ge(logits_ps, 1)
            dve.wait_ge(small_in, 64)
            link(v.tensor_tensor(logits[:, :], banks[0:B, 4, 8:8 + EXPERTS], gb2_sb[:, :], ALU.add))
            v.tensor_reduce(neg_top[:, :], logits[:, :], axis=AX.X, op=ALU.max, negate=True
            ).then_inc(shifted_ready, 1)
            sh = [B, EXPERTS, EXPERTS]
            of_j = logits[:, :].rearrange("b (o j) -> b o j", o=1).to_broadcast(sh)
            of_e = logits[:, :].rearrange("b (e o) -> b e o", o=1).to_broadcast(sh)
            link(v.tensor_tensor(gt[:, :, :], of_j, of_e, ALU.is_gt))
            link(v.tensor_tensor(eq[:, :, :], of_j, of_e, ALU.is_equal))
            dve.wait_ge(lower_ok, 1)
            link(v.tensor_tensor(eq[:, :, :], eq[:, :, :], lower[:, :, :], ALU.mult))
            link(v.tensor_tensor(gt[:, :, :], gt[:, :, :], eq[:, :, :], ALU.add))
            link(v.reduce_sum(rank[:, :], gt[:, :, :], axis=AX.X))
            link(v.tensor_scalar(chosen[:, :], rank[:, :], 2.0, None, ALU.is_lt))
            dve.wait_ge(gexp_ready, 1)
            link(v.tensor_tensor(gexp[:, :], gexp[:, :], chosen[:, :], ALU.mult))
            link(v.reduce_sum(gsum[:, :], gexp[:, :], axis=AX.X))
            link(v.reciprocal(gsum[:, :], gsum[:, :]))
            link(v.tensor_scalar(gates[:, :], gexp[:, :], gsum[:, 0:1], None, ALU.mult))
            v.tensor_copy(gates_r[:, :, :], gates[:, :].rearrange("b (e o) -> b e o", o=1).to_broadcast(
                [B, EXPERTS, RANK])).then_inc(gates_ready, 1)
            dve.wait_ge(gcol_ps, 1)
            link(v.tensor_copy(gcol[:, :], banks[:, 4, 16:16 + B]))
            dve.wait_ge(cols_in, 16)
            for i, name in enumerate(("qS", "kS", "vS", "oS")):
                v.tensor_scalar(sg[:, i, :], gcol[:, :], col(name), None, ALU.mult).then_inc(sg_ready, 1)
            dve.wait_ge(sg_ready, 4)
            dve.wait_ge(moe_in, 16)
            for i, name in enumerate(("qU", "kU", "vU", "oU")):
                for b in range(B):
                    v.tensor_scalar(u_s[:, i, b, :], mat(name), sg[:, i, b:b + 1], None, ALU.mult
                    ).then_inc(us_ready, 1)
            def add_main(i):
                dve.wait_ge(weff_ps, i + 1)
                v.tensor_tensor(w_eff[:, i, :, :], bank(WEFF_BANKS[i])[:, 0:B * P].rearrange(
                    "p (b o) -> p b o", b=B), mat("qkvo"[i] + "W").rearrange("p (u o) -> p u o", u=1).to_broadcast(
                    [P, B, P]), ALU.add).then_inc(weff_ready, 1)

            add_main(0)
            add_main(1)

            def split(m, t, n, done):
                dve.wait_ge(qk_ready, QK_ORDER.index((t, n)) + 1)
                qf, qr = qk_f[:, t, n, :], res[:, t, n, :]
                q0, q1, q2 = (parts[:, t, i, n, :] for i in range(PARTS))
                v.tensor_copy(q0, qf).then_inc(q_part, 1)
                dve.wait_ge(q_part, 3 * m + 1)
                v.tensor_tensor(qr, qf, q0, ALU.subtract).then_inc(q_part, 1)
                dve.wait_ge(q_part, 3 * m + 2)
                v.tensor_copy(q1, qr).then_inc(q_part, 1)
                dve.wait_ge(q_part, 3 * m + 3)
                v.tensor_tensor(q2, qr, q1, ALU.subtract).then_inc(done, 1)

            for m, (t, n, done) in enumerate(((0, 0, q_split), (0, 1, q_split), (1, 1, k1_split),
                                              (0, 2, q_split), (0, 3, q_split))):
                split(m, t, n, done)
                if m == 0:
                    add_main(2)
                    add_main(3)
            dve.wait_ge(rows_in, 16)
            vb = vb_ob[:, 0:1, :].rearrange("p u (r w) -> p u r w", w=2 * HD).to_broadcast([P, 4, 8, 2 * HD])
            for n in range(CHUNKS):
                dve.wait_ge(v_ps, n + 1)
                for k in range(4):
                    tc = 4 * (n % 2) + k
                    ins = v.tensor_tensor(V[:, 8 * (n // 2):8 * (n // 2) + 8, tc, :],
                                          bank(n)[:, P * k:P * k + P].rearrange("p (r w) -> p r w", w=2 * HD),
                                          vb[:, 0, :, :], ALU.add)
                ins.then_inc(v_ready, 1)

            def scan(q, out_, c0, c1, op0, op1, done):
                for b in range(B):
                    data1 = c1.to_broadcast([P, QT]) if c1 is not None and len(c1.shape) == 2 else c1[:, b, :]
                    v.tensor_tensor_scan(out_[:, b, 1:], c0[:, b, :], data1, out_[:, b, 0:1], op0, op1
                    ).then_inc(done, 1)

            def branch(t, q):
                if t == 2:
                    dve.wait_ge(carried, q + 1)
                    dve.wait_ge(windows, q * 4 + 1)
                    scan(q, run_max, k_q, col("decay"), ALU.max, ALU.add, run_max_ready)
                if t == 6:
                    dve.wait_ge(decays_ready, q * 2 + 2)
                    scan(q, run_sum, w1, w2, ALU.mult, ALU.add, sum_ready)
                if t == 12:
                    dve.wait_ge(ev_ready, q + 1)
                    scan(q, run_acc, lo_u, ev, ALU.mult, ALU.add, acc_ready)
                if t == PRODUCT_STEP["mean"]:
                    dve.wait_ge(mean2_ps, q + 1)
                    v.tensor_tensor(flat(xc2), flat(x1), product_bank("mean"), ALU.subtract).then_inc(centred2, 1)
                if t == PRODUCT_STEP["cv"]:
                    dve.wait_ge(cr_ready, q + 1)
                    dve.wait_ge(cv_ps, q + 1)
                    v.tensor_tensor(flat(gx), product_bank("cv"), flat(ecr), ALU.mult).then_inc(gated, 1)
                    dve.wait_ge(gated, q + 1)
                    v.tensor_tensor(RT[:, :, bass.ds(q * QT, QT)], x1[:, :, :], gx[:, :, :], ALU.add
                    ).then_inc(rt_ready, 1)

            def read_place(it, pair, k, src):
                if not exists(it, pair, k):
                    return
                n, s, pair_n = a_count(it, pair, k), pair % 2, it * SETS + pair
                if k == 2:
                    if not isinstance(pair_n, int) or pair_n >= 2:
                        dve.wait_ge(max_parts_ready, pair_n - 1)
                    dve.wait_ge(a_ready, n + 1)
                    v.tensor_copy(max_rows[:, (s + 1) % 2, :], src[0:2 * KEY_TILES, 0:P]).then_inc(a_read, 1)
                    return
                u = k if k < 2 else k - 1
                dve.wait_ge(a_ready, n + 1)
                v.tensor_reduce(neg_half[:, s, u:u + 1], src, axis=AX.X, op=ALU.max, negate=True
                ).then_inc(a_read, 1)
                if u == 31:
                    dve.wait_ge(a_read, n + 1)
                    v.tensor_reduce(neg_max[:, s, :], neg_half[:, s, :].rearrange("p (c h) -> p c h", h=2),
                                    axis=AX.X, op=ALU.min).then_inc(half_combined, 1)

            for pair, k in places(0, A_PLACES + LEAD):
                read_place(0, pair, k, bank(A_BANK + a_count(0, pair, k) % 3))

            def one_step(t, it):
                for turn in place_turns[t]:
                    read_place(it, *turns[turn], turn_bank(turn))
                branch(t, it)

            def head(p, j, it):
                one_step(j * KEY_TILES, it)

            def rest(p, j, it):
                for step in range(1, KEY_TILES):
                    one_step(j * KEY_TILES + step, it)

            def tail():
                dve.wait_ge(xob_ready, CHUNKS)
                for b in range(B):
                    for n in (2 * b, 2 * b + 1):
                        dve.wait_ge(attn_in[n], 32)
                        dve.wait_ge(den_step, 2 * n + 2)
                        v.tensor_tensor(ctx_T[:, n, :], ctx_T[:, n, :], den_T[:, n, :], ALU.mult
                        ).then_inc(attn_ready, 1)
                    for n in (2 * b, 2 * b + 1):
                        dve.wait_ge(final_ps, n + 1)
                        here = x_sb[:, 4 * n:4 * n + 4, :].rearrange("p k c -> p (k c)")
                        v.tensor_tensor(here, here, bank(n), ALU.add).then_inc(final_ready, 1)

            program(dve, head, rest, tail)

        @block.tensor
        def _(pe):
            mm = nc.tensor.matmul
            pe.wait_ge(ident_ok, 1)
            for n in range(CHUNKS):
                pe.wait_ge(x_in[n], 16)
                for k in range(4):
                    last = nc.tensor.transpose(bank(n)[:, P * k:P * k + P], x_sb[:, 4 * n + k, :], ident[:, :])
                last.then_inc(x_transposed, 1)
            pe.wait_ge(mean_w_ok, 1)
            for n in range(CHUNKS):
                pe.wait_ge(xT_ready, n + 1)
                mm(bank(4 + n), mean_w[:, :], xT[:, n, :], start=True, stop=True).then_inc(mean_ready, 1)
            for n in range(CHUNKS):
                pe.wait_ge(squared, n + 1)
                mm(bank(n), mean_w[:, :], sq[:, n, :], start=True, stop=True).then_inc(var_ready, 1)
            pe.wait_ge(pooled_ready, 1)
            pe.wait_ge(small_in, 64)
            mm(banks[0:GATE_H, 4, 0:B], gw1_sb[:, :], pooled[:, :], start=True, stop=True).then_inc(gate_h_ps, 1)
            pe.wait_ge(gate_h_ready, 1)
            mm(banks[0:B, 4, 8:8 + EXPERTS], gate_h[:, :], gw2_sb[:, :], start=True, stop=True
            ).then_inc(logits_ps, 1)
            pe.wait_ge(gates_ready, 1)
            mm(banks[:, 4, 16:16 + B], gates_r[:, :, :].rearrange("b e r -> b (e r)"), ident[0:B, 0:B],
               start=True, stop=True).then_inc(gcol_ps, 1)
            pe.wait_ge(moe_in, 16)
            pe.wait_ge(var_copied, CHUNKS)
            for m, (t, n) in enumerate(QK_ORDER):
                if m in (0, 2):
                    for i in (m, m + 1):
                        pe.wait_ge(us_ready, 2 * i + 2)
                        mm(bank(WEFF_BANKS[i])[:, 0:B * P], mat("qkvo"[i] + "V"),
                           u_s[:, i, :, :].rearrange("p b o -> p (b o)"), start=True, stop=True
                           ).then_inc(weff_ps, 1)
                pe.wait_ge(weff_ready, (1, 1, 2, 2, 4, 4, 4, 4)[m])
                mm(bank(4 * t + n), w_eff[:, t, n // 2, :], xnT[:, n // 2, CHUNK * (n % 2):CHUNK * (n % 2 + 1)],
                   start=True, stop=True).then_inc(proj_ps, 1)
            for n in range(CHUNKS):
                pe.wait_ge(qk_ready, QK_ORDER.index((0, n)) + 1)
                for k in range(4):
                    at = CHUNK * (n % 2) + P * k
                    last = mm(bank(n)[:, P * k:P * k + P], xnT[:, n // 2, at:at + P], w_eff[:, 2, n // 2, :],
                              start=True, stop=True)
                last.then_inc(v_ps, 1)
            pe.wait_ge(qk_ready, 2 * CHUNKS)
            pe.wait_ge(rest_in, 16)

            pe.wait_ge(ones_set, 1)

            def fill_place(it, pair, k, dst):
                s = pair % SETS
                if k == 2:
                    pe.wait_ge(half_combined, it * SETS + pair)
                    nc.tensor.transpose(dst[0:2 * KEY_TILES, 0:P], neg_max[:, (pair + 1) % 2, :],
                                        ident[:, :]).then_inc(a_ready, 1)
                    return
                u = k if k < 2 else k - 1
                e, c, h = u // 16, u // 2 % 8, u % 2
                if u % 16 == 0:
                    pe.wait_ge(op_in[s][e], (it + pair // SETS + 1) * 32)
                mm(dst, q_op[0:MAX_ROW, s, e, P * c:P * c + P],
                   k_op[0:MAX_ROW, s, e, CHUNK * h:CHUNK * h + CHUNK],
                   start=True, stop=True).then_inc(a_ready, 1)

            def project(m, now):
                n, i = divmod(m, 3)
                if not now:
                    at = CHUNK * (n % 2)
                    mm(project_bank(m), w_mix[:, i, 1, :], hT[:, n // 2, at:at + CHUNK],
                       start=False, stop=True).then_inc(kvr_ps, 1)
                    return
                if m == 0:
                    pe.wait_ge(w_mix_ready, 6)
                if i == 0:
                    pe.wait_ge(h_ready, n + 1)
                if 4 <= m < 8:
                    pe.wait_ge(v_ready, m - 3)
                if m >= 8:
                    pe.wait_ge(kvr_read, m - 3)
                at = 1 + CHUNK * (n % 2)
                mm(project_bank(m), w_mix[:, i, 0, :], hT[:, n // 2, at:at + CHUNK], start=True, stop=False)

            for m in range(PROJECT_EARLY):
                project(m, True)
                project(m, False)
            pe.wait_ge(kvr_read, 4)
            pe.wait_ge(v_ready, CHUNKS)

            for pair, k in places(0, A_PLACES + LEAD):
                if not exists(0, pair, k):
                    continue
                n = a_count(0, pair, k)
                if n >= 3:
                    pe.wait_ge(a_read, n - 2)
                fill_place(0, pair, k, bank(A_BANK + n % 3))
                m, gap = divmod(n - PROJECT_FROM, PROJECT_GAP)
                if m >= 0 and m + PROJECT_EARLY < 3 * CHUNKS and gap in (0, 2):
                    project(m + PROJECT_EARLY, gap == 0)
            pe.wait_ge(kvr_read, 3 * CHUNKS)

            def fill_turn(it, turn):
                if exists(it, *turns[turn]):
                    wait_for_bank(pe, it, turn)
                    fill_place(it, *turns[turn], turn_bank(turn))

            def product(q, name):
                turn = turns.index(name)
                dst = turn_bank(turn)
                wait_for_bank(pe, q, turn)
                if name == "mean":
                    pe.wait_ge(x1_ready, q + 1)
                    mm(dst, mean_w[:, :], flat(x1), start=True, stop=True).then_inc(mean2_ps, 1)
                elif name == "var":
                    pe.wait_ge(squared2, q + 1)
                    mm(dst, mean_w[:, :], flat(sq2), start=True, stop=True).then_inc(var2_ps, 1)
                elif name == "cr":
                    pe.wait_ge(mixed, q * 2 + 1)
                    mm(dst, mat("cr"), flat(mix_in[0]), start=True, stop=True).then_inc(cr_ps, 1)
                elif name == "cv":
                    for i in range(4):
                        pe.wait_ge(kk_ready, q * 4 + i + 1)
                        last = mm(dst, mat(f"cv{i}"), flat(kk[i]), start=(i == 0), stop=(i == 3))
                    last.then_inc(cv_ps, 1)
                else:
                    pe.wait_ge(mixed, q * 2 + 2)
                    mm(dst, mat(name), flat(mix_in[1]), start=True, stop=True).then_inc(ck_ps, 1)

            def scores(p, s, step, e):
                if not (first(p) and step == 0):
                    pe.wait_ge(b_read, p * 16 + 2 * step + e - 1)
                for h in range(2):
                    last = mm(bank(2 * e + h), k_op[0:MAX_ROW + PARTS, s, e, P * step:P * step + P],
                              q_op[0:MAX_ROW + PARTS, s, e, CHUNK * h:CHUNK * h + CHUNK], start=True, stop=True)
                last.then_inc(b_ready, 1)

            def values(p, s, step):
                pe.wait_ge(b_read, p * 16 + 2 * step + 2)
                for e in range(2):
                    for h in range(2):
                        g = 32 * (2 * e + h)
                        last = mm(banks[g:g + 32, PV_BANK, :], v_op[:, s % 2, step, e, :],
                                  probs[:, (2 * step + e) % 4, h, :], start=(step == 0), stop=(step == KEY_TILES - 1))
                last.then_inc(pv_done, 1)

            def one_step(p, j, it, step):
                t = j * KEY_TILES + step
                todo = place_turns[t]
                fill_turn(it, todo[0])
                if step == 0:
                    pe.wait_ge(max_in[j % 2], (it * 2 + j // 2 + 1) * 16 * PARTS)
                scores(p, j, step, 0)
                fill_turn(it, todo[1])
                scores(p, j, step, 1)
                fill_turn(it, todo[2])
                if step == 1:
                    pe.wait_ge(v_in[j % 2], (it * 2 + j // 2 + 1) * 32)
                    pe.wait_ge(ctx_copied, p + 1)
                if step > 0:
                    values(p, j, step - 1)
                elif not first(p):
                    values(p - 1, (j - 1) % SETS, KEY_TILES - 1)
                for turn in todo[3:]:
                    fill_turn(it, turn)
                for name, at in PRODUCT_STEP.items():
                    if at == t:
                        product(it, name)

            def head(p, j, it):
                one_step(p, j, it, 0)

            def rest(p, j, it):
                for step in range(1, KEY_TILES):
                    one_step(p, j, it, step)

            def tail():
                values(PAIRS - 1, SETS - 1, KEY_TILES - 1)
                pe.wait_ge(b_read, PAIRS * 2 * KEY_TILES)
                pe.wait_ge(rt_ready, QUARTERS + 1)
                for n in range(CHUNKS):
                    for k in range(4):
                        at, dst = CHUNK * (n % 2) + P * k, bank(n)[:, P * k:P * k + P]
                        mm(dst, RT[:, n // 2, at:at + P], ident[:, :], start=(k == 0), stop=False)
                for n in range(CHUNKS):
                    pe.wait_ge(attn_ready, n + 1)
                    for k in range(4):
                        last = mm(bank(n)[:, P * k:P * k + P], ctx_T[:, n, P * k:P * k + P],
                                  w_eff[:, 3, n // 2, :], start=False, stop=(k == 3))
                    last.then_inc(final_ps, 1)

            program(pe, head, rest, tail)


def kernel(**inputs):
    import numpy as np
    import concourse.bacc as bacc
    from concourse.bass_utils import run_bass_kernel_spmd

    def arr(name):
        return np.asarray(inputs[name])

    a, f = "L0_attn_", "L0_ffn_"
    col_of = {n: arr(a + n).reshape(C) for n in COLS[:9]}
    col_of.update(decay=arr(a + "time_decay"), first=arr(a + "time_first"), qb=arr(f + "qb"), kb=arr(f + "kb"))
    for p in "qkvo":
        col_of[p + "S"] = arr(f + p + "S").reshape(EXPERTS * RANK)
    mat_of = {n: arr(a + "w_" + n) for n in ("tk", "tv", "tr", "cr")}
    for i in range(4):
        mat_of[f"ck{i}"] = arr(a + "w_ck")[:, P * i:P * (i + 1)]
        mat_of[f"cv{i}"] = arr(a + "w_cv")[P * i:P * (i + 1), :]
    for p in "qkvo":
        mat_of[p + "W"] = arr(f + p + "Wm").T
        mat_of[p + "V"] = arr(f + p + "V").reshape(EXPERTS * RANK, C)
        mat_of[p + "U"] = arr(f + p + "U").transpose(0, 2, 1).reshape(EXPERTS * RANK, C)
    arrays = {
        "x": arr(a + "x"),
        "cols": np.stack([col_of[n] for n in COLS], axis=1),
        "mats": np.stack([mat_of[n] for n in MATS], axis=1),
        "rows": np.stack([arr(f + "vb"), arr(f + "ob")]),
        "gw1": arr(f + "gw1").T,
        "gb1": arr(f + "gb1").reshape(GATE_H, 1),
        "gw2": arr(f + "gw2").T,
        "gb2": arr(f + "gb2").reshape(1, EXPERTS),
    }
    arrays = {f"in_{n}_dram": np.ascontiguousarray(v) for n, v in arrays.items()}
    nc = bacc.Bacc("TRN2", target_bir_lowering=False, num_devices=1)
    args = [nc.dram_tensor(n, v.shape, mybir.dt.from_np(v.dtype), kind="ExternalInput").ap()
            for n, v in arrays.items()]
    out = nc.dram_tensor("out_0_dram", (B, T, C), mybir.dt.float32, kind="ExternalOutput").ap()
    build(nc, *args, out)
    r = run_bass_kernel_spmd(nc, [arrays], core_ids=[0])
    return r.results[0]["out_0_dram"]
```
